# Optimizing a Trainium2 kernel written in Bass

```python
import numpy as np
import jax
import jax.numpy as jnp

def _softmax(x, axis=-1):
    return jax.nn.softmax(x, axis=axis)

def _gelu(x):
    return jax.nn.gelu(x, approximate=True)

def _silu(x):
    return jax.nn.silu(x)

def _sigmoid(x):
    return jax.nn.sigmoid(x)

def _layernorm(x, axis=-1, eps=1e-05):
    m = jnp.mean(x, axis=axis, keepdims=True)
    v = jnp.var(x, axis=axis, keepdims=True)
    return (x - m) / jnp.sqrt(v + eps)

def _scatter_add(tgt, idx, src, axis=0):
    return tgt.at[idx].add(src)

def _segment_sum(src, seg, n):
    return jax.ops.segment_sum(src, seg, n)
kernel_name = 'mk_lm_tower_d2_tok_ids1024_r4_4c1b38'

def setup_inputs(seed: int=0):
    np.random.seed(seed)
    _w = jnp.asarray

    def _rec_inputs():
        import jax
        import jax.numpy as jnp
        _rk = jax.random.key(seed)
        x = jax.random.randint(jax.random.fold_in(_rk, 1), (8, 512), 0, 28, jnp.int32)
        mask_BS_i1_0 = jnp.where(jnp.ones((8, 512), dtype=bool), 1, 0).astype(jnp.int32)
        return (x, mask_BS_i1_0)
    x, mask_BS_i1_0 = _rec_inputs()

    def _L0_tok_setup():
        import jax, jax.numpy as jnp
        import numpy as np
        WINDOW_SIZE = 3
        LN_EPS = 1e-05

        def _sliding_window_features(base_pca, mask_f):
            B, S, F = base_pca.shape
            h = WINDOW_SIZE // 2
            idx = jnp.arange(S)
            start = jnp.maximum(idx - h, 0)
            end = jnp.minimum(idx + h + 1, S)
            masked = base_pca * mask_f[..., None]
            csum = jnp.pad(jnp.cumsum(masked, axis=1), ((0, 0), (1, 0), (0, 0)))
            wsum = csum[:, end, :] - csum[:, start, :]
            mcs = jnp.pad(jnp.cumsum(mask_f, axis=1), ((0, 0), (1, 0)))
            lengths = jnp.maximum(mcs[:, end] - mcs[:, start], 1.0)
            return wsum / lengths[..., None]
        key = jax.random.key(seed)
        ks = jax.random.split(key, 8)
        B, S, V, E = (8, 1024, 28, 256)
        input_ids = jax.random.randint(ks[0], (B, S), 0, V, dtype=jnp.int64)
        attention_mask = jnp.ones((B, S), dtype=jnp.int32)
        emb = jax.random.normal(ks[1], (V, E), dtype=jnp.float32) * 0.02
        emb = emb.at[0].set(0.0)
        pca_lookup = jax.random.normal(ks[2], (V, 20), dtype=jnp.float32)
        proj_w = jax.random.normal(ks[3], (20, E), dtype=jnp.float32) * 0.2
        proj_b = jnp.zeros((E,), dtype=jnp.float32)
        fus_w = jax.random.normal(ks[4], (2 * E, E), dtype=jnp.float32) * 0.02
        fus_b = jnp.zeros((E,), dtype=jnp.float32)
        ln_g = jnp.ones((E,), dtype=jnp.float32)
        ln_b = jnp.zeros((E,), dtype=jnp.float32)
        return {'input_ids': input_ids, 'attention_mask': attention_mask, 'emb': emb, 'pca_lookup': pca_lookup, 'proj_w': proj_w, 'proj_b': proj_b, 'fus_w': fus_w, 'fus_b': fus_b, 'ln_g': ln_g, 'ln_b': ln_b}
    _L0_tok_all = _L0_tok_setup()
    _L0_tok_in = {k: v for k, v in _L0_tok_all.items() if k in ('emb', 'pca_lookup', 'proj_w', 'proj_b', 'fus_w', 'fus_b', 'ln_g', 'ln_b')}
    del _L0_tok_all

    def _L0_attn_setup():
        import jax, jax.numpy as jnp
        import numpy as np
        D_MODEL = 256
        NHEAD = 16
        MAX_LEN = 512
        B, L = (2, 512)
        key = jax.random.key(seed)
        ks = jax.random.split(key, 6)
        s = 0.02
        inp = {'queries': jax.random.normal(ks[0], (B, L, D_MODEL), dtype=jnp.float32), 'Wq': jax.random.normal(ks[1], (D_MODEL, D_MODEL), dtype=jnp.float32) * s, 'bq': jnp.zeros((D_MODEL,), dtype=jnp.float32), 'Wk': jax.random.normal(ks[2], (D_MODEL, D_MODEL), dtype=jnp.float32) * s, 'bk': jnp.zeros((D_MODEL,), dtype=jnp.float32), 'Wv': jax.random.normal(ks[3], (D_MODEL, D_MODEL), dtype=jnp.float32) * s, 'bv': jnp.zeros((D_MODEL,), dtype=jnp.float32), 'Wo': jax.random.normal(ks[4], (D_MODEL, D_MODEL), dtype=jnp.float32) * s, 'bo': jnp.zeros((D_MODEL,), dtype=jnp.float32)}
        m = jnp.arange(2 * MAX_LEN - 1, dtype=jnp.float32)
        pb_row = -jnp.abs(MAX_LEN - 1 - m) / MAX_LEN
        inp['pos_bias'] = jnp.tile(pb_row[None, :], (NHEAD, 1))
        return inp
    _L0_attn_all = _L0_attn_setup()
    _L0_attn_in = {k: v for k, v in _L0_attn_all.items() if k in ('Wq', 'bq', 'Wk', 'bk', 'Wv', 'bv', 'Wo', 'bo', 'pos_bias')}
    del _L0_attn_all

    def _L0_ffn_setup():
        import jax, jax.numpy as jnp
        import numpy as np
        D_MODEL = 256
        M = 64
        INNER = 16
        key = jax.random.key(seed)
        ks = jax.random.split(key, 9)

        def init(k, shape, fan_in):
            bound = 1.0 / np.sqrt(fan_in)
            return jax.random.uniform(k, shape, jnp.float32, -bound, bound)
        x = jax.random.normal(ks[0], (16, 1024, D_MODEL), dtype=jnp.float32)
        Win = init(ks[1], (D_MODEL, M), D_MODEL)
        bin_ = init(ks[2], (M,), D_MODEL)
        W1 = init(ks[3], (M, INNER), 1)
        b1 = init(ks[4], (M, INNER), 1)
        W2 = init(ks[5], (M, INNER), INNER)
        b2 = init(ks[6], (M,), INNER)
        Wout = init(ks[7], (M, D_MODEL), M)
        bout = init(ks[8], (D_MODEL,), M)
        return {'x': x, 'Win': Win, 'bin_': bin_, 'W1': W1, 'b1': b1, 'W2': W2, 'b2': b2, 'Wout': Wout, 'bout': bout}
    _L0_ffn_all = _L0_ffn_setup()
    _L0_ffn_in = {k: v for k, v in _L0_ffn_all.items() if k in ('Win', 'bin_', 'W1', 'b1', 'W2', 'b2', 'Wout', 'bout')}
    del _L0_ffn_all

    def _L1_attn_setup():
        import jax, jax.numpy as jnp
        import numpy as np
        B, T, D, H = (8, 1024, 256, 8)

        def _block_linear(x, w, b):
            Bx, Tx, Dx = x.shape
            h, bw = (w.shape[0], w.shape[1])
            xb = x.reshape(Bx, Tx, h, bw)
            y = jnp.einsum('bthi,hij->bthj', xb, w) + b
            return y.reshape(Bx, Tx, Dx)

        def _rglru(x, a_param, ig_w, ig_b, ag_w, ag_b, sqrt_fn):
            gate_x = jax.nn.sigmoid(_block_linear(x, ig_w, ig_b))
            gate_a = jax.nn.sigmoid(_block_linear(x, ag_w, ag_b))
            log_a = -8.0 * gate_a * jax.nn.softplus(a_param)
            a = jnp.exp(log_a)
            a2 = jnp.exp(2.0 * log_a)
            multiplier = sqrt_fn(jnp.maximum(1.0 - a2, 1e-07))
            normed_x = x * gate_x * multiplier
            p = jnp.cumprod(a, axis=1)
            p_prefix = jnp.concatenate([jnp.ones_like(p[:, :1]), p[:, :-1]], axis=1)
            p_prefix = jnp.maximum(p_prefix, 1e-07)
            S = jnp.cumsum(normed_x / p_prefix, axis=1)
            h = p_prefix * S
            return (h, h[:, -1, :])

        def _reference_tuple_inner(x, segment_pos, a_param, ig_w, ig_b, ag_w, ag_b):
            y, last_h = _rglru(x, a_param, ig_w, ig_b, ag_w, ag_b, jnp.sqrt)
            return (y, last_h)
        key = jax.random.key(seed)
        k0, k1, k2, k3 = jax.random.split(key, 4)
        bw = D // H
        std = (1.0 / bw) ** 0.5
        x = jax.random.normal(k0, (B, T, D), dtype=jnp.float32)
        segment_pos = jnp.tile(jnp.arange(T, dtype=jnp.int32)[None, :], (B, 1))
        ig_w = jax.random.normal(k1, (H, bw, bw), dtype=jnp.float32) * std
        ig_b = jnp.zeros((H, bw), dtype=jnp.float32)
        ag_w = jax.random.normal(k2, (H, bw, bw), dtype=jnp.float32) * std
        ag_b = jnp.zeros((H, bw), dtype=jnp.float32)
        eps = 1e-08
        u = jax.random.uniform(k3, (D,), minval=0.9 ** 2 + eps, maxval=0.999 ** 2 + eps)
        a_param = jnp.log(jnp.exp(-0.5 * jnp.log(u)) - 1.0).astype(jnp.float32)
        return dict(x=x, segment_pos=segment_pos, a_param=a_param, ig_w=ig_w, ig_b=ig_b, ag_w=ag_w, ag_b=ag_b)
    _L1_attn_all = _L1_attn_setup()
    _L1_attn_in = {k: v for k, v in _L1_attn_all.items() if k in ('segment_pos', 'a_param', 'ig_w', 'ig_b', 'ag_w', 'ag_b')}
    del _L1_attn_all

    def _L1_ffn_setup():
        import jax, jax.numpy as jnp
        import numpy as np
        HIDDEN = 256
        FFN = 1024
        NUM_EXPERTS = 8
        TOP_K = 2
        BATCH, SEQ = (2, 512)
        key = jax.random.key(seed)
        ks = jax.random.split(key, 6)
        s_h = 1.0 / np.sqrt(HIDDEN)
        s_f = 1.0 / np.sqrt(FFN)
        return {'hidden_states': jax.random.normal(ks[0], (BATCH, SEQ, HIDDEN), jnp.float32), 'gate_w': jax.random.uniform(ks[1], (HIDDEN, NUM_EXPERTS), jnp.float32, -s_h, s_h), 'gate_b': jax.random.uniform(ks[2], (NUM_EXPERTS,), jnp.float32, -s_h, s_h), 'w1': jax.random.uniform(ks[3], (NUM_EXPERTS, HIDDEN, FFN), jnp.float32, -s_h, s_h), 'w3': jax.random.uniform(ks[4], (NUM_EXPERTS, HIDDEN, FFN), jnp.float32, -s_h, s_h), 'w2': jax.random.uniform(ks[5], (NUM_EXPERTS, FFN, HIDDEN), jnp.float32, -s_f, s_f)}
    _L1_ffn_all = _L1_ffn_setup()
    _L1_ffn_in = {k: v for k, v in _L1_ffn_all.items() if k in ('gate_w', 'gate_b', 'w1', 'w3', 'w2')}
    del _L1_ffn_all
    return {'x': x, 'mask_BS_i1_0': mask_BS_i1_0, 'L0_tok_emb': _L0_tok_in['emb'], 'L0_tok_pca_lookup': _L0_tok_in['pca_lookup'], 'L0_tok_proj_w': _L0_tok_in['proj_w'], 'L0_tok_proj_b': _L0_tok_in['proj_b'], 'L0_tok_fus_w': _L0_tok_in['fus_w'], 'L0_tok_fus_b': _L0_tok_in['fus_b'], 'L0_tok_ln_g': _L0_tok_in['ln_g'], 'L0_tok_ln_b': _L0_tok_in['ln_b'], 'L0_attn_Wq': _L0_attn_in['Wq'], 'L0_attn_bq': _L0_attn_in['bq'], 'L0_attn_Wk': _L0_attn_in['Wk'], 'L0_attn_bk': _L0_attn_in['bk'], 'L0_attn_Wv': _L0_attn_in['Wv'], 'L0_attn_bv': _L0_attn_in['bv'], 'L0_attn_Wo': _L0_attn_in['Wo'], 'L0_attn_bo': _L0_attn_in['bo'], 'L0_attn_pos_bias': _L0_attn_in['pos_bias'], 'L0_ffn_Win': _L0_ffn_in['Win'], 'L0_ffn_bin_': _L0_ffn_in['bin_'], 'L0_ffn_W1': _L0_ffn_in['W1'], 'L0_ffn_b1': _L0_ffn_in['b1'], 'L0_ffn_W2': _L0_ffn_in['W2'], 'L0_ffn_b2': _L0_ffn_in['b2'], 'L0_ffn_Wout': _L0_ffn_in['Wout'], 'L0_ffn_bout': _L0_ffn_in['bout'], 'L1_attn_segment_pos': _L1_attn_in['segment_pos'], 'L1_attn_a_param': _L1_attn_in['a_param'], 'L1_attn_ig_w': _L1_attn_in['ig_w'], 'L1_attn_ig_b': _L1_attn_in['ig_b'], 'L1_attn_ag_w': _L1_attn_in['ag_w'], 'L1_attn_ag_b': _L1_attn_in['ag_b'], 'L1_ffn_gate_w': _L1_ffn_in['gate_w'], 'L1_ffn_gate_b': _L1_ffn_in['gate_b'], 'L1_ffn_w1': _L1_ffn_in['w1'], 'L1_ffn_w3': _L1_ffn_in['w3'], 'L1_ffn_w2': _L1_ffn_in['w2']}

def reference(x, mask_BS_i1_0, L0_tok_emb, L0_tok_pca_lookup, L0_tok_proj_w, L0_tok_proj_b, L0_tok_fus_w, L0_tok_fus_b, L0_tok_ln_g, L0_tok_ln_b, L0_attn_Wq, L0_attn_bq, L0_attn_Wk, L0_attn_bk, L0_attn_Wv, L0_attn_bv, L0_attn_Wo, L0_attn_bo, L0_attn_pos_bias, L0_ffn_Win, L0_ffn_bin_, L0_ffn_W1, L0_ffn_b1, L0_ffn_W2, L0_ffn_b2, L0_ffn_Wout, L0_ffn_bout, L1_attn_segment_pos, L1_attn_a_param, L1_attn_ig_w, L1_attn_ig_b, L1_attn_ag_w, L1_attn_ag_b, L1_ffn_gate_w, L1_ffn_gate_b, L1_ffn_w1, L1_ffn_w3, L1_ffn_w2):
    import jax
    import jax.numpy as jnp

    def _L0_tok_ref(input_ids, attention_mask, emb, pca_lookup, proj_w, proj_b, fus_w, fus_b, ln_g, ln_b):
        import jax, jax.numpy as jnp
        import numpy as np
        WINDOW_SIZE = 3
        LN_EPS = 1e-05

        def _sliding_window_features(base_pca, mask_f):
            B, S, F = base_pca.shape
            h = WINDOW_SIZE // 2
            idx = jnp.arange(S)
            start = jnp.maximum(idx - h, 0)
            end = jnp.minimum(idx + h + 1, S)
            masked = base_pca * mask_f[..., None]
            csum = jnp.pad(jnp.cumsum(masked, axis=1), ((0, 0), (1, 0), (0, 0)))
            wsum = csum[:, end, :] - csum[:, start, :]
            mcs = jnp.pad(jnp.cumsum(mask_f, axis=1), ((0, 0), (1, 0)))
            lengths = jnp.maximum(mcs[:, end] - mcs[:, start], 1.0)
            return wsum / lengths[..., None]
        token_embeds = emb[input_ids]
        base_pca = pca_lookup[input_ids]
        pca_feat = _sliding_window_features(base_pca, attention_mask.astype(jnp.float32))
        cont = pca_feat @ proj_w + proj_b
        combined = jnp.concatenate([token_embeds, cont], axis=-1)
        fused = combined @ fus_w + fus_b
        mu = jnp.mean(fused, axis=-1, keepdims=True)
        var = jnp.mean(jnp.square(fused - mu), axis=-1, keepdims=True)
        return (fused - mu) * jax.lax.rsqrt(var + LN_EPS) * ln_g + ln_b

    def _L0_attn_ref(queries, Wq, bq, Wk, bk, Wv, bv, Wo, bo, pos_bias):
        import jax, jax.numpy as jnp
        import numpy as np
        D_MODEL = 256
        NHEAD = 16
        MAX_LEN = 512
        B, L = (2, 512)
        Bq, L1, D = queries.shape
        L2 = L1
        H = NHEAD
        Dh = D // H
        q = queries @ Wq.T + bq
        k = queries @ Wk.T + bk
        v = queries @ Wv.T + bv
        q = q.reshape(Bq, L1, H, Dh).transpose(0, 2, 1, 3)
        k = k.reshape(Bq, L2, H, Dh).transpose(0, 2, 1, 3)
        v = v.reshape(Bq, L2, H, Dh).transpose(0, 2, 1, 3)
        idx = jnp.arange(L1)[:, None] - jnp.arange(L2)[None, :] + (L2 - 1)
        attn_mask = pos_bias[:, idx]
        scale = 1.0 / jnp.sqrt(jnp.asarray(Dh, dtype=q.dtype))
        scores = jnp.einsum('bhqd,bhkd->bhqk', q, k) * scale + attn_mask[None]
        attn = jax.nn.softmax(scores, axis=-1)
        heads = jnp.einsum('bhqk,bhkd->bhqd', attn, v)
        out = heads.transpose(0, 2, 1, 3).reshape(Bq, L1, D)
        return out @ Wo.T + bo

    def _L0_ffn_ref(x, Win, bin_, W1, b1, W2, b2, Wout, bout):
        import jax, jax.numpy as jnp
        import numpy as np
        D_MODEL = 256
        M = 64
        INNER = 16
        s = jnp.einsum('btd,dm->btm', x, Win) + bin_
        h = jax.nn.relu(s[..., None] * W1 + b1)
        g = jnp.einsum('btmh,mh->btm', h, W2) + b2
        out = jnp.einsum('btm,md->btd', g, Wout) + bout
        return out

    def _L1_attn_ref(x, segment_pos, a_param, ig_w, ig_b, ag_w, ag_b):
        import jax, jax.numpy as jnp
        import numpy as np
        B, T, D, H = (8, 1024, 256, 8)

        def _block_linear(x, w, b):
            Bx, Tx, Dx = x.shape
            h, bw = (w.shape[0], w.shape[1])
            xb = x.reshape(Bx, Tx, h, bw)
            y = jnp.einsum('bthi,hij->bthj', xb, w) + b
            return y.reshape(Bx, Tx, Dx)

        def _rglru(x, a_param, ig_w, ig_b, ag_w, ag_b, sqrt_fn):
            gate_x = jax.nn.sigmoid(_block_linear(x, ig_w, ig_b))
            gate_a = jax.nn.sigmoid(_block_linear(x, ag_w, ag_b))
            log_a = -8.0 * gate_a * jax.nn.softplus(a_param)
            a = jnp.exp(log_a)
            a2 = jnp.exp(2.0 * log_a)
            multiplier = sqrt_fn(jnp.maximum(1.0 - a2, 1e-07))
            normed_x = x * gate_x * multiplier
            p = jnp.cumprod(a, axis=1)
            p_prefix = jnp.concatenate([jnp.ones_like(p[:, :1]), p[:, :-1]], axis=1)
            p_prefix = jnp.maximum(p_prefix, 1e-07)
            S = jnp.cumsum(normed_x / p_prefix, axis=1)
            h = p_prefix * S
            return (h, h[:, -1, :])

        def _reference_tuple_inner(x, segment_pos, a_param, ig_w, ig_b, ag_w, ag_b):
            y, last_h = _rglru(x, a_param, ig_w, ig_b, ag_w, ag_b, jnp.sqrt)
            return (y, last_h)
        return _reference_tuple_inner(x, segment_pos, a_param, ig_w, ig_b, ag_w, ag_b)[0]

    def _L1_ffn_ref(hidden_states, gate_w, gate_b, w1, w3, w2):
        import jax, jax.numpy as jnp
        import numpy as np
        HIDDEN = 256
        FFN = 1024
        NUM_EXPERTS = 8
        TOP_K = 2
        BATCH, SEQ = (2, 512)
        B, S, D = hidden_states.shape
        T = B * S
        x = hidden_states.reshape(T, D)
        logits = x @ gate_w + gate_b
        probs = jax.nn.softmax(logits.astype(jnp.float32), axis=-1)
        top_w, top_idx = jax.lax.top_k(probs, TOP_K)
        top_w = top_w / jnp.sum(top_w, axis=-1, keepdims=True)
        combine = jnp.zeros((T, NUM_EXPERTS), jnp.float32)
        combine = combine.at[jnp.arange(T)[:, None], top_idx].set(top_w)
        combine = combine.astype(x.dtype)
        h = jax.nn.silu(jnp.einsum('td,edf->tef', x, w1)) * jnp.einsum('td,edf->tef', x, w3)
        out_e = jnp.einsum('tef,efd->ted', h, w2)
        out = jnp.einsum('ted,te->td', out_e, combine)
        return out.reshape(B, S, D)
    h = _L0_tok_ref(x, mask_BS_i1_0, L0_tok_emb, L0_tok_pca_lookup, L0_tok_proj_w, L0_tok_proj_b, L0_tok_fus_w, L0_tok_fus_b, L0_tok_ln_g, L0_tok_ln_b)
    h = h + _L0_attn_ref(_layernorm(h, axis=-1), L0_attn_Wq, L0_attn_bq, L0_attn_Wk, L0_attn_bk, L0_attn_Wv, L0_attn_bv, L0_attn_Wo, L0_attn_bo, L0_attn_pos_bias)
    h = h + _L0_ffn_ref(_layernorm(h, axis=-1), L0_ffn_Win, L0_ffn_bin_, L0_ffn_W1, L0_ffn_b1, L0_ffn_W2, L0_ffn_b2, L0_ffn_Wout, L0_ffn_bout)
    h = h + _L1_attn_ref(_layernorm(h, axis=-1), L1_attn_segment_pos, L1_attn_a_param, L1_attn_ig_w, L1_attn_ig_b, L1_attn_ag_w, L1_attn_ag_b)
    h = h + _L1_ffn_ref(_layernorm(h, axis=-1), L1_ffn_gate_w, L1_ffn_gate_b, L1_ffn_w1, L1_ffn_w3, L1_ffn_w2)
    return h

_drawn_inputs = setup_inputs


def setup_inputs(seed=0):
    import zlib

    import numpy as np

    out = dict(_drawn_inputs(seed))
    spreads = {'L0_tok_proj_b': (0.0, 0.1),
     'L0_tok_fus_b': (0.0, 0.1),
     'L0_tok_ln_g': (1.0, 0.2),
     'L0_tok_ln_b': (0.0, 0.1),
     'L0_attn_bq': (0.0, 0.8),
     'L0_attn_bk': (0.0, 0.8),
     'L0_attn_bv': (0.0, 0.1),
     'L0_attn_bo': (0.0, 0.1),
     'L1_attn_ig_b': (0.0, 0.1),
     'L1_attn_ag_b': (0.0, 0.327)}
    factors = {'L0_tok_emb': 4.922,
     'L0_attn_Wq': 8.0,
     'L0_attn_Wk': 8.0,
     'L0_attn_pos_bias': 8.0,
     'L0_ffn_bin_': 8.0,
     'L1_ffn_gate_w': 8.0,
     'L1_ffn_gate_b': 8.0,
     'L1_ffn_w1': 8.0,
     'L1_ffn_w3': 8.0,
     'L1_ffn_w2': 8.0}
    for name, (base, spread) in spreads.items():
        noise = np.random.default_rng([zlib.crc32(name.encode()), seed]).standard_normal(out[name].shape)
        drawn = base * np.exp(spread * noise) if base else spread * noise
        out[name] = jnp.asarray(drawn.astype(out[name].dtype))
    for name, factor in factors.items():
        out[name] = (out[name] * factor).astype(out[name].dtype)
    return out
```

```python
from contextlib import ExitStack

import concourse.bass as bass
from concourse import mybir

F32 = mybir.dt.float32
BF16 = mybir.dt.bfloat16
F16 = mybir.dt.float16
I32 = mybir.dt.int32
U32 = mybir.dt.uint32
ALU = mybir.AluOpType
ACT = mybir.ActivationFunctionType
AX = mybir.AxisListType

P = 128
B, S, D = 8, 512, 256
C = D // P
T = S // P
TILES = B * T
V = 28
HEADS, DH = 16, 16
PAIRS = HEADS // 2
MAXLEN = 512
SCALE = float(DH) ** -0.5
BIASW = S + MAXLEN - P
SPLITS = ((0, 0), (0, 1), (1, 0), (1, 1), (0, 2), (2, 0))
STACK = DH * len(SPLITS)
VW = 3 * DH + 1
LIFT = 10.0
M, INNER = 64, 16
FFN, EXPERTS = 1024, 8
SLOTS = 2 * TILES + EXPERTS
EPS = 1e-5
TOKENS = B * S
XW = D + 1


class Phase:

    used = []

    def __init__(self, nc, ctx, name):
        self.nc, self.ctx, self.name = nc, ctx, name

    def sb(self, name, shape, dt=F32):
        return self.ctx.enter_context(self.nc.sbuf_tensor(f"{self.name}_{name}", shape, dt))

    def ps(self, name, shape, dt=F32):
        return self.ctx.enter_context(self.nc.psum_tensor(f"{self.name}_{name}", shape, dt))

    def sem(self, name):
        Phase.used.append(self.nc.alloc_semaphore(f"{self.name}_{name}"))
        return Phase.used[-1]


def recycle(nc):
    nc.clear_and_free_semaphores(Phase.used)
    Phase.used = []
    with nc.Block() as block:
        @block.gpsimd
        def _(pool):
            pool.nop(nofuse=True)


def row_to_all(dram_row, n=P):
    return dram_row.rearrange("(a w) -> a w", a=1).partition_broadcast(n)


def columns(dram_vec):
    return dram_vec.rearrange("(c p) -> p c", p=P)


def constants(nc, K):
    with ExitStack() as ctx:
        ph = Phase(nc, ctx, "const")
        s_id = ph.sem("id")
        row = ph.sb("row", [P, 1], I32)
        block = ctx.enter_context(nc.Block())

        @block.gpsimd
        def _(pool):
            pool.memset(K.ident[:], 1.0).then_inc(s_id, 1)
            pool.wait_ge(s_id, 1)
            pool.affine_select(out=K.ident[:], in_=K.ident[:], compare_op=ALU.is_equal, fill=0.0, base=0,
                               pattern=[[-1, P]], channel_multiplier=1).then_inc(s_id, 1)
            pool.memset(K.minus_half[:], -0.5).then_inc(s_id, 1)
            pool.iota(row[:], [[0, 1]], base=2 * TOKENS, channel_multiplier=1).then_inc(s_id, 1)
            pool.memset(K.pad[:], 0.0).then_inc(s_id, 1)
            pool.wait_ge(s_id, 5)

        @block.vector
        def _(dve):
            dve.wait_ge(s_id, 5)
            dve.tensor_copy(K.pad[:, D:XW], row[:]).then_inc(s_id, 1)
            dve.wait_ge(s_id, 6)


def rstd_from_stats(dve, pool, K, st, sems, done=0):
    s_var, s_rstd, s_chain = sems
    ev, od = K.stats[:, :, 0:3], K.stats[:, :, 3:6]
    if dve is not None:
        n = done

        def step(ins):
            nonlocal n
            n += 1
            ins.then_inc(s_chain, 1)
            dve.wait_ge(s_chain, n)

        step(dve.tensor_tensor(K.mean[:], ev[:, :, 1], od[:, :, 1], ALU.add))
        step(dve.tensor_scalar(K.mean[:], K.mean[:], 0.5, None, ALU.mult))
        step(dve.tensor_tensor(K.var[:], ev[:, :, 1], od[:, :, 1], ALU.subtract))
        step(dve.scalar_tensor_tensor(K.var[:], K.var[:], 0.25, K.var[:], ALU.mult, ALU.mult))
        step(dve.scalar_tensor_tensor(K.var[:], ev[:, :, 2], 1.0 / D, K.var[:], ALU.mult, ALU.add))
        step(dve.scalar_tensor_tensor(K.var[:], od[:, :, 2], 1.0 / D, K.var[:], ALU.mult, ALU.add))
        dve.tensor_scalar(K.var[:], K.var[:], EPS, None, ALU.add).then_inc(s_var, 1)
    if pool is not None:
        pool.wait_ge(s_var, 1)
        pool.tensor_tensor(K.rstd[:], K.var[:], K.minus_half[:], ALU.pow).then_inc(s_rstd, 1)


def embed(nc, K, x, mask, embT, pcaT, proj_w, proj_b, fus_w, fus_b, ln_g, ln_b, rlen_dram):
    HB = B // 2
    with ExitStack() as ctx:
        ph = Phase(nc, ctx, "emb")
        ids = ph.sb("ids", [P, HB, S], I32)
        mk = ph.sb("mk", [P, HB, S], I32)
        m8 = ph.sb("m8", [B, S], I32)
        mf = ph.sb("mf", [B, S + 2])
        rl8 = ph.sb("rl8", [B, S])
        rl = ph.sb("rl", [P, HB, S])
        vocab = ph.sb("vocab", [P, 1], I32)
        vocabf = ph.sb("vocabf", [P, 1])
        onerow = ph.sb("onerow", [P, 1])
        hot = ph.sb("hot", [P, HB, S])
        win = ph.sb("win", [P, HB, S + 2])
        embT_sb = ph.sb("embT", [P, C, V])
        pcaT_sb = ph.sb("pcaT", [20, V])
        proj_sb = ph.sb("proj", [20, D])
        projb_sb = ph.sb("projb", [P, C])
        fus_sb = ph.sb("fus", [P, 2 * C, D])
        fusb_sb = ph.sb("fusb", [1, D])
        fold = ph.sb("fold", [P, 2 * C, P])
        foldb = ph.sb("foldb", [1, P])
        table = ph.sb("table", [P, D])
        g_sb = ph.sb("g", [P, D])
        b_sb = ph.sb("b", [P, D])
        ps_c = ph.ps("c", [P, C, V])
        ps_t = ph.ps("t", [P, D])
        ps_f = [ph.ps(f"f{i}", [P, 2, D]) for i in range(4)]
        s_io, s_w, s_m8, s_voc, s_rl, s_rlb = (ph.sem(n) for n in ("io", "w", "m8", "voc", "rl", "rlb"))
        s_zero, s_fold, s_c, s_tab, s_tabsb, s_cols = (ph.sem(n) for n in ("zero", "fold", "c", "tab", "tabsb", "cols"))
        s_mm, s_keep, s_st, s_ch, s_var, s_rstd, s_ln = (ph.sem(n) for n in ("mm", "keep", "st", "ch", "var", "rstd", "ln"))
        block = ctx.enter_context(nc.Block())

        @block.sync
        def _(sp):
            sp.dma_start(m8[:], mask).then_inc(s_m8, 16)
            for h in range(2):
                sp.dma_start(ids[64 * h:64 * h + 64].rearrange("p b s -> p (b s)"),
                             row_to_all(x[HB * h:HB * h + HB].rearrange("b s -> (b s)"), 64)).then_inc(s_io, 16)
                sp.dma_start(mk[64 * h:64 * h + 64].rearrange("p b s -> p (b s)"),
                             row_to_all(mask[HB * h:HB * h + HB].rearrange("b s -> (b s)"), 64)).then_inc(s_io, 16)
            sp.wait_ge(s_rl, 1)
            sp.dma_start(rlen_dram[:], rl8[:]).then_inc(s_rlb, 16)
            sp.wait_ge(s_rlb, 16)
            for h in range(2):
                sp.dma_start(rl[64 * h:64 * h + 64].rearrange("p b s -> p (b s)"),
                             row_to_all(rlen_dram[HB * h:HB * h + HB].rearrange("b s -> (b s)"), 64)).then_inc(s_rlb, 16)

        @block.scalar
        def _(act):
            act.dma_start(fus_sb[:], fus_w.rearrange("(c p) n -> p c n", p=P)).then_inc(s_w, 16)
            act.dma_start(embT_sb[:], embT.rearrange("(c p) v -> p c v", p=P)).then_inc(s_w, 16)
            act.dma_start(pcaT_sb[:], pcaT).then_inc(s_w, 16)
            act.dma_start(proj_sb[:], proj_w).then_inc(s_w, 16)
            act.dma_start(projb_sb[:], columns(proj_b), allow_slow_non_contiguous=True).then_inc(s_w, 16)
            act.dma_start(fusb_sb[:], fus_b.rearrange("(a n) -> a n", a=1)).then_inc(s_w, 16)
            act.dma_start(g_sb[:], row_to_all(ln_g)).then_inc(s_w, 16)
            act.dma_start(b_sb[:], row_to_all(ln_b)).then_inc(s_w, 16)
            for i in range(TILES // 2):
                act.wait_ge(s_mm, i + 1)
                act.activation(K.H[:, 2 * i:2 * i + 2, :], ps_f[i % 4][:], ACT.Copy).then_inc(s_keep, 1)

        @block.gpsimd
        def _(pool):
            pool.iota(vocab[:], [[0, 1]], base=0, channel_multiplier=1).then_inc(s_voc, 1)
            pool.memset(fold[:], 0.0).then_inc(s_zero, 1)
            pool.memset(foldb[:], 0.0).then_inc(s_zero, 1)
            pool.memset(win[:], 0.0).then_inc(s_zero, 1)
            rstd_from_stats(None, pool, K, None, (s_var, s_rstd, s_ch))

        @block.tensor
        def _(pe):
            pe.wait_ge(s_w, 128)
            for c in range(C):
                pe.matmul(ps_c[:, c, :], proj_sb[:, c * P:(c + 1) * P], pcaT_sb[:], start=True, stop=True).then_inc(s_c, 1)
            pe.wait_ge(s_fold, 1)
            for c in range(2 * C):
                pe.matmul(ps_t[:], fold[:, c, :], fus_sb[:, c, :], start=(c == 0), stop=False)
            pe.matmul(ps_t[:], foldb[:], fusb_sb[:], start=False, stop=True).then_inc(s_tab, 1)
            pe.wait_ge(s_tabsb, 1)
            pe.wait_ge(s_cols, 1)
            for i in range(TILES // 2):
                if i >= 4:
                    pe.wait_ge(s_keep, i - 3)
                for j in range(2):
                    t = 2 * i + j
                    h, b, q = t // (TILES // 2), t // T % HB, t % T
                    last = pe.matmul(ps_f[i % 4][:, j, :], hot[64 * h:64 * h + 64, b, q * P:(q + 1) * P],
                                     table[64 * h:64 * h + 64, :], start=True, stop=True)
                last.then_inc(s_mm, 1)

        @block.vector
        def _(dve):
            n = 0

            def step(ins):
                nonlocal n
                n += 1
                ins.then_inc(s_ch, 1)
                dve.wait_ge(s_ch, n)

            step(dve.memset(mf[:], 0.0))
            dve.wait_ge(s_m8, 16)
            step(dve.tensor_copy(mf[:, 1:S + 1], m8[:]))
            step(dve.tensor_tensor(rl8[:], mf[:, 0:S], mf[:, 1:S + 1], ALU.add))
            step(dve.tensor_tensor(rl8[:], rl8[:], mf[:, 2:S + 2], ALU.add))
            step(dve.tensor_scalar(rl8[:], rl8[:], 1.0, None, ALU.max))
            n += 1
            dve.reciprocal(rl8[:], rl8[:]).then_inc(s_ch, 1)
            dve.wait_ge(s_ch, n)
            dve.sem_inc(s_rl, 1)
            dve.wait_ge(s_voc, 1)
            step(dve.tensor_single_scalar(vocab[:], vocab[:], 31, ALU.bitwise_and))
            step(dve.tensor_copy(vocabf[:], vocab[:]))
            step(dve.tensor_scalar(onerow[:], vocabf[:], float(V), None, ALU.is_equal))
            dve.wait_ge(s_zero, 3)
            dve.wait_ge(s_w, 128)
            dve.wait_ge(s_c, C)
            for h in range(2):
                step(dve.tensor_copy(fold[:, 0:C, 64 * h:64 * h + V], embT_sb[:]))
                step(dve.tensor_copy(fold[:, C:2 * C, 64 * h + 32:64 * h + 32 + V], ps_c[:]))
                step(dve.tensor_copy(fold[:, C:2 * C, 64 * h + V:64 * h + V + 1], projb_sb[:].rearrange("p (c a) -> p c a", a=1)))
                step(dve.memset(foldb[:, 64 * h + V:64 * h + V + 1], 1.0))
            dve.sem_inc(s_fold, 1)
            dve.wait_ge(s_io, 64)
            for h in range(2):
                p = slice(64 * h, 64 * h + 32)
                step(dve.tensor_scalar(hot[p], ids[p], vocabf[p], onerow[p], ALU.is_equal, ALU.max))
            step(dve.scalar_tensor_tensor(win[:, :, 1:S + 1], ids[:], vocabf[:], mk[:], ALU.is_equal, ALU.mult))
            for h in range(2):
                p = slice(64 * h + 32, 64 * h + 64)
                step(dve.tensor_tensor(hot[p], win[p, :, 0:S], win[p, :, 1:S + 1], ALU.add))
                step(dve.tensor_tensor(hot[p], hot[p], win[p, :, 2:S + 2], ALU.add))
            dve.wait_ge(s_rlb, 48)
            for h in range(2):
                p = slice(64 * h + 32, 64 * h + 64)
                step(dve.tensor_tensor(hot[p], hot[p], rl[p], ALU.mult))
            dve.sem_inc(s_cols, 1)
            dve.wait_ge(s_tab, 1)
            dve.tensor_copy(table[:], ps_t[:]).then_inc(s_tabsb, 1)
            for i in range(TILES // 2):
                dve.wait_ge(s_keep, i + 1)
                for j in range(2):
                    last = dve.bn_stats(K.stats[:, 2 * i + j, :], K.H[:, 2 * i + j, :])
                last.then_inc(s_st, 1)
            dve.wait_ge(s_st, TILES // 2)
            rstd_from_stats(dve, None, K, None, (s_var, s_rstd, s_ln))
            dve.wait_ge(s_rstd, 1)
            dve.wait_ge(s_keep, TILES // 2)
            base = 6
            for t in range(TILES):
                dve.scalar_tensor_tensor(K.H[:, t, :], K.H[:, t, :], K.mean[:, t:t + 1], g_sb[:], ALU.subtract, ALU.mult)\
                   .then_inc(s_ln, 1)
                if t >= 1:
                    dve.wait_ge(s_ln, base + 2 * t - 1)
                    dve.scalar_tensor_tensor(K.H[:, t - 1, :], K.H[:, t - 1, :], K.rstd[:, t - 1:t], b_sb[:], ALU.mult, ALU.add)\
                       .then_inc(s_ln, 1)
            dve.wait_ge(s_ln, base + 2 * TILES - 1)
            dve.scalar_tensor_tensor(K.H[:, TILES - 1, :], K.H[:, TILES - 1, :], K.rstd[:, TILES - 1:TILES], b_sb[:], ALU.mult, ALU.add)\
               .then_inc(s_ln, 1)
            for t in range(TILES):
                if t % 8 == 0:
                    dve.wait_ge(s_ln, min(base + 2 * (t + 8) + 1, base + 2 * TILES))
                last = dve.bn_stats(K.stats[:, t, :], K.H[:, t, :])
            last.then_inc(s_st, 1)
            dve.wait_ge(s_st, TILES // 2 + 1)


def slots(eng, body):
    with eng.Fori(0, B // 2 - 1) as i:
        for k in range(2):
            body(i, k, True)
    body(B // 2 - 1, 0, True)
    body(B // 2 - 1, 1, False)


def apply_norm(dve, K, xn, b):
    for q in range(T):
        t = b * T + q
        last = dve.tensor_scalar(xn[:, q, :], K.H[:, bass.ds(t, 1), :].rearrange("p a d -> p (a d)"),
                                 K.mean[:, bass.ds(t, 1)], K.rstd[:, bass.ds(t, 1)], ALU.subtract, ALU.mult)
    return last


def transpose_row(pe, K, xp, xn):
    for q in range(T):
        for c in range(C):
            last = pe.transpose(xp[:, c, q * P:(q + 1) * P], xn[:, q, c * P:(c + 1) * P], K.ident[:])
    return last


def project_qkv(nc, K, wqT, bq, wkT, bk, wvT, bv, q_dram, k_dram, v_dram):
    with ExitStack() as ctx:
        ph = Phase(nc, ctx, "qkv")
        w_sb = {n: ph.sb(f"w{n}", [P, C, D]) for n in "qkv"}
        bq_sb, bk_sb, bqs = ph.sb("bq", [P, C]), ph.sb("bk", [P, C]), ph.sb("bqs", [P, C])
        bv_sb = ph.sb("bv", [P, D])
        xn = [ph.sb(f"xn{k}", [P, T, D]) for k in range(2)]
        xt = [ph.sb(f"xt{k}", [P, C, S]) for k in range(2)]
        full = {n: ph.sb(f"full{n}", [P, C * S]) for n in "qkv"}
        rest = {n: ph.sb(f"rest{n}", [P, C * S]) for n in "qkv"}
        part = {n: [ph.sb(f"part{n}{k}", [P, 3, C, S], BF16) for k in range(2)] for n in "qk"}
        vpart = [ph.sb(f"partv{k}", [P, PAIRS, T, 2 * VW], BF16) for k in range(2)]
        xp = ph.ps("xp", [P, C, S])
        ps = {n: ph.ps(f"ps{n}", [P, C * S]) for n in "qkv"}
        s_w, s_ones, s_bq, s_xn, s_T, s_xt = (ph.sem(n) for n in ("w", "ones", "bq", "xn", "T", "xt"))
        s_ch, s_var, s_rstd = (ph.sem(n) for n in ("ch", "var", "rstd"))
        s_mm, s_full, s_hi, s_rest, s_mid, s_lo = ({n: ph.sem(f"{m}{n}") for n in "qkv"}
                                                  for m in ("mm", "full", "hi", "rest", "mid", "lo"))
        s_out = [ph.sem(f"out{k}") for k in range(2)]
        NOUT = 16 * (2 * len(SPLITS) + 1)
        block = ctx.enter_context(nc.Block())

        def vcols(tile, q, part):
            return tile[:, :, q, :].rearrange("p h (e w) -> p h e w", e=2)[:, :, :, part * DH:(part + 1) * DH]

        def vfull(tile, q):
            return tile[:, q * D:(q + 1) * D].rearrange("p (h e d) -> p h e d", e=2, d=DH)

        @block.sync
        def _(sp):
            for n, w in zip("qkv", (wqT, wkT, wvT)):
                sp.dma_start(w_sb[n][:], w.rearrange("(c p) n -> p c n", p=P)).then_inc(s_w, 16)
            sp.dma_start(bq_sb[:], columns(bq), allow_slow_non_contiguous=True).then_inc(s_w, 16)
            sp.dma_start(bk_sb[:], columns(bk), allow_slow_non_contiguous=True).then_inc(s_w, 16)
            sp.dma_start(bv_sb[:], row_to_all(bv)).then_inc(s_w, 16)

            def body(i, k, more):
                b = 2 * i + k
                for side, (n, dram) in enumerate((("q", q_dram), ("k", k_dram))):
                    sp.wait_ge(s_lo[n], b + 1)
                    for blk, parts in enumerate(SPLITS):
                        sp.dma_start(dram[bass.ds(b, 1), blk].rearrange("a (c p) s -> p (a c) s", p=P),
                                     part[n][k][:, parts[side], :, :]).then_inc(s_out[k], 16)
                sp.wait_ge(s_lo["v"], b + 1)
                sp.dma_start(v_dram[:, bass.ds(b, 1)].rearrange("h a p w -> p (a h) w"),
                             vpart[k][:].rearrange("p h q w -> p h (q w)")).then_inc(s_out[k], 16)

            slots(sp, body)
            for k in range(2):
                sp.wait_ge(s_out[k], NOUT * (B // 2))

        @block.tensor
        def _(pe):
            def turn(b, k):
                pe.wait_ge(s_xn, b + 1)
                pe.wait_ge(s_xt, b)
                transpose_row(pe, K, xp, xn[k]).then_inc(s_T, 1)

            def body(i, k, more):
                b = 2 * i + k
                if more:
                    turn(b + 1, 1 - k)
                pe.wait_ge(s_xt, b + 1)
                for n in "qk":
                    pe.wait_ge(s_full[n], b)
                    for m in range(C):
                        for c in range(C):
                            last = pe.matmul(ps[n][:, m * S:(m + 1) * S], w_sb[n][:, c, m * P:(m + 1) * P], xt[k][:, c, :],
                                             start=(c == 0), stop=(c == C - 1))
                    last.then_inc(s_mm[n], 1)
                pe.wait_ge(s_full["v"], b)
                for q in range(T):
                    for c in range(C):
                        last = pe.matmul(ps["v"][:, q * D:(q + 1) * D], xt[k][:, c, q * P:(q + 1) * P], w_sb["v"][:, c, :],
                                         start=(c == 0), stop=(c == C - 1))
                last.then_inc(s_mm["v"], 1)

            turn(0, 0)
            pe.wait_ge(s_w, 96)
            slots(pe, body)

        @block.scalar
        def _(act):
            def body(i, k, more):
                b = 2 * i + k
                if more:
                    act.wait_ge(s_T, b + 2)
                    act.wait_ge(s_mm["v"], b)
                    act.activation(xt[1 - k][:], xp[:], ACT.Copy).then_inc(s_xt, 1)
                act.wait_ge(s_out[k], NOUT * i)
                for n in "qk":
                    act.wait_ge(s_full[n], b + 1)
                    act.activation(part[n][k][:, 0].rearrange("p c s -> p (c s)"), full[n][:], ACT.Copy).then_inc(s_hi[n], 1)
                act.wait_ge(s_full["v"], b + 1)
                for q in range(T):
                    last = act.activation(vcols(vpart[k], q, 0), vfull(full["v"], q), ACT.Copy)
                last.then_inc(s_hi["v"], 1)
                for n in "qk":
                    act.wait_ge(s_rest[n], b + 1)
                    act.activation(part[n][k][:, 1].rearrange("p c s -> p (c s)"), rest[n][:], ACT.Copy).then_inc(s_mid[n], 1)
                act.wait_ge(s_rest["v"], b + 1)
                for q in range(T):
                    last = act.activation(vcols(vpart[k], q, 1), vfull(rest["v"], q), ACT.Copy)
                last.then_inc(s_mid["v"], 1)

            act.wait_ge(s_T, 1)
            act.activation(xt[0][:], xp[:], ACT.Copy).then_inc(s_xt, 1)
            act.wait_ge(s_ones, 2)
            slots(act, body)

        @block.gpsimd
        def _(pool):
            rstd_from_stats(None, pool, K, None, (s_var, s_rstd, s_ch))
            for k in range(2):
                pool.memset(vpart[k][:], 1.0).then_inc(s_ones, 1)

            def body(i, k, more):
                b = 2 * i + k
                for n in "qk":
                    pool.wait_ge(s_hi[n], b + 1)
                    pool.wait_ge(s_lo[n], b)
                    pool.tensor_tensor(rest[n][:], full[n][:], part[n][k][:, 0].rearrange("p c s -> p (c s)"), ALU.subtract)\
                        .then_inc(s_rest[n], 1)
                pool.wait_ge(s_hi["v"], b + 1)
                pool.wait_ge(s_lo["v"], b)
                for q in range(T):
                    last = pool.tensor_tensor(vfull(rest["v"], q), vfull(full["v"], q), vcols(vpart[k], q, 0), ALU.subtract)
                last.then_inc(s_rest["v"], 1)

            slots(pool, body)

        @block.vector
        def _(dve):
            rstd_from_stats(dve, None, K, None, (s_var, s_rstd, s_ch))
            dve.wait_ge(s_rstd, 1)
            dve.wait_ge(s_w, 96)
            dve.tensor_scalar(bqs[:], bq_sb[:], SCALE, None, ALU.mult).then_inc(s_bq, 1)
            apply_norm(dve, K, xn[0], 0).then_inc(s_xn, 1)
            dve.wait_ge(s_bq, 1)

            def body(i, k, more):
                b = 2 * i + k
                if more:
                    dve.wait_ge(s_T, b)
                    apply_norm(dve, K, xn[1 - k], b + 1).then_inc(s_xn, 1)
                for n in "qk":
                    dve.wait_ge(s_mm[n], b + 1)
                    dve.wait_ge(s_rest[n], b)
                    for m in range(C):
                        cols = slice(m * S, (m + 1) * S)
                        if n == "q":
                            last = dve.tensor_scalar(full[n][:, cols], ps[n][:, cols], SCALE, bqs[:, m:m + 1], ALU.mult, ALU.add)
                        else:
                            last = dve.tensor_scalar(full[n][:, cols], ps[n][:, cols], bk_sb[:, m:m + 1], None, ALU.add)
                    last.then_inc(s_full[n], 1)
                dve.wait_ge(s_mm["v"], b + 1)
                dve.wait_ge(s_rest["v"], b)
                dve.tensor_tensor(full["v"][:].rearrange("p (q d) -> p q d", d=D), ps["v"][:].rearrange("p (q d) -> p q d", d=D),
                                  bv_sb[:].rearrange("p (a d) -> p a d", a=1).to_broadcast([P, T, D]), ALU.add)\
                   .then_inc(s_full["v"], 1)
                for n in "qk":
                    dve.wait_ge(s_mid[n], b + 1)
                    dve.tensor_tensor(part[n][k][:, 2].rearrange("p c s -> p (c s)"), rest[n][:],
                                      part[n][k][:, 1].rearrange("p c s -> p (c s)"), ALU.subtract).then_inc(s_lo[n], 1)
                dve.wait_ge(s_mid["v"], b + 1)
                for q in range(T):
                    last = dve.tensor_tensor(vcols(vpart[k], q, 2), vfull(rest["v"], q), vcols(vpart[k], q, 1), ALU.subtract)
                last.then_inc(s_lo["v"], 1)

            slots(dve, body)


def attention(nc, K, pos_bias, q_dram, k_dram, v_dram, heads_dram):
    BODY = 8
    PER_HP = B * 4 // BODY
    UNITS = PAIRS * B * 4
    EXP_LAG, T_LAG, HI_LAG, LO_LAG, PV_LAG, NORM_LAG = 1, 2, 2, 3, 4, 5
    with ExitStack() as ctx:
        ph = Phase(nc, ctx, "att")
        qs = [ph.sb(f"qs{k}", [STACK, 2, S], BF16) for k in range(2)]
        ks = [ph.sb(f"ks{k}", [STACK, 2, S], BF16) for k in range(2)]
        vs = [ph.sb(f"vs{k}", [P, T, 2 * VW], BF16) for k in range(2)]
        bias = [ph.sb(f"bias{k}", [P, 2, BIASW]) for k in range(2)]
        score = [ph.sb(f"score{k}", [P, 2, S]) for k in range(4)]
        top = [ph.sb(f"top{k}", [P, 2]) for k in range(4)]
        shift = [ph.sb(f"shift{k}", [P, 2]) for k in range(4)]
        prob = [ph.sb(f"prob{k}", [P, 2, S]) for k in range(2)]
        hi = [ph.sb(f"hi{k}", [P, 2, T, P], F16) for k in range(2)]
        lo = [ph.sb(f"lo{k}", [P, 2, T, P], F16) for k in range(2)]
        osum = [ph.sb(f"osum{k}", [P, 2, T, DH]) for k in range(2)]
        rec = [ph.sb(f"rec{k}", [P, 2, T]) for k in range(2)]
        heads = [ph.sb(f"heads{k}", [P, T, 2, DH]) for k in range(2)]
        ps_s = [ph.ps(f"s{j}", [P, S]) for j in range(2)]
        ps_t = [ph.ps(f"t{k}", [P, 2, T, P]) for k in range(2)]
        ps_o = [ph.ps(f"o{k}", [P, 512]) for k in range(2)]
        s_qk, s_top, s_shift, s_exp, s_turn, s_hi, s_lo, s_pv, s_norm, s_part = (
            ph.sem(n) for n in ("qk", "top", "shift", "exp", "turn", "hi", "lo", "pv", "norm", "part"))
        s_ldqk = [ph.sem(f"ldqk{k}") for k in range(2)]
        s_ldv = [ph.sem(f"ldv{k}") for k in range(2)]
        s_bias = [ph.sem(f"bias{k}") for k in range(2)]
        s_store = [ph.sem(f"store{k}") for k in range(2)]
        block = ctx.enter_context(nc.Block())

        def wait(eng, sem, value):
            if not (isinstance(value, int) and value <= 0):
                eng.wait_ge(sem, value)

        def flat(eng, steps):
            for j in range(BODY):
                steps(0, j)
            with eng.Fori(1, UNITS // BODY) as m:
                for j in range(BODY):
                    steps(m, j)
            for j in range(BODY):
                steps(UNITS // BODY, j)

        def live(m, j, lag):
            return not (isinstance(m, int) and not 0 <= m * BODY + j - lag < UNITS)

        @block.sync
        def _(sp):
            def load_bias(hp, k):
                src = bass.AP(pos_bias.tensor, pos_bias.offset + hp * (2 * (2 * MAXLEN - 1)),
                              [[1, P], [2 * MAXLEN - 1, 2], [1, BIASW]])
                sp.dma_start(bias[k][:], src).then_inc(s_bias[k], 16)

            def load_pair(hp, b, n, k):
                wait(sp, s_qk, 8 * (n - 1))
                for dst, dram in ((qs, q_dram), (ks, k_dram)):
                    for e in range(2):
                        sp.dma_start(dst[k][:, e, :], dram[bass.ds(b, 1), :, bass.ds(hp * 2 * DH + e * DH, DH), :]
                                     .rearrange("a c d s -> (a c) d s")).then_inc(s_ldqk[k], 16)
                wait(sp, s_pv, 4 * (n - 1))
                sp.dma_start(vs[k][:].rearrange("p q w -> p (q w)"),
                             v_dram[bass.ds(hp, 1), bass.ds(b, 1)].rearrange("h a p w -> (h a p) w"))\
                    .then_inc(s_ldv[k], 16)

            def rows(hp, first):
                for k in range(2):
                    load_pair(hp, k, hp * B + k, k)
                with sp.Fori(1, B // 2) as i:
                    for k in range(2):
                        load_pair(hp, 2 * i + k, hp * B + 2 * i + k, k)

            load_bias(0, 0)
            load_bias(1, 1)
            rows(0, True)
            rows(1, False)
            with sp.Fori(1, PAIRS // 2) as i:
                for k in range(2):
                    hp = 2 * i + k
                    sp.wait_ge(s_top, (hp - 1) * (2 * 4 * B))
                    load_bias(hp, k)
                    with sp.Fori(0, B // 2) as r:
                        for kk in range(2):
                            load_pair(hp, 2 * r + kk, hp * B + 2 * r + kk, kk)

        @block.gpsimd
        def _(pool):
            def store(n, k):
                pool.wait_ge(s_norm, n + 1)
                pool.dma_start(heads_dram[bass.ds(n, 1)].rearrange("a p w -> (a p) w"),
                               heads[k][:].rearrange("p q e d -> p (q e d)")).then_inc(s_store[k], 16)

            with pool.Fori(0, PAIRS * B // 2) as i:
                for k in range(2):
                    store(2 * i + k, k)
            for k in range(2):
                pool.wait_ge(s_store[k], 16 * (PAIRS * B // 2))

        @block.tensor
        def _(pe):
            def steps(m, j):
                if live(m, j, 0):
                    e, half, k = j // 2 % 2, j % 2, j // 4
                    if j % 4 == 0:
                        pe.wait_ge(s_ldqk[k], 64 * m + 64)
                    for t in range(2):
                        tile = 2 * (m * BODY + j) + t
                        wait(pe, s_top, tile - 1)
                        q = 2 * half + t
                        pe.matmul(ps_s[t][:], qs[k][:, e, q * P:(q + 1) * P], ks[k][:, e, :], start=True, stop=True)\
                            .then_inc(s_qk, 1)
                if live(m, j, PV_LAG):
                    jj = (j - PV_LAG) % BODY
                    u = m * BODY + j - PV_LAG
                    e, half, k, sl = jj // 2 % 2, jj % 2, jj // 4, jj % 2
                    if jj % 4 == 0:
                        n = 2 * m + (j - PV_LAG) // 4
                        pe.wait_ge(s_ldv[k], 16 * (m + (j - PV_LAG) // BODY) + 16)
                        wait(pe, s_norm, n - 1)
                    pe.wait_ge(s_lo, u + 1)
                    for t in range(2):
                        o = (e * T + 2 * half + t) * VW
                        for kt in range(T):
                            for part in (hi, lo):
                                last = pe.matmul(ps_o[k][:, o:o + VW], part[sl][:, t, kt, :], vs[k][:, kt, e * VW:(e + 1) * VW],
                                                 start=(kt == 0 and part is hi), stop=(kt == T - 1 and part is lo))
                    last.then_inc(s_pv, 1)
                if live(m, j, T_LAG):
                    u = m * BODY + j - T_LAG
                    sl = (j - T_LAG) % 2
                    pe.wait_ge(s_exp, u + 1)
                    wait(pe, s_lo, u - 1)
                    for t in range(2):
                        for kt in range(T):
                            last = pe.transpose(ps_t[sl][:, t, kt, :], prob[sl][:, t, kt * P:(kt + 1) * P], K.ident[:])
                    last.then_inc(s_turn, 1)

            flat(pe, steps)

        @block.scalar
        def _(act):
            def steps(m, j):
                if live(m, j, EXP_LAG):
                    u, jj = m * BODY + j - EXP_LAG, (j - EXP_LAG) % BODY
                    act.wait_ge(s_shift, u + 1)
                    wait(act, s_turn, u - 1)
                    for t in range(2):
                        last = act.activation(prob[jj % 2][:, t, :], score[jj % 4][:, t, :], ACT.Exp, bias=shift[jj % 4][:, t:t + 1])
                    last.then_inc(s_exp, 1)
                if live(m, j, HI_LAG):
                    u, jj = m * BODY + j - HI_LAG, (j - HI_LAG) % BODY
                    act.wait_ge(s_turn, u + 1)
                    wait(act, s_pv, u - 1)
                    act.activation(hi[jj % 2][:], ps_t[jj % 2][:], ACT.Copy).then_inc(s_hi, 1)

            flat(act, steps)

        @block.vector
        def _(dve):
            def steps(m, j, bk):
                if live(m, j, 0):
                    e, half, r = j // 2 % 2, j % 2, j % 4
                    u = m * BODY + j
                    wait(dve, s_exp, u - 3)
                    for t in range(2):
                        dve.wait_ge(s_qk, 2 * u + t + 1)
                        dve.nop(nofuse=True)
                        off = (2 * half + t) * P
                        dve.tensor_tensor_reduce(score[r][:, t, :], ps_s[t][:], bias[bk][:, e, off:off + S][:, ::-1], 1.0, -3.0e38,
                                                 ALU.add, ALU.max, top[r][:, t:t + 1]).then_inc(s_top, 1)
                    dve.wait_ge(s_top, 2 * u + 2)
                    dve.tensor_scalar(shift[r][:], top[r][:], -1.0, LIFT, ALU.mult, ALU.add).then_inc(s_shift, 1)
                if live(m, j, LO_LAG):
                    u, sl = m * BODY + j - LO_LAG, (j - LO_LAG) % 2
                    dve.wait_ge(s_hi, u + 1)
                    wait(dve, s_pv, u - 1)
                    dve.tensor_tensor(lo[sl][:], ps_t[sl][:], hi[sl][:], ALU.subtract).then_inc(s_lo, 1)
                if (j - NORM_LAG) % 4 == 3 and live(m, j, NORM_LAG):
                    k = (j - NORM_LAG) % BODY // 4
                    n = 2 * m + (j - NORM_LAG) // 4
                    dve.wait_ge(s_pv, m * BODY + j - NORM_LAG + 1)
                    wait(dve, s_store[k], 16 * (m + (j - NORM_LAG) // BODY))
                    o = ps_o[k][:, 0:2 * T * VW].rearrange("p (e w) -> p e w", w=VW)
                    dve.tensor_reduce(osum[k][:].rearrange("p e q d -> p (e q) d"),
                                      o[:, :, 0:3 * DH].rearrange("p e (c d) -> p e d c", d=DH), AX.X, ALU.add).then_inc(s_part, 1)
                    dve.reciprocal(rec[k][:].rearrange("p e q -> p (e q)"), o[:, :, 3 * DH]).then_inc(s_part, 1)
                    dve.wait_ge(s_part, 2 * n + 2)
                    dve.tensor_tensor(heads[k][:].rearrange("p q e d -> p e q d"), osum[k][:],
                                      rec[k][:].rearrange("p e (q a) -> p e q a", a=1).to_broadcast([P, 2, T, DH]), ALU.mult)\
                        .then_inc(s_norm, 1)

            def bodies(first, last, bk):
                with dve.Fori(first, last) as m:
                    for j in range(BODY):
                        steps(m, j, bk)

            dve.wait_ge(s_bias[0], 16)
            for j in range(BODY):
                steps(0, j, 0)
            bodies(1, PER_HP, 0)
            dve.wait_ge(s_bias[1], 16)
            bodies(PER_HP, 2 * PER_HP, 1)
            with dve.Fori(1, PAIRS // 2) as h:
                for bk in range(2):
                    dve.wait_ge(s_bias[bk], 16 * h + 16)
                    bodies(h * (2 * PER_HP) + bk * PER_HP, h * (2 * PER_HP) + (bk + 1) * PER_HP, bk)
            for j in range(BODY):
                steps(UNITS // BODY, j, 0)


def attention_output(nc, K, heads_dram, woT, bo):
    with ExitStack() as ctx:
        ph = Phase(nc, ctx, "wo")
        w = ph.sb("w", [P, C, D])
        bo_sb = ph.sb("bo", [P, D])
        heads = [ph.sb(f"heads{k}", [P, T, PAIRS, 2 * DH]) for k in range(2)]
        ht = [ph.sb(f"ht{k}", [P, C, S]) for k in range(2)]
        xp = ph.ps("xp", [P, C, S])
        po = [ph.ps(f"po{k}", [P, T, D]) for k in range(2)]
        s_w, s_T, s_ht, s_mm, s_add, s_bias, s_st, s_ch, s_var, s_rstd = (
            ph.sem(n) for n in ("w", "T", "ht", "mm", "add", "bias", "st", "ch", "var", "rstd"))
        s_in = [ph.sem(f"in{k}") for k in range(2)]
        block = ctx.enter_context(nc.Block())

        @block.sync
        def _(sp):
            sp.dma_start(w[:], woT.rearrange("(c p) n -> p c n", p=P)).then_inc(s_w, 16)
            sp.dma_start(bo_sb[:], row_to_all(bo)).then_inc(s_w, 16)

            def load(b, k):
                row = heads_dram.rearrange("(h b) p w -> b p h w", b=B)[bass.ds(b, 1)].rearrange("a p h w -> (a p) h w")
                for q in range(T):
                    sp.dma_start(heads[k][:, q], row[:, :, q * 2 * DH:(q + 1) * 2 * DH]).then_inc(s_in[k], 16)

            for k in range(2):
                load(k, k)
            with sp.Fori(1, B // 2) as i:
                for k in range(2):
                    sp.wait_ge(s_T, 2 * i + k - 1)
                    load(2 * i + k, k)

        @block.tensor
        def _(pe):
            def turn(i, b, k):
                pe.wait_ge(s_in[k], 16 * T * i + 16 * T)
                pe.wait_ge(s_ht, b)
                for q in range(T):
                    for c in range(C):
                        last = pe.transpose(xp[:, c, q * P:(q + 1) * P], heads[k][:, q, 4 * c:4 * c + 4, :].rearrange("p h d -> p (h d)"), K.ident[:])
                last.then_inc(s_T, 1)

            def body(i, k, more):
                b = 2 * i + k
                if more:
                    turn(i + k, b + 1, 1 - k)
                pe.wait_ge(s_ht, b + 1)
                pe.wait_ge(s_add, b)
                for q in range(T):
                    for c in range(C):
                        last = pe.matmul(po[k][:, q, :], ht[k][:, c, q * P:(q + 1) * P], w[:, c, :], start=(c == 0), stop=(c == C - 1))
                last.then_inc(s_mm, 1)

            turn(0, 0, 0)
            pe.wait_ge(s_w, 32)
            slots(pe, body)

        @block.scalar
        def _(act):
            def body(i, k, more):
                b = 2 * i + k
                act.wait_ge(s_T, b + 1)
                if not (isinstance(i, int) and i == 0):
                    act.wait_ge(s_mm, b)
                else:
                    act.wait_ge(s_mm, b)
                act.activation(ht[k][:], xp[:], ACT.Copy).then_inc(s_ht, 1)

            slots(act, body)

        @block.gpsimd
        def _(pool):
            rstd_from_stats(None, pool, K, None, (s_var, s_rstd, s_ch))

        @block.vector
        def _(dve):
            dve.wait_ge(s_w, 32)

            def body(i, k, more):
                b = 2 * i + k
                rows = K.H[:, bass.ds(b * T, T), :]
                dve.tensor_tensor(rows, rows, bo_sb[:].rearrange("p (a d) -> p a d", a=1).to_broadcast([P, T, D]), ALU.add)\
                   .then_inc(s_bias, 1)
                dve.wait_ge(s_bias, b + 1)
                dve.wait_ge(s_mm, b + 1)
                dve.tensor_tensor(rows, rows, po[k][:], ALU.add).then_inc(s_add, 1)
                dve.wait_ge(s_add, b + 1)
                stats_of_row(dve, K, b).then_inc(s_st, 1)

            slots(dve, body)
            dve.wait_ge(s_st, B)
            rstd_from_stats(dve, None, K, None, (s_var, s_rstd, s_ch))
            dve.wait_ge(s_rstd, 1)


def stats_of_row(dve, K, b):
    for q in range(T):
        last = dve.bn_stats(K.stats[:, bass.ds(b * T + q, 1), :].rearrange("p a d -> p (a d)"),
                            K.H[:, bass.ds(b * T + q, 1), :].rearrange("p a d -> p (a d)"))
    return last


def inner_ffn(nc, K, w_in, b_in, w1, b1, w2, b2, w_out, b_out, xs_dram):
    RING = 4
    with ExitStack() as ctx:
        ph = Phase(nc, ctx, "ffn")
        win_sb = ph.sb("win", [P, C, M])
        bin_sb = ph.sb("bin", [P, 1])
        w1_sb, b1_sb, w2_sb = (ph.sb(n, [P, INNER]) for n in ("w1", "b1", "w2"))
        b2_sb = ph.sb("b2", [P, 1])
        wout_sb = ph.sb("wout", [P, D])
        bout_sb = ph.sb("bout", [P, D])
        xn = [ph.sb(f"xn{k}", [P, T, D]) for k in range(2)]
        xt = [ph.sb(f"xt{k}", [P, C, S]) for k in range(2)]
        sv = ph.sb("s", [P, S])
        unit = [ph.sb(f"unit{r}", [P, S]) for r in range(RING)]
        g = ph.sb("g", [P, S])
        xp = ph.ps("xp", [P, C, S])
        ps_s = ph.ps("sp", [P, S])
        po = [ph.ps(f"po{k}", [P, T, D]) for k in range(2)]
        s_w, s_xn, s_T, s_xt, s_s, s_sv, s_unit, s_g, s_mm, s_add, s_bias, s_st, s_ch, s_var, s_rstd = (
            ph.sem(n) for n in ("w", "xn", "T", "xt", "s", "sv", "unit", "g", "mm", "add", "bias", "st", "ch", "var", "rstd"))
        s_fill = ph.sem("fill")
        NLOAD = 16 * (2 + 2 * 6)
        block = ctx.enter_context(nc.Block())

        @block.sync
        def _(sp):
            sp.dma_start(win_sb[:], w_in.rearrange("(c p) n -> p c n", p=P)).then_inc(s_w, 16)
            sp.dma_start(bout_sb[:], row_to_all(b_out)).then_inc(s_w, 16)
            for h in range(2):
                half = slice(M * h, M * h + M)
                sp.dma_start(bin_sb[half], b_in.rearrange("(m a) -> m a", a=1)).then_inc(s_w, 16)
                sp.dma_start(b2_sb[half], b2.rearrange("(m a) -> m a", a=1)).then_inc(s_w, 16)
                sp.dma_start(w1_sb[half], w1).then_inc(s_w, 16)
                sp.dma_start(b1_sb[half], b1).then_inc(s_w, 16)
                sp.dma_start(w2_sb[half], w2).then_inc(s_w, 16)
                sp.dma_start(wout_sb[half], w_out).then_inc(s_w, 16)
            sp.dma_start(xs_dram.rearrange("(t p) w -> p t w", p=P),
                         K.pad[:].rearrange("p (a w) -> p a w", a=1).to_broadcast([P, SLOTS, XW])).then_inc(s_fill, 16)
            sp.wait_ge(s_fill, 16)

        @block.tensor
        def _(pe):
            pe.wait_ge(s_w, NLOAD)

            with pe.Fori(0, B // 2) as i:
                for k in range(2):
                    b = 2 * i + k
                    pe.wait_ge(s_xn, b + 1)
                    pe.wait_ge(s_xt, b)
                    transpose_row(pe, K, xp, xn[k]).then_inc(s_T, 1)
                    pe.wait_ge(s_xt, b + 1)
                    pe.wait_ge(s_sv, i)
                    for c in range(C):
                        last = pe.matmul(ps_s[M * k:M * k + M, :], win_sb[:, c, :], xt[k][:, c, :], start=(c == 0), stop=(c == C - 1))
                    last.then_inc(s_s, 1)
                pe.wait_ge(s_g, INNER * i + INNER)
                for k in range(2):
                    pe.wait_ge(s_add, 2 * i)
                    for q in range(T):
                        last = pe.matmul(po[k][:, q, :], g[M * k:M * k + M, q * P:(q + 1) * P], wout_sb[M * k:M * k + M, :],
                                         start=True, stop=True)
                    last.then_inc(s_mm, 1)

        @block.scalar
        def _(act):
            act.wait_ge(s_w, NLOAD)
            with act.Fori(0, B // 2) as i:
                for k in range(2):
                    b = 2 * i + k
                    act.wait_ge(s_T, b + 1)
                    act.wait_ge(s_s, b)
                    act.activation(xt[k][:], xp[:], ACT.Copy).then_inc(s_xt, 1)
                act.wait_ge(s_s, 2 * i + 2)
                act.wait_ge(s_unit, INNER * i)
                act.activation(sv[:], ps_s[:], ACT.Identity, bias=bin_sb[:]).then_inc(s_sv, 1)
                act.wait_ge(s_sv, i + 1)
                for h in range(INNER):
                    if h >= RING:
                        act.wait_ge(s_g, INNER * i + h - RING + 1)
                    else:
                        act.wait_ge(s_g, INNER * i)
                    act.activation(unit[h % RING][:], sv[:], ACT.Relu, scale=w1_sb[:, h:h + 1], bias=b1_sb[:, h:h + 1])\
                        .then_inc(s_unit, 1)

        @block.gpsimd
        def _(pool):
            rstd_from_stats(None, pool, K, None, (s_var, s_rstd, s_ch))

        @block.vector
        def _(dve):
            dve.wait_ge(s_w, NLOAD)
            with dve.Fori(0, B // 2) as i:
                for k in range(2):
                    b = 2 * i + k
                    dve.wait_ge(s_T, b)
                    apply_norm(dve, K, xn[k], b).then_inc(s_xn, 1)
                    rows = K.H[:, bass.ds(b * T, T), :]
                    dve.wait_ge(s_xn, b + 1)
                    dve.tensor_tensor(rows, rows, bout_sb[:].rearrange("p (a d) -> p a d", a=1).to_broadcast([P, T, D]), ALU.add)\
                       .then_inc(s_bias, 1)
                dve.wait_ge(s_mm, 2 * i)
                for h in range(INNER):
                    dve.wait_ge(s_unit, INNER * i + h + 1)
                    if h == 0:
                        last = dve.tensor_scalar(g[:], unit[0][:], w2_sb[:, 0:1], b2_sb[:], ALU.mult, ALU.add)
                    else:
                        dve.wait_ge(s_g, INNER * i + h)
                        last = dve.scalar_tensor_tensor(g[:], unit[h % RING][:], w2_sb[:, h:h + 1], g[:], ALU.mult, ALU.add)
                    last.then_inc(s_g, 1)
                for k in range(2):
                    b = 2 * i + k
                    rows = K.H[:, bass.ds(b * T, T), :]
                    dve.wait_ge(s_mm, b + 1)
                    dve.wait_ge(s_bias, b + 1)
                    dve.tensor_tensor(rows, rows, po[k][:], ALU.add).then_inc(s_add, 1)
                    dve.wait_ge(s_add, b + 1)
                    stats_of_row(dve, K, b).then_inc(s_st, 1)
            dve.wait_ge(s_st, B)
            rstd_from_stats(dve, None, K, None, (s_var, s_rstd, s_ch))
            dve.wait_ge(s_rstd, 1)


def recurrence(nc, K, a_param, ig_w, ig_b, ag_w, ag_b):
    FLOOR = 1e-7
    BLK = D // 8
    with ExitStack() as ctx:
        ph = Phase(nc, ctx, "rg")
        gate_in = ph.sb("gatein", [P, B, C, S])
        gate_a = ph.sb("gatea", [P, B, C, S])
        igw, agw = ph.sb("igw", [P, C, P]), ph.sb("agw", [P, C, P])
        igb, agb, ap = ph.sb("igb", [P, C]), ph.sb("agb", [P, C]), ph.sb("ap", [P, C])
        z, w, d, l, t1 = (ph.sb(n, [P, C]) for n in ("z", "w", "d", "l", "t1"))
        rate = {n: ph.sb(f"rate{n}", [P, C]) for n in (1, 2, -1)}
        s_w, s_z, s_ch, s_rate, s_act = (ph.sem(n) for n in ("w", "z", "ch", "rate", "act"))
        s_xn, s_T, s_xt, s_g, s_sig, s_xg = (ph.sem(n) for n in ("xn", "T", "xt", "g", "sig", "xg"))
        NLOAD = 16 * (3 + 16)
        with ExitStack() as c1:
            p1 = Phase(nc, c1, "rga")
            xn = [p1.sb(f"xn{k}", [P, T, D]) for k in range(2)]
            xt = [p1.sb(f"xt{k}", [P, C, S]) for k in range(2)]
            sig = [p1.sb(f"sig{k}", [P, C, S]) for k in range(2)]
            xp = p1.ps("xp", [P, C, S])
            ps_i = p1.ps("i", [P, C, S])
            ps_a = p1.ps("a", [P, C, S])
            block = c1.enter_context(nc.Block())

            @block.sync
            def _(sp):
                sp.dma_start(igb[:], columns(ig_b.rearrange("h w -> (h w)")), allow_slow_non_contiguous=True).then_inc(s_w, 16)
                sp.dma_start(agb[:], columns(ag_b.rearrange("h w -> (h w)")), allow_slow_non_contiguous=True).then_inc(s_w, 16)
                sp.dma_start(ap[:], columns(a_param), allow_slow_non_contiguous=True).then_inc(s_w, 16)
                sp.wait_ge(s_z, 2)
                for dst, src in ((igw, ig_w), (agw, ag_w)):
                    for blk in range(8):
                        at = blk % 4 * BLK
                        sp.dma_start(dst[at:at + BLK, blk // 4, at:at + BLK], src[blk]).then_inc(s_w, 16)

            @block.gpsimd
            def _(pool):
                pool.memset(igw[:], 0.0).then_inc(s_z, 1)
                pool.memset(agw[:], 0.0).then_inc(s_z, 1)

                def body(i, k, more):
                    b = 2 * i + k
                    pool.wait_ge(s_sig, 2 * b + 1)
                    pool.tensor_tensor(gate_in[:, bass.ds(b, 1)].rearrange("p a c s -> p (a c s)"),
                                       sig[k][:].rearrange("p c s -> p (c s)"), xt[k][:].rearrange("p c s -> p (c s)"), ALU.mult)\
                        .then_inc(s_xg, 1)

                slots(pool, body)

            @block.tensor
            def _(pe):
                def turn(b, k):
                    pe.wait_ge(s_xn, b + 1)
                    pe.wait_ge(s_xt, b)
                    transpose_row(pe, K, xp, xn[k]).then_inc(s_T, 1)

                def body(i, k, more):
                    b = 2 * i + k
                    if more:
                        turn(b + 1, 1 - k)
                    pe.wait_ge(s_xt, b + 1)
                    for n, (ps, gw) in enumerate(((ps_i, igw), (ps_a, agw))):
                        pe.wait_ge(s_sig, 2 * b - 1 + n if not isinstance(b, int) or b else 0)
                        for c in range(C):
                            last = pe.matmul(ps[:, c, :], gw[:, c, :], xt[k][:, c, :], start=True, stop=True)
                        last.then_inc(s_g, 1)

                turn(0, 0)
                pe.wait_ge(s_w, NLOAD)
                for k in range(2):
                    body(0, k, True)
                with pe.Fori(1, B // 2 - 1) as i:
                    for k in range(2):
                        body(i, k, True)
                body(B // 2 - 1, 0, True)
                body(B // 2 - 1, 1, False)

            @block.scalar
            def _(act):
                act.wait_ge(s_w, NLOAD)
                act.wait_ge(s_ch, 2)
                act.activation(z[:], t1[:], ACT.Exp).then_inc(s_act, 1)
                act.wait_ge(s_ch, 3)
                act.activation(l[:], w[:], ACT.Ln).then_inc(s_act, 1)

                def body(i, k, more):
                    b = 2 * i + k
                    if more:
                        act.wait_ge(s_T, b + 2)
                        act.wait_ge(s_xg, b)
                        act.activation(xt[1 - k][:], xp[:], ACT.Copy).then_inc(s_xt, 1)
                    act.wait_ge(s_g, 2 * b + 1)
                    act.wait_ge(s_xg, b)
                    for c in range(C):
                        last = act.activation(sig[k][:, c, :], ps_i[:, c, :], ACT.Sigmoid, bias=igb[:, c:c + 1])
                    last.then_inc(s_sig, 1)
                    act.wait_ge(s_g, 2 * b + 2)
                    act.nop(nofuse=True)
                    for c in range(C):
                        last = act.activation(gate_a[:, bass.ds(b, 1), c, :].rearrange("p a s -> p (a s)"), ps_a[:, c, :],
                                              ACT.Sigmoid, bias=agb[:, c:c + 1])
                    last.then_inc(s_sig, 1)

                act.wait_ge(s_T, 1)
                act.activation(xt[0][:], xp[:], ACT.Copy).then_inc(s_xt, 1)
                slots(act, body)

            @block.vector
            def _(dve):
                n = 0

                def step(ins):
                    nonlocal n
                    n += 1
                    ins.then_inc(s_ch, 1)
                    dve.wait_ge(s_ch, n)

                apply_norm(dve, K, xn[0], 0).then_inc(s_xn, 1)
                dve.wait_ge(s_w, NLOAD)
                step(dve.tensor_scalar(t1[:], ap[:], -1.0, None, ALU.mult))
                step(dve.tensor_tensor(t1[:], t1[:], ap[:], ALU.min))
                dve.wait_ge(s_act, 1)
                step(dve.tensor_scalar(w[:], z[:], 1.0, None, ALU.add))
                step(dve.tensor_scalar(d[:], w[:], -1.0, None, ALU.add))
                step(dve.tensor_scalar(t1[:], d[:], 0.0, None, ALU.is_equal))
                step(dve.tensor_tensor(d[:], d[:], t1[:], ALU.add))
                step(dve.reciprocal(d[:], d[:]))
                dve.wait_ge(s_act, 2)
                step(dve.tensor_tensor(l[:], l[:], d[:], ALU.mult))
                step(dve.tensor_tensor(l[:], l[:], t1[:], ALU.add))
                step(dve.tensor_tensor(l[:], l[:], z[:], ALU.mult))
                step(dve.tensor_scalar(ap[:], ap[:], 0.0, None, ALU.max))
                step(dve.tensor_tensor(l[:], l[:], ap[:], ALU.add))
                for m, r in rate.items():
                    dve.tensor_scalar(r[:], l[:], -8.0 * m, None, ALU.mult).then_inc(s_rate, 1)

                def body(i, k, more):
                    b = 2 * i + k
                    if more:
                        dve.wait_ge(s_T, b)
                        apply_norm(dve, K, xn[1 - k], b + 1).then_inc(s_xn, 1)

                slots(dve, body)
                dve.wait_ge(s_rate, 3)

        with ExitStack() as c2:
            p2 = Phase(nc, c2, "rgb")
            a = [p2.sb(f"a{k}", [P, C, S]) for k in range(2)]
            ai = [p2.sb(f"ai{k}", [P, C, S]) for k in range(2)]
            q = [p2.sb(f"q{k}", [P, C, S]) for k in range(2)]
            ratio = p2.sb("ratio", [P, B, C, S])
            h = [p2.sb(f"h{k}", [P, C, S]) for k in range(2)]
            cap = p2.sb("cap", [P, S])
            pt = [p2.ps(f"t{k}", [P, T, D]) for k in range(2)]
            s_a, s_ai, s_a2, s_q, s_r, s_om, s_root, s_x, s_h, s_turn, s_add, s_st, s_cap, s_c2, s_var, s_rstd = (
                p2.sem(n) for n in ("a", "ai", "a2", "q", "r", "om", "root", "x", "h", "turn", "add", "st", "cap", "c2", "var", "rstd"))
            block = c2.enter_context(nc.Block())

            def row(t, b):
                return t[:, bass.ds(b, 1)].rearrange("p a c s -> p (a c) s")

            @block.scalar
            def _(act):
                def body(i, k, more):
                    b = 2 * i + k
                    act.wait_ge(s_r, b)
                    act.nop(nofuse=True)
                    for c in range(C):
                        last = act.activation(a[k][:, c, :], row(gate_a, b)[:, c, :], ACT.Exp, scale=rate[1][:, c:c + 1])
                    last.then_inc(s_a, 1)
                    for c in range(C):
                        last = act.activation(ai[k][:, c, :], row(gate_a, b)[:, c, :], ACT.Exp, scale=rate[-1][:, c:c + 1])
                    last.then_inc(s_ai, 1)
                    act.wait_ge(s_ai, b + 1)
                    act.nop(nofuse=True)
                    for c in range(C):
                        last = act.activation(row(gate_a, b)[:, c, :], row(gate_a, b)[:, c, :], ACT.Exp, scale=rate[2][:, c:c + 1])
                    last.then_inc(s_a2, 1)

                slots(act, body)
                with act.Fori(0, B) as b:
                    act.wait_ge(s_om, b + 1)
                    act.nop(nofuse=True)
                    act.activation(row(gate_a, b), row(gate_a, b), ACT.Sqrt).then_inc(s_root, 1)

            @block.gpsimd
            def _(pool):
                with pool.Fori(0, B) as b:
                    pool.wait_ge(s_root, b + 1)
                    x = gate_in[:, bass.ds(b, 1)].rearrange("p a c s -> p (a c s)")
                    pool.tensor_tensor(x, x, gate_a[:, bass.ds(b, 1)].rearrange("p a c s -> p (a c s)"), ALU.mult).then_inc(s_x, 1)
                rstd_from_stats(None, pool, K, None, (s_var, s_rstd, s_c2))

            @block.tensor
            def _(pe):
                def body(i, k, more):
                    b = 2 * i + k
                    pe.wait_ge(s_h, b + 1)
                    pe.wait_ge(s_add, b)
                    for t in range(T):
                        for c in range(C):
                            last = pe.transpose(pt[k][:, t, c * P:(c + 1) * P], h[k][:, c, t * P:(t + 1) * P], K.ident[:])
                    last.then_inc(s_turn, 1)

                slots(pe, body)

            @block.vector
            def _(dve):
                dve.memset(cap[:], 1.0 / FLOOR).then_inc(s_cap, 1)
                for k in range(2):
                    dve.memset(q[k][:, :, 0:1], 1.0).then_inc(s_cap, 1)
                dve.memset(ratio[:, :, :, 0:1], 0.0).then_inc(s_cap, 1)
                dve.wait_ge(s_cap, 4)

                def body(i, k, more):
                    b = 2 * i + k
                    dve.wait_ge(s_ai, b + 1)
                    for c in range(C):
                        last = dve.tensor_tensor_scan(q[k][:, c, 1:S], ai[k][:, c, 0:S - 1], cap[:, 0:S - 1], 1.0, ALU.mult, ALU.min)
                    last.then_inc(s_q, 1)
                    dve.wait_ge(s_q, b + 1)
                    dve.wait_ge(s_a, b + 1)
                    dve.scalar_tensor_tensor(row(ratio, b)[:, :, 1:S], q[k][:, :, 0:S - 1], FLOOR, a[k][:, :, 0:S - 1], ALU.mult, ALU.max)\
                       .then_inc(s_r, 1)
                    dve.wait_ge(s_a2, b + 1)
                    dve.tensor_scalar(row(gate_a, b), row(gate_a, b), -1.0, 1.0, ALU.mult, ALU.add).then_inc(s_c2, 1)
                    dve.wait_ge(s_c2, b + 1)
                    dve.tensor_scalar(row(gate_a, b), row(gate_a, b), FLOOR, None, ALU.max).then_inc(s_om, 1)

                slots(dve, body)

                def scan(i, k, more):
                    b = 2 * i + k
                    dve.wait_ge(s_x, b + 1)
                    dve.wait_ge(s_turn, b)
                    for c in range(C):
                        last = dve.tensor_tensor_scan(h[k][:, c, :], row(ratio, b)[:, c, :], row(gate_in, b)[:, c, :], 0.0,
                                                      ALU.mult, ALU.add)
                    last.then_inc(s_h, 1)
                    dve.wait_ge(s_turn, b + 1)
                    rows = K.H[:, bass.ds(b * T, T), :]
                    dve.tensor_tensor(rows, rows, pt[k][:], ALU.add).then_inc(s_add, 1)
                    dve.wait_ge(s_add, b + 1)
                    stats_of_row(dve, K, b).then_inc(s_st, 1)

                slots(dve, scan)
                dve.wait_ge(s_st, B)
                rstd_from_stats(dve, None, K, None, (s_var, s_rstd, s_c2), B)
                dve.wait_ge(s_rstd, 1)


def route(nc, K, gate_w, gate_b, h_dram, xs_dram):
    E = EXPERTS
    with ExitStack() as ctx:
        ph = Phase(nc, ctx, "route")
        gw, gb = ph.sb("gw", [P, C, E]), ph.sb("gb", [P, E])
        xa = [ph.sb(f"xa{j}", [P, TILES, XW]) for j in range(2)]
        xt = [ph.sb(f"xt{k}", [P, C, S]) for k in range(2)]
        tok_i, tok = ph.sb("toki", [P, TILES], I32), ph.sb("tok", [P, TILES])
        rank_i, rank = ph.sb("ranki", [P, E], I32), ph.sb("rank", [P, E])
        start_i, start = ph.sb("starti", [1, SLOTS], I32), ph.sb("start", [1, SLOTS])
        before, ones = ph.sb("before", [P, P]), ph.sb("ones", [P, P])
        pr, eq, tot, inc, slot, hit = (ph.sb(n, [P, TILES, E]) for n in ("pr", "eq", "tot", "inc", "slot", "hit"))
        pick = [ph.sb(f"pick{j}", [P, TILES, E]) for j in range(2)]
        best = [ph.sb(f"best{j}", [P, TILES]) for j in range(2)]
        col, posf = ph.sb("col", [P, TILES]), ph.sb("posf", [P, TILES])
        size, end, base = ph.sb("size", [P, E]), ph.sb("end", [P, E]), ph.sb("base", [P, E])
        size_i = ph.sb("sizei", [P, E], I32)
        ge = ph.sb("ge", [1, SLOTS, E])
        owner = ph.sb("owner", [1, SLOTS])
        pos = [ph.sb(f"pos{j}", [P, TILES], U32) for j in range(2)]
        xp = ph.ps("xp", [P, C, S])
        ps_g = [ph.ps(f"g{k}", [P, T, E]) for k in range(2)]
        ps_b, ps_n = ph.ps("b", [P, TILES, E]), ph.ps("n", [P, TILES, E])
        s_w, s_const, s_made, s_xn, s_T, s_xt, s_g, s_lg, s_ch, s_sub, s_exp, s_pick, s_cnt, s_copy, s_pos, s_xs, s_h, s_half = (
            ph.sem(n) for n in ("w", "const", "made", "xn", "T", "xt", "g", "lg", "ch", "sub", "exp", "pick", "cnt", "copy",
                                "pos", "xs", "h", "half"))
        block = ctx.enter_context(nc.Block())

        @block.sync
        def _(sp):
            sp.dma_start(gw[:], gate_w.rearrange("(c p) n -> p c n", p=P)).then_inc(s_w, 16)
            sp.dma_start(gb[:], row_to_all(gate_b)).then_inc(s_w, 16)
            sp.dma_start(h_dram.rearrange("(t p) d -> p t d", p=P), K.H[:]).then_inc(s_h, 16)
            sp.wait_ge(s_h, 16)

        @block.gpsimd
        def _(pool):
            pool.iota(tok_i[:], [[P, TILES]], base=0, channel_multiplier=1).then_inc(s_const, 1)
            pool.iota(rank_i[:], [[-1, E]], base=E, channel_multiplier=0).then_inc(s_const, 1)
            pool.iota(start_i[:], [[P, SLOTS]], base=0, channel_multiplier=0).then_inc(s_const, 1)
            pool.memset(ones[:], 1.0).then_inc(s_const, 1)
            pool.wait_ge(s_const, 4)
            pool.affine_select(out=before[:], in_=ones[:], compare_op=ALU.is_gt, fill=0.0, base=0,
                               pattern=[[1, P]], channel_multiplier=-1).then_inc(s_const, 1)
            pool.wait_ge(s_copy, B)
            for j in range(2):
                pool.wait_ge(s_pos, j + 1)
                for t in range(TILES):
                    pool.indirect_dma_start(out=xs_dram[:], out_offset=bass.IndirectOffsetOnAxis(ap=pos[j][:, t:t + 1], axis=0),
                                            in_=xa[j][:, t, :], in_offset=None).then_inc(s_xs, 16)
            pool.wait_ge(s_xs, 16 * 2 * TILES)

        @block.tensor
        def _(pe):
            def turn(b):
                pe.wait_ge(s_xn, b + 1)
                pe.wait_ge(s_xt, b)
                for q in range(T):
                    for c in range(C):
                        last = pe.transpose(xp[:, c, q * P:(q + 1) * P], xa[0][:, b * T + q, c * P:(c + 1) * P], K.ident[:])
                last.then_inc(s_T, 1)

            turn(0)
            pe.wait_ge(s_w, 32)
            for b in range(B):
                if b + 1 < B:
                    turn(b + 1)
                pe.wait_ge(s_xt, b + 1)
                if b >= 2:
                    pe.wait_ge(s_lg, b - 1)
                for q in range(T):
                    for c in range(C):
                        last = pe.matmul(ps_g[b % 2][:, q, :], xt[b % 2][:, c, q * P:(q + 1) * P], gw[:, c, :],
                                         start=(c == 0), stop=(c == C - 1))
                last.then_inc(s_g, 1)
            pe.wait_ge(s_pick, 1)
            pe.wait_ge(s_const, 5)
            both = hit[:].rearrange("p t e -> p (t e)")
            pe.matmul(ps_b[:].rearrange("p t e -> p (t e)"), before[:], both, start=True, stop=True)
            pe.matmul(ps_n[:].rearrange("p t e -> p (t e)"), ones[:], both, start=True, stop=True).then_inc(s_cnt, 1)

        @block.scalar
        def _(act):
            for b in range(B):
                act.wait_ge(s_T, b + 1)
                if b >= 2:
                    act.wait_ge(s_g, b - 1)
                act.activation(xt[b % 2][:], xp[:], ACT.Copy).then_inc(s_xt, 1)
                act.activation(xa[1][:, b * T:b * T + T, 0:D], xa[0][:, b * T:b * T + T, 0:D], ACT.Copy).then_inc(s_copy, 1)
            act.wait_ge(s_sub, 1)
            act.activation(pr[:], pr[:], ACT.Exp).then_inc(s_exp, 1)

        @block.vector
        def _(dve):
            n = 0

            def step(ins):
                nonlocal n
                n += 1
                ins.then_inc(s_ch, 1)
                dve.wait_ge(s_ch, n)

            def wide(col):
                return col[:].rearrange("p (t a) -> p t a", a=1).to_broadcast([P, TILES, E])

            def by_expert(row, n=TILES, parts=P):
                return row[0:parts].rearrange("p (a e) -> p a e", a=1).to_broadcast([parts, n, E])

            for b in range(B):
                for q in range(T):
                    t = b * T + q
                    last = dve.tensor_scalar(xa[0][:, t, 0:D], K.H[:, t, :], K.mean[:, t:t + 1], K.rstd[:, t:t + 1],
                                             ALU.subtract, ALU.mult)
                last.then_inc(s_xn, 1)
            dve.wait_ge(s_const, 5)
            step(dve.tensor_copy(tok[:], tok_i[:]))
            step(dve.tensor_copy(rank[:], rank_i[:]))
            step(dve.tensor_copy(start[:], start_i[:]))
            step(dve.tensor_copy(xa[0][:, :, D:XW], tok[:].rearrange("p (t a) -> p t a", a=1)))
            step(dve.tensor_scalar(xa[1][:, :, D:XW], tok[:].rearrange("p (t a) -> p t a", a=1), float(TOKENS), None, ALU.add))
            dve.wait_ge(s_w, 32)
            for b in range(B):
                dve.wait_ge(s_g, b + 1)
                dve.tensor_tensor(pr[:, b * T:b * T + T, :], ps_g[b % 2][:], by_expert(gb, T), ALU.add).then_inc(s_lg, 1)
            dve.wait_ge(s_lg, B)
            step(dve.tensor_reduce(col[:], pr[:], AX.X, ALU.max))
            dve.tensor_tensor(pr[:], pr[:], wide(col), ALU.subtract).then_inc(s_sub, 1)
            dve.wait_ge(s_exp, 1)
            step(dve.tensor_reduce(col[:], pr[:], AX.X, ALU.add))
            step(dve.reciprocal(col[:], col[:]))
            step(dve.tensor_tensor(pr[:], pr[:], wide(col), ALU.mult))
            for j in range(2):
                step(dve.tensor_reduce(best[j][:], pr[:], AX.X, ALU.max))
                step(dve.tensor_tensor(eq[:], pr[:], wide(best[j]), ALU.is_equal))
                step(dve.tensor_tensor(eq[:], eq[:], by_expert(rank), ALU.mult))
                step(dve.tensor_reduce(col[:], eq[:], AX.X, ALU.max))
                step(dve.tensor_tensor(pick[j][:], eq[:], wide(col), ALU.is_equal))
                if j == 0:
                    step(dve.scalar_tensor_tensor(pr[:], pick[0][:], -2.0, pr[:], ALU.mult, ALU.add))
            dve.tensor_tensor(hit[:], pick[0][:], pick[1][:], ALU.add).then_inc(s_pick, 1)
            step(dve.tensor_tensor(col[:], best[0][:], best[1][:], ALU.add))
            step(dve.reciprocal(col[:], col[:]))
            for j in range(2):
                step(dve.tensor_tensor(K.share[j][:], best[j][:], col[:], ALU.mult))
            dve.wait_ge(s_cnt, 1)
            step(dve.tensor_copy(tot[:], ps_n[:]))
            step(dve.memset(eq[:], 1.0))
            for e in range(E):
                step(dve.tensor_tensor_scan(inc[:, :, e], eq[:, :, e], tot[:, :, e], 0.0, ALU.mult, ALU.add))
            step(dve.tensor_scalar(size[:], inc[:, TILES - 1, :], float(P - 1), None, ALU.add))
            step(dve.tensor_copy(size_i[:], size[:]))
            step(dve.tensor_single_scalar(size_i[:], size_i[:], 0x7FFFFFFF - (P - 1), ALU.bitwise_and))
            step(dve.tensor_copy(size[:], size_i[:]))
            step(dve.tensor_tensor_scan(end[:], eq[:, 0, :], size[:], 0.0, ALU.mult, ALU.add))
            step(dve.tensor_tensor(base[:], end[:], size[:], ALU.subtract))
            step(dve.tensor_tensor(slot[:], inc[:], tot[:], ALU.subtract))
            step(dve.tensor_tensor(slot[:], slot[:], ps_b[:], ALU.add))
            step(dve.tensor_tensor(slot[:], slot[:], by_expert(base), ALU.add))
            for j in range(2):
                step(dve.tensor_tensor(eq[:], pick[j][:], slot[:], ALU.mult))
                step(dve.tensor_reduce(posf[:], eq[:], AX.X, ALU.add))
                dve.tensor_copy(pos[j][:], posf[:]).then_inc(s_pos, 1)
                dve.wait_ge(s_pos, j + 1)
            step(dve.tensor_tensor(ge[:], start[:].rearrange("p (t a) -> p t a", a=1).to_broadcast([1, SLOTS, E]),
                                   by_expert(end, SLOTS, 1), ALU.is_ge))
            step(dve.tensor_reduce(owner[:], ge[:], AX.X, ALU.add))
            step(dve.tensor_scalar(owner[:], owner[:], float(E - 1), None, ALU.min))
            step(dve.tensor_copy(K.owner[:], owner[:]))


def experts(nc, K, w1, w3, w2, xs_dram, y_dram):
    HALF = FFN // 2
    FC = FFN // P
    with ExitStack() as ctx:
        ph = Phase(nc, ctx, "moe")
        w1_sb, w3_sb = (ph.sb(n, [P, EXPERTS, C, FFN]) for n in ("w1", "w3"))
        w2_sb = ph.sb("w2", [P, EXPERTS, FC, D])
        xin = [ph.sb(f"xin{k}", [P, D]) for k in range(2)]
        dest_all = ph.sb("destall", [P, SLOTS])
        xt = [ph.sb(f"xt{k}", [P, C, P]) for k in range(2)]
        dest = [ph.sb(f"dest{k}", [P, 1], U32) for k in range(2)]
        h = ph.sb("h", [P, 2, HALF])
        ht = ph.sb("ht", [P, 2, FC // 2, P])
        y = [ph.sb(f"y{k}", [P, D]) for k in range(2)]
        ps_a = [ph.ps(f"a{j}", [P, HALF]) for j in range(2)]
        ps_b = [ph.ps(f"b{j}", [P, HALF]) for j in range(2)]
        ps_h = [ph.ps(f"h{j}", [P, FC // 2, P]) for j in range(2)]
        ps_y = ph.ps("y", [P, 512])
        ps_x = ph.ps("x", [P, 4, P])
        s_w, s_turnx, s_xt, s_turnh, s_mmy, s_yc, s_dest = (ph.sem(n) for n in ("w", "turnx", "xt", "turnh", "mmy", "yc", "dest"))
        s_x = [ph.sem(f"x{k}") for k in range(2)]
        s_out = ph.sem("out")
        s_a, s_b, s_silu, s_h, s_ht = ([ph.sem(f"{n}{j}") for j in range(2)] for n in ("a", "b", "silu", "h", "ht"))
        block = ctx.enter_context(nc.Block())

        @block.sync
        def _(sp):
            def load(t, k):
                sp.dma_start(xin[k][:], xs_dram[bass.ds(t * P, P), 0:D]).then_inc(s_x[k], 16)

            for k in range(2):
                load(k, k)
            sp.dma_start(dest_all[:], xs_dram[:, D:XW].rearrange("(t p) a -> p (t a)", p=P), allow_slow_non_contiguous=True)\
                .then_inc(s_dest, 16)
            with sp.Fori(1, SLOTS // 2) as i:
                for k in range(2):
                    sp.wait_ge(s_turnx, 2 * i + k - 1)
                    load(2 * i + k, k)

        @block.gpsimd
        def _(pool):
            for e in range(EXPERTS):
                pool.dma_start(w1_sb[:, e], w1[e].rearrange("(c p) f -> p c f", p=P)).then_inc(s_w, 16)
                pool.dma_start(w3_sb[:, e], w3[e].rearrange("(c p) f -> p c f", p=P)).then_inc(s_w, 16)
                pool.dma_start(w2_sb[:, e], w2[e].rearrange("(c p) n -> p c n", p=P)).then_inc(s_w, 16)
                pool.wait_ge(s_w, 48 * e + 48)

            def store(i, k):
                t = 2 * i + k
                pool.wait_ge(s_yc, t + 1)
                pool.wait_ge(s_out, 16 * t)
                pool.nop(nofuse=True)
                pool.indirect_dma_start(out=y_dram[:], out_offset=bass.IndirectOffsetOnAxis(ap=dest[k][:, 0:1], axis=0),
                                        in_=y[k][:], in_offset=None).then_inc(s_out, 16)

            with pool.Fori(0, SLOTS // 2) as i:
                for k in range(2):
                    store(i, k)
            pool.wait_ge(s_out, 16 * SLOTS)

        @block.tensor
        def _(pe):
            def turn_x(i, t, k):
                pe.wait_ge(s_x[k], 16 * i + 16)
                pe.wait_ge(s_xt, t)
                for c in range(C):
                    last = pe.transpose(ps_x[:, c, :], xin[k][:, c * P:(c + 1) * P], K.ident[:])
                last.then_inc(s_turnx, 1)

            def first(ps, w, half, k, e):
                for c in range(C):
                    last = pe.matmul(ps[half][:], xt[k][:, c, :],
                                     w[:, bass.ds(e, 1), c, half * HALF:(half + 1) * HALF].rearrange("p a f -> p (a f)"),
                                     start=(c == 0), stop=(c == C - 1))
                return last

            def turn_h(t):
                for j in range(2):
                    pe.wait_ge(s_h[j], t + 1)
                    if not (isinstance(t, int) and t < 1):
                        pe.wait_ge(s_ht[j], t)
                    for f in range(FC // 2):
                        last = pe.transpose(ps_h[j][:, f, :], h[:, j, f * P:(f + 1) * P], K.ident[:])
                last.then_inc(s_turnh, 1)

            def last_product(t, e):
                if not (isinstance(t, int) and t < 1):
                    pe.wait_ge(s_yc, t)
                for j in range(2):
                    pe.wait_ge(s_ht[j], t + 1)
                    for f in range(FC // 2):
                        g = j * (FC // 2) + f
                        last = pe.matmul(ps_y[:, 0:D], ht[:, j, f, :],
                                         w2_sb[:, bass.ds(e, 1), g, :].rearrange("p a n -> p (a n)"), start=(g == 0), stop=(g == FC - 1))
                last.then_inc(s_mmy, 1)

            def owner(t):
                return pe.value_load(K.owner[0:1, bass.ds(t, 1)], min_val=0, max_val=EXPERTS - 1)

            def body(i, k, start=False, end=False):
                t = 2 * i + k
                e = owner(t)
                pe.wait_ge(s_w, 48 * e + 48)
                pe.wait_ge(s_xt, t + 1)
                pe.wait_ge(s_silu[0], t)
                first(ps_a, w1_sb, 0, k, e).then_inc(s_a[0], 1)
                pe.wait_ge(s_h[0], t)
                first(ps_b, w3_sb, 0, k, e).then_inc(s_b[0], 1)
                if not start:
                    turn_h(t - 1)
                pe.wait_ge(s_silu[1], t)
                first(ps_a, w1_sb, 1, k, e).then_inc(s_a[1], 1)
                if not start:
                    last_product(t - 1, owner(t - 1))
                if not end:
                    turn_x(i + k, t + 1, 1 - k)
                pe.wait_ge(s_h[1], t)
                first(ps_b, w3_sb, 1, k, e).then_inc(s_b[1], 1)

            turn_x(0, 0, 0)
            body(0, 0, start=True)
            body(0, 1)
            with pe.Fori(1, SLOTS // 2 - 1) as i:
                for k in range(2):
                    body(i, k)
            body(SLOTS // 2 - 1, 0)
            body(SLOTS // 2 - 1, 1, end=True)
            turn_h(SLOTS - 1)
            last_product(SLOTS - 1, owner(SLOTS - 1))

        @block.scalar
        def _(act):
            act.wait_ge(s_dest, 16)

            def copy_h(t):
                act.wait_ge(s_turnh, t + 1)
                if not (isinstance(t, int) and t < 1):
                    act.wait_ge(s_mmy, t)
                act.activation(ht[:, 0], ps_h[0][:], ACT.Copy).then_inc(s_ht[0], 1)

            def copy_y(k, t):
                act.wait_ge(s_mmy, t + 1)
                if not (isinstance(t, int) and t < 2):
                    act.wait_ge(s_out, 16 * (t - 1))
                act.nop(nofuse=True)
                act.activation(dest[k][:], dest_all[:, bass.ds(t, 1)], ACT.Copy)
                act.activation(y[k][:], ps_y[:, 0:D], ACT.Copy).then_inc(s_yc, 1)

            def body(i, k, start=False):
                t = 2 * i + k
                if not start:
                    copy_h(t - 1)
                act.wait_ge(s_a[0], t + 1)
                act.wait_ge(s_turnh, t)
                act.activation(h[:, 0], ps_a[0][:], ACT.Silu).then_inc(s_silu[0], 1)
                act.wait_ge(s_a[1], t + 1)
                act.activation(h[:, 1], ps_a[1][:], ACT.Silu).then_inc(s_silu[1], 1)
                if not start:
                    copy_y(1 - k, t - 1)

            body(0, 0, start=True)
            body(0, 1)
            with act.Fori(1, SLOTS // 2) as i:
                for k in range(2):
                    body(i, k)
            copy_h(SLOTS - 1)
            copy_y(1, SLOTS - 1)

        @block.vector
        def _(dve):
            def copy_x(t, k):
                dve.wait_ge(s_turnx, t + 1)
                if not (isinstance(t, int) and t < 2):
                    dve.wait_ge(s_b[1], t - 1)
                dve.tensor_copy(xt[k][:], ps_x[:, 0:C, :]).then_inc(s_xt, 1)

            def copy_h(t):
                dve.wait_ge(s_turnh, t + 1)
                if not (isinstance(t, int) and t < 1):
                    dve.wait_ge(s_mmy, t)
                dve.tensor_copy(ht[:, 1], ps_h[1][:]).then_inc(s_ht[1], 1)

            def body(i, k, start=False, end=False):
                t = 2 * i + k
                if not start:
                    copy_h(t - 1)
                for j in range(2):
                    if j == 1 and not end:
                        copy_x(t + 1, 1 - k)
                    dve.wait_ge(s_silu[j], t + 1)
                    dve.wait_ge(s_b[j], t + 1)
                    dve.tensor_tensor(h[:, j], h[:, j], ps_b[j][:], ALU.mult).then_inc(s_h[j], 1)

            copy_x(0, 0)
            body(0, 0, start=True)
            body(0, 1)
            with dve.Fori(1, SLOTS // 2 - 1) as i:
                for k in range(2):
                    body(i, k)
            body(SLOTS // 2 - 1, 0)
            body(SLOTS // 2 - 1, 1, end=True)
            copy_h(SLOTS - 1)


def combine(nc, K, h_dram, y_dram, out):
    G = 4
    N = TILES // G
    with ExitStack() as ctx:
        ph = Phase(nc, ctx, "comb")
        hh = ph.sb("h", [P, TILES, D])
        yy = [ph.sb(f"y{j}", [P, TILES, D]) for j in range(2)]
        s_in, s_one, s_two, s_out = (ph.sem(n) for n in ("in", "one", "two", "out"))
        block = ctx.enter_context(nc.Block())
        s_step = [ph.sem(f"step{g}") for g in range(N)]

        def rows(dram, g, first=0):
            return dram[first + g * G * P:first + (g + 1) * G * P, :].rearrange("(t p) d -> p t d", p=P)

        @block.sync
        def _(sp):
            for g in range(N):
                cut = slice(g * G, (g + 1) * G)
                sp.dma_start(hh[:, cut, :], rows(h_dram, g)).then_inc(s_step[g], 16)
                for j in range(2):
                    sp.dma_start(yy[j][:, cut, :], rows(y_dram, g, j * TOKENS)).then_inc(s_step[g], 16)

        @block.scalar
        def _(act):
            flat = out.rearrange("b s d -> (b s) d")
            for g in range(N):
                act.wait_ge(s_two, g + 1)
                act.dma_start(rows(flat, g), hh[:, g * G:(g + 1) * G, :]).then_inc(s_out, 16)
            act.wait_ge(s_out, 16 * N)

        @block.vector
        def _(dve):
            for g in range(N):
                dve.wait_ge(s_step[g], 48)
                for j, s in ((0, s_one), (1, s_two)):
                    for t in range(g * G, (g + 1) * G):
                        last = dve.scalar_tensor_tensor(hh[:, t, :], yy[j][:, t, :], K.share[j][:, t:t + 1], hh[:, t, :],
                                                        ALU.mult, ALU.add)
                    last.then_inc(s, 1)
                    if j == 0:
                        dve.wait_ge(s_one, g + 1)


def program(nc, I, out):
    Phase.used = []
    with ExitStack() as ctx:
        class K:
            pass
        ph = Phase(nc, ctx, "k")
        K.ident = ph.sb("ident", [P, P])
        K.share = [ph.sb(f"share{j}", [P, TILES]) for j in range(2)]
        K.owner = ph.sb("owner", [1, SLOTS], I32)

        def dram(name, shape, dt=F32):
            return nc.dram_tensor(name, shape, dt, kind="Internal")

        h_dram = dram("h", [TOKENS, D])
        xs_dram = dram("x_sorted", [SLOTS * P, XW])
        y_dram = dram("y", [2 * TOKENS + P, D])
        with ExitStack() as stream:
            ph = Phase(nc, stream, "k")
            K.H = ph.sb("H", [P, TILES, D])
            K.pad = ph.sb("pad", [P, XW])
            K.stats = ph.sb("stats", [P, TILES, 6])
            K.mean = ph.sb("mean", [P, TILES])
            K.var = ph.sb("var", [P, TILES])
            K.rstd = ph.sb("rstd", [P, TILES])
            K.minus_half = ph.sb("mhalf", [P, TILES])
            rlen = dram("rlen", [B, S])
            q_dram = dram("q_parts", [B, len(SPLITS), D, S], BF16)
            k_dram = dram("k_parts", [B, len(SPLITS), D, S], BF16)
            v_dram = dram("v_parts", [PAIRS, B, P, T * 2 * VW], BF16)
            heads_dram = dram("heads", [PAIRS * B, P, T * 2 * DH])
            constants(nc, K)
            embed(nc, K, I["x"], I["mask"], I["embT"], I["pcaT"], I["proj_w"], I["proj_b"], I["fus_w"], I["fus_b"],
                  I["ln_g"], I["ln_b"], rlen)
            project_qkv(nc, K, I["wqT"], I["bq"], I["wkT"], I["bk"], I["wvT"], I["bv"], q_dram, k_dram, v_dram)
            attention(nc, K, I["pos_bias"], q_dram, k_dram, v_dram, heads_dram)
            attention_output(nc, K, heads_dram, I["woT"], I["bo"])
            inner_ffn(nc, K, *(I[n] for n in ("f_win", "f_bin", "f_w1", "f_b1", "f_w2", "f_b2", "f_wout", "f_bout")), xs_dram)
            recurrence(nc, K, *(I[n] for n in ("a_param", "ig_w", "ig_b", "ag_w", "ag_b")))
            recycle(nc)
            route(nc, K, I["gate_w"], I["gate_b"], h_dram, xs_dram)
        experts(nc, K, I["w1"], I["w3"], I["w2"], xs_dram, y_dram)
        combine(nc, K, h_dram, y_dram, out)


def kernel(**inputs):
    import numpy as np
    import concourse.bacc as bacc
    from concourse.bass_utils import run_bass_kernel_spmd

    a = {k: np.asarray(v) for k, v in inputs.items()}
    arrays = {
        "x": a["x"], "mask": a["mask_BS_i1_0"],
        "embT": a["L0_tok_emb"].T, "pcaT": a["L0_tok_pca_lookup"].T,
        "wqT": a["L0_attn_Wq"].T, "bq": a["L0_attn_bq"], "wkT": a["L0_attn_Wk"].T, "bk": a["L0_attn_bk"],
        "wvT": a["L0_attn_Wv"].T, "bv": a["L0_attn_bv"],
        "pos_bias": a["L0_attn_pos_bias"],
        "woT": a["L0_attn_Wo"].T, "bo": a["L0_attn_bo"],
        "f_win": a["L0_ffn_Win"], "f_bin": a["L0_ffn_bin_"], "f_w1": a["L0_ffn_W1"], "f_b1": a["L0_ffn_b1"],
        "f_w2": a["L0_ffn_W2"], "f_b2": a["L0_ffn_b2"], "f_wout": a["L0_ffn_Wout"], "f_bout": a["L0_ffn_bout"],
        "a_param": a["L1_attn_a_param"], "ig_w": a["L1_attn_ig_w"], "ig_b": a["L1_attn_ig_b"],
        "ag_w": a["L1_attn_ag_w"], "ag_b": a["L1_attn_ag_b"],
        "gate_w": a["L1_ffn_gate_w"], "gate_b": a["L1_ffn_gate_b"], "w1": a["L1_ffn_w1"], "w3": a["L1_ffn_w3"], "w2": a["L1_ffn_w2"],
        "proj_w": a["L0_tok_proj_w"], "proj_b": a["L0_tok_proj_b"],
        "fus_w": a["L0_tok_fus_w"], "fus_b": a["L0_tok_fus_b"], "ln_g": a["L0_tok_ln_g"], "ln_b": a["L0_tok_ln_b"],
    }
    arrays = {k: np.ascontiguousarray(v) for k, v in arrays.items()}
    nc = bacc.Bacc("TRN2", target_bir_lowering=False, num_devices=1)
    args = {k: nc.dram_tensor(f"in_{k}", v.shape, mybir.dt.from_np(v.dtype), kind="ExternalInput").ap() for k, v in arrays.items()}
    out = nc.dram_tensor("out", (B, S, D), F32, kind="ExternalOutput").ap()
    program(nc, args, out)
    r = run_bass_kernel_spmd(nc, [{f"in_{k}": v for k, v in arrays.items()}], core_ids=[0])
    return r.results[0]["out"]
```

```python
from contextlib import ExitStack

import concourse.bass as bass
from concourse import mybir

F32 = mybir.dt.float32
BF16 = mybir.dt.bfloat16
F16 = mybir.dt.float16
I32 = mybir.dt.int32
U32 = mybir.dt.uint32
ALU = mybir.AluOpType
ACT = mybir.ActivationFunctionType
AX = mybir.AxisListType

P = 128
B, S, D = 8, 512, 256
C = D // P
T = S // P
TILES = B * T
V = 28
HEADS, DH = 16, 16
PAIRS = HEADS // 2
MAXLEN = 512
SCALE = float(DH) ** -0.5
BIASW = S + MAXLEN - P
SPLITS = ((0, 0), (0, 1), (1, 0), (1, 1), (0, 2), (2, 0))
STACK = DH * len(SPLITS)
VW = 3 * DH + 1
LIFT = 10.0
M, INNER = 64, 16
FFN, EXPERTS = 1024, 8
SLOTS = 2 * TILES + EXPERTS
EPS = 1e-5
TOKENS = B * S
SLABS, SLAB = 3 * EXPERTS, C * FFN
XW = D + 1


class Phase:

    used = []

    def __init__(self, nc, ctx, name):
        self.nc, self.ctx, self.name = nc, ctx, name

    def sb(self, name, shape, dt=F32):
        return self.ctx.enter_context(self.nc.sbuf_tensor(f"{self.name}_{name}", shape, dt))

    def ps(self, name, shape, dt=F32):
        return self.ctx.enter_context(self.nc.psum_tensor(f"{self.name}_{name}", shape, dt))

    def sem(self, name):
        Phase.used.append(self.nc.alloc_semaphore(f"{self.name}_{name}"))
        return Phase.used[-1]


def recycle(nc):
    nc.clear_and_free_semaphores(Phase.used)
    Phase.used = []
    with nc.Block() as block:
        @block.gpsimd
        def _(pool):
            pool.nop(nofuse=True)


def row_to_all(dram_row, n=P):
    return dram_row.rearrange("(a w) -> a w", a=1).partition_broadcast(n)


def columns(dram_vec):
    return dram_vec.rearrange("(c p) -> p c", p=P)


def constants(nc, K):
    with ExitStack() as ctx:
        ph = Phase(nc, ctx, "const")
        s_id = ph.sem("id")
        row = ph.sb("row", [P, 1], I32)
        block = ctx.enter_context(nc.Block())

        @block.gpsimd
        def _(pool):
            pool.memset(K.ident[:], 1.0).then_inc(s_id, 1)
            pool.wait_ge(s_id, 1)
            pool.affine_select(out=K.ident[:], in_=K.ident[:], compare_op=ALU.is_equal, fill=0.0, base=0,
                               pattern=[[-1, P]], channel_multiplier=1).then_inc(s_id, 1)
            pool.memset(K.minus_half[:], -0.5).then_inc(s_id, 1)
            pool.iota(row[:], [[0, 1]], base=2 * TOKENS, channel_multiplier=1).then_inc(s_id, 1)
            pool.memset(K.pad[:], 0.0).then_inc(s_id, 1)
            pool.wait_ge(s_id, 5)

        @block.vector
        def _(dve):
            dve.wait_ge(s_id, 5)
            dve.tensor_copy(K.pad[:, D:XW], row[:]).then_inc(s_id, 1)
            dve.wait_ge(s_id, 6)


def rstd_from_stats(dve, pool, K, st, sems, done=0):
    s_var, s_rstd, s_chain = sems
    ev, od = K.stats[:, :, 0:3], K.stats[:, :, 3:6]
    if dve is not None:
        n = done

        def step(ins):
            nonlocal n
            n += 1
            ins.then_inc(s_chain, 1)
            dve.wait_ge(s_chain, n)

        step(dve.tensor_tensor(K.mean[:], ev[:, :, 1], od[:, :, 1], ALU.add))
        step(dve.tensor_scalar(K.mean[:], K.mean[:], 0.5, None, ALU.mult))
        step(dve.tensor_tensor(K.var[:], ev[:, :, 1], od[:, :, 1], ALU.subtract))
        step(dve.scalar_tensor_tensor(K.var[:], K.var[:], 0.25, K.var[:], ALU.mult, ALU.mult))
        step(dve.scalar_tensor_tensor(K.var[:], ev[:, :, 2], 1.0 / D, K.var[:], ALU.mult, ALU.add))
        step(dve.scalar_tensor_tensor(K.var[:], od[:, :, 2], 1.0 / D, K.var[:], ALU.mult, ALU.add))
        dve.tensor_scalar(K.var[:], K.var[:], EPS, None, ALU.add).then_inc(s_var, 1)
    if pool is not None:
        pool.wait_ge(s_var, 1)
        pool.tensor_tensor(K.rstd[:], K.var[:], K.minus_half[:], ALU.pow).then_inc(s_rstd, 1)


def embed(nc, K, x, mask, embT, pcaT, proj_w, proj_b, fus_w, fus_b, ln_g, ln_b, rlen_dram):
    HB = B // 2
    with ExitStack() as ctx:
        ph = Phase(nc, ctx, "emb")
        ids = ph.sb("ids", [P, HB, S], I32)
        mk = ph.sb("mk", [P, HB, S], I32)
        m8 = ph.sb("m8", [B, S], I32)
        mf = ph.sb("mf", [B, S + 2])
        rl8 = ph.sb("rl8", [B, S])
        rl = ph.sb("rl", [P, HB, S])
        vocab = ph.sb("vocab", [P, 1], I32)
        vocabf = ph.sb("vocabf", [P, 1])
        onerow = ph.sb("onerow", [P, 1])
        hot = ph.sb("hot", [P, HB, S])
        win = ph.sb("win", [P, HB, S + 2])
        embT_sb = ph.sb("embT", [P, C, V])
        pcaT_sb = ph.sb("pcaT", [20, V])
        proj_sb = ph.sb("proj", [20, D])
        projb_sb = ph.sb("projb", [P, C])
        fus_sb = ph.sb("fus", [P, 2 * C, D])
        fusb_sb = ph.sb("fusb", [1, D])
        fold = ph.sb("fold", [P, 2 * C, P])
        foldb = ph.sb("foldb", [1, P])
        table = ph.sb("table", [P, D])
        g_sb = ph.sb("g", [P, D])
        b_sb = ph.sb("b", [P, D])
        ps_c = ph.ps("c", [P, C, V])
        ps_t = ph.ps("t", [P, D])
        ps_f = [ph.ps(f"f{i}", [P, 2, D]) for i in range(4)]
        s_io, s_w, s_m8, s_voc, s_rl, s_rlb = (ph.sem(n) for n in ("io", "w", "m8", "voc", "rl", "rlb"))
        s_zero, s_fold, s_c, s_tab, s_tabsb, s_cols = (ph.sem(n) for n in ("zero", "fold", "c", "tab", "tabsb", "cols"))
        s_mm, s_keep, s_st, s_ch, s_var, s_rstd, s_ln = (ph.sem(n) for n in ("mm", "keep", "st", "ch", "var", "rstd", "ln"))
        block = ctx.enter_context(nc.Block())

        @block.sync
        def _(sp):
            sp.dma_start(m8[:], mask).then_inc(s_m8, 16)
            for h in range(2):
                sp.dma_start(ids[64 * h:64 * h + 64].rearrange("p b s -> p (b s)"),
                             row_to_all(x[HB * h:HB * h + HB].rearrange("b s -> (b s)"), 64)).then_inc(s_io, 16)
                sp.dma_start(mk[64 * h:64 * h + 64].rearrange("p b s -> p (b s)"),
                             row_to_all(mask[HB * h:HB * h + HB].rearrange("b s -> (b s)"), 64)).then_inc(s_io, 16)
            sp.wait_ge(s_rl, 1)
            sp.dma_start(rlen_dram[:], rl8[:]).then_inc(s_rlb, 16)
            sp.wait_ge(s_rlb, 16)
            for h in range(2):
                sp.dma_start(rl[64 * h:64 * h + 64].rearrange("p b s -> p (b s)"),
                             row_to_all(rlen_dram[HB * h:HB * h + HB].rearrange("b s -> (b s)"), 64)).then_inc(s_rlb, 16)

        @block.scalar
        def _(act):
            act.dma_start(fus_sb[:], fus_w.rearrange("(c p) n -> p c n", p=P)).then_inc(s_w, 16)
            act.dma_start(embT_sb[:], embT.rearrange("(c p) v -> p c v", p=P)).then_inc(s_w, 16)
            act.dma_start(pcaT_sb[:], pcaT).then_inc(s_w, 16)
            act.dma_start(proj_sb[:], proj_w).then_inc(s_w, 16)
            act.dma_start(projb_sb[:], columns(proj_b), allow_slow_non_contiguous=True).then_inc(s_w, 16)
            act.dma_start(fusb_sb[:], fus_b.rearrange("(a n) -> a n", a=1)).then_inc(s_w, 16)
            act.dma_start(g_sb[:], row_to_all(ln_g)).then_inc(s_w, 16)
            act.dma_start(b_sb[:], row_to_all(ln_b)).then_inc(s_w, 16)
            for i in range(TILES // 2):
                act.wait_ge(s_mm, i + 1)
                act.activation(K.H[:, 2 * i:2 * i + 2, :], ps_f[i % 4][:], ACT.Copy).then_inc(s_keep, 1)

        @block.gpsimd
        def _(pool):
            pool.iota(vocab[:], [[0, 1]], base=0, channel_multiplier=1).then_inc(s_voc, 1)
            pool.memset(fold[:], 0.0).then_inc(s_zero, 1)
            pool.memset(foldb[:], 0.0).then_inc(s_zero, 1)
            pool.memset(win[:], 0.0).then_inc(s_zero, 1)
            rstd_from_stats(None, pool, K, None, (s_var, s_rstd, s_ch))

        @block.tensor
        def _(pe):
            pe.wait_ge(s_w, 128)
            for c in range(C):
                pe.matmul(ps_c[:, c, :], proj_sb[:, c * P:(c + 1) * P], pcaT_sb[:], start=True, stop=True).then_inc(s_c, 1)
            pe.wait_ge(s_fold, 1)
            for c in range(2 * C):
                pe.matmul(ps_t[:], fold[:, c, :], fus_sb[:, c, :], start=(c == 0), stop=False)
            pe.matmul(ps_t[:], foldb[:], fusb_sb[:], start=False, stop=True).then_inc(s_tab, 1)
            pe.wait_ge(s_tabsb, 1)
            pe.wait_ge(s_cols, 1)
            for i in range(TILES // 2):
                if i >= 4:
                    pe.wait_ge(s_keep, i - 3)
                for j in range(2):
                    t = 2 * i + j
                    h, b, q = t // (TILES // 2), t // T % HB, t % T
                    last = pe.matmul(ps_f[i % 4][:, j, :], hot[64 * h:64 * h + 64, b, q * P:(q + 1) * P],
                                     table[64 * h:64 * h + 64, :], start=True, stop=True)
                last.then_inc(s_mm, 1)

        @block.vector
        def _(dve):
            n = 0

            def step(ins):
                nonlocal n
                n += 1
                ins.then_inc(s_ch, 1)
                dve.wait_ge(s_ch, n)

            step(dve.memset(mf[:], 0.0))
            dve.wait_ge(s_m8, 16)
            step(dve.tensor_copy(mf[:, 1:S + 1], m8[:]))
            step(dve.tensor_tensor(rl8[:], mf[:, 0:S], mf[:, 1:S + 1], ALU.add))
            step(dve.tensor_tensor(rl8[:], rl8[:], mf[:, 2:S + 2], ALU.add))
            step(dve.tensor_scalar(rl8[:], rl8[:], 1.0, None, ALU.max))
            n += 1
            dve.reciprocal(rl8[:], rl8[:]).then_inc(s_ch, 1)
            dve.wait_ge(s_ch, n)
            dve.sem_inc(s_rl, 1)
            dve.wait_ge(s_voc, 1)
            step(dve.tensor_single_scalar(vocab[:], vocab[:], 31, ALU.bitwise_and))
            step(dve.tensor_copy(vocabf[:], vocab[:]))
            step(dve.tensor_scalar(onerow[:], vocabf[:], float(V), None, ALU.is_equal))
            dve.wait_ge(s_zero, 3)
            dve.wait_ge(s_w, 128)
            dve.wait_ge(s_c, C)
            for h in range(2):
                step(dve.tensor_copy(fold[:, 0:C, 64 * h:64 * h + V], embT_sb[:]))
                step(dve.tensor_copy(fold[:, C:2 * C, 64 * h + 32:64 * h + 32 + V], ps_c[:]))
                step(dve.tensor_copy(fold[:, C:2 * C, 64 * h + V:64 * h + V + 1], projb_sb[:].rearrange("p (c a) -> p c a", a=1)))
                step(dve.memset(foldb[:, 64 * h + V:64 * h + V + 1], 1.0))
            dve.sem_inc(s_fold, 1)
            dve.wait_ge(s_io, 64)
            for h in range(2):
                p = slice(64 * h, 64 * h + 32)
                step(dve.tensor_scalar(hot[p], ids[p], vocabf[p], onerow[p], ALU.is_equal, ALU.max))
            step(dve.scalar_tensor_tensor(win[:, :, 1:S + 1], ids[:], vocabf[:], mk[:], ALU.is_equal, ALU.mult))
            for h in range(2):
                p = slice(64 * h + 32, 64 * h + 64)
                step(dve.tensor_tensor(hot[p], win[p, :, 0:S], win[p, :, 1:S + 1], ALU.add))
                step(dve.tensor_tensor(hot[p], hot[p], win[p, :, 2:S + 2], ALU.add))
            dve.wait_ge(s_rlb, 48)
            for h in range(2):
                p = slice(64 * h + 32, 64 * h + 64)
                step(dve.tensor_tensor(hot[p], hot[p], rl[p], ALU.mult))
            dve.sem_inc(s_cols, 1)
            dve.wait_ge(s_tab, 1)
            dve.tensor_copy(table[:], ps_t[:]).then_inc(s_tabsb, 1)
            for i in range(TILES // 2):
                dve.wait_ge(s_keep, i + 1)
                for j in range(2):
                    last = dve.bn_stats(K.stats[:, 2 * i + j, :], K.H[:, 2 * i + j, :])
                last.then_inc(s_st, 1)
            dve.wait_ge(s_st, TILES // 2)
            rstd_from_stats(dve, None, K, None, (s_var, s_rstd, s_ln))
            dve.wait_ge(s_rstd, 1)
            dve.wait_ge(s_keep, TILES // 2)
            base = 6
            for t in range(TILES):
                dve.scalar_tensor_tensor(K.H[:, t, :], K.H[:, t, :], K.mean[:, t:t + 1], g_sb[:], ALU.subtract, ALU.mult)\
                   .then_inc(s_ln, 1)
                if t >= 1:
                    dve.wait_ge(s_ln, base + 2 * t - 1)
                    dve.scalar_tensor_tensor(K.H[:, t - 1, :], K.H[:, t - 1, :], K.rstd[:, t - 1:t], b_sb[:], ALU.mult, ALU.add)\
                       .then_inc(s_ln, 1)
            dve.wait_ge(s_ln, base + 2 * TILES - 1)
            dve.scalar_tensor_tensor(K.H[:, TILES - 1, :], K.H[:, TILES - 1, :], K.rstd[:, TILES - 1:TILES], b_sb[:], ALU.mult, ALU.add)\
               .then_inc(s_ln, 1)
            for t in range(TILES):
                if t % 8 == 0:
                    dve.wait_ge(s_ln, min(base + 2 * (t + 8) + 1, base + 2 * TILES))
                last = dve.bn_stats(K.stats[:, t, :], K.H[:, t, :])
            last.then_inc(s_st, 1)
            dve.wait_ge(s_st, TILES // 2 + 1)


def slots(eng, body):
    for k in range(2):
        body(0, k, True)
    with eng.Fori(1, B // 2 - 1) as i:
        for k in range(2):
            body(i, k, True)
    body(B // 2 - 1, 0, True)
    body(B // 2 - 1, 1, False)


def apply_norm(dve, K, xn, b):
    for q in range(T):
        t = b * T + q
        last = dve.tensor_scalar(xn[:, q, :], K.H[:, bass.ds(t, 1), :].rearrange("p a d -> p (a d)"),
                                 K.mean[:, bass.ds(t, 1)], K.rstd[:, bass.ds(t, 1)], ALU.subtract, ALU.mult)
    return last


def transpose_row(pe, K, xp, xn):
    for q in range(T):
        for c in range(C):
            last = pe.transpose(xp[:, c, q * P:(q + 1) * P], xn[:, q, c * P:(c + 1) * P], K.ident[:])
    return last


def project_qkv(nc, K, wqT, bq, wkT, bk, wvT, bv, q_dram, k_dram, v_dram):
    with ExitStack() as ctx:
        ph = Phase(nc, ctx, "qkv")
        w_sb = {n: ph.sb(f"w{n}", [P, C, D]) for n in "qkv"}
        bq_sb, bk_sb, bqs = ph.sb("bq", [P, C]), ph.sb("bk", [P, C]), ph.sb("bqs", [P, C])
        bv_sb = ph.sb("bv", [P, D])
        xn = [ph.sb(f"xn{k}", [P, T, D]) for k in range(2)]
        xt = [ph.sb(f"xt{k}", [P, C, S]) for k in range(2)]
        full = {n: [ph.sb(f"full{n}{k}", [P, C * S]) for k in range(2)] for n in "qkv"}
        rest = {n: [ph.sb(f"rest{n}{k}", [P, C * S]) for k in range(2)] for n in "qkv"}
        part = {n: [ph.sb(f"part{n}{k}", [P, 3, C, S], BF16) for k in range(2)] for n in "qk"}
        vpart = [ph.sb(f"partv{k}", [P, PAIRS, T, 2 * VW], BF16) for k in range(2)]
        xp = ph.ps("xp", [P, C, S])
        ps = {n: ph.ps(f"ps{n}", [P, C * S]) for n in "qkv"}
        s_w, s_ones, s_bq, s_xn, s_T, s_xt = (ph.sem(n) for n in ("w", "ones", "bq", "xn", "T", "xt"))
        s_ch, s_var, s_rstd = (ph.sem(n) for n in ("ch", "var", "rstd"))
        s_mm, s_full, s_hi, s_rest, s_mid, s_lo = ({n: ph.sem(f"{m}{n}") for n in "qkv"}
                                                  for m in ("mm", "full", "hi", "rest", "mid", "lo"))
        s_out = [ph.sem(f"out{k}") for k in range(2)]
        NOUT = 16 * (2 * len(SPLITS) + 1)
        block = ctx.enter_context(nc.Block())

        def vcols(tile, q, part):
            return tile[:, :, q, :].rearrange("p h (e w) -> p h e w", e=2)[:, :, :, part * DH:(part + 1) * DH]

        def vfull(tile, q):
            return tile[:, q * D:(q + 1) * D].rearrange("p (h e d) -> p h e d", e=2, d=DH)

        @block.sync
        def _(sp):
            for n, w in zip("qkv", (wqT, wkT, wvT)):
                sp.dma_start(w_sb[n][:], w.rearrange("(c p) n -> p c n", p=P)).then_inc(s_w, 16)
            sp.dma_start(bq_sb[:], columns(bq), allow_slow_non_contiguous=True).then_inc(s_w, 16)
            sp.dma_start(bk_sb[:], columns(bk), allow_slow_non_contiguous=True).then_inc(s_w, 16)
            sp.dma_start(bv_sb[:], row_to_all(bv)).then_inc(s_w, 16)

            def body(i, k, more):
                b = 2 * i + k
                for side, (n, dram) in enumerate((("q", q_dram), ("k", k_dram))):
                    sp.wait_ge(s_lo[n], b + 1)
                    for blk, parts in enumerate(SPLITS):
                        sp.dma_start(dram[bass.ds(b, 1), blk].rearrange("a (c p) s -> p (a c) s", p=P),
                                     part[n][k][:, parts[side], :, :]).then_inc(s_out[k], 16)
                sp.wait_ge(s_lo["v"], b + 1)
                sp.dma_start(v_dram[:, bass.ds(b, 1)].rearrange("h a p w -> p (a h) w"),
                             vpart[k][:].rearrange("p h q w -> p h (q w)")).then_inc(s_out[k], 16)

            slots(sp, body)
            for k in range(2):
                sp.wait_ge(s_out[k], NOUT * (B // 2))

        @block.tensor
        def _(pe):
            def turn(b, k):
                pe.wait_ge(s_xn, b + 1)
                pe.wait_ge(s_xt, b)
                transpose_row(pe, K, xp, xn[k]).then_inc(s_T, 1)

            def body(i, k, more):
                b = 2 * i + k
                if more:
                    turn(b + 1, 1 - k)
                pe.wait_ge(s_xt, b + 1)
                for n in "qk":
                    pe.wait_ge(s_full[n], b)
                    for m in range(C):
                        for c in range(C):
                            last = pe.matmul(ps[n][:, m * S:(m + 1) * S], w_sb[n][:, c, m * P:(m + 1) * P], xt[k][:, c, :],
                                             start=(c == 0), stop=(c == C - 1))
                    last.then_inc(s_mm[n], 1)
                pe.wait_ge(s_full["v"], b)
                for q in range(T):
                    for c in range(C):
                        last = pe.matmul(ps["v"][:, q * D:(q + 1) * D], xt[k][:, c, q * P:(q + 1) * P], w_sb["v"][:, c, :],
                                         start=(c == 0), stop=(c == C - 1))
                last.then_inc(s_mm["v"], 1)

            turn(0, 0)
            pe.wait_ge(s_w, 96)
            slots(pe, body)

        @block.scalar
        def _(act):
            def middle(b, k):
                for n in "qk":
                    act.wait_ge(s_rest[n], b + 1)
                    act.activation(part[n][k][:, 1].rearrange("p c s -> p (c s)"), rest[n][k][:], ACT.Copy).then_inc(s_mid[n], 1)
                act.wait_ge(s_rest["v"], b + 1)
                for q in range(T):
                    last = act.activation(vcols(vpart[k], q, 1), vfull(rest["v"][k], q), ACT.Copy)
                last.then_inc(s_mid["v"], 1)

            def body(i, k, more):
                b = 2 * i + k
                if more:
                    act.wait_ge(s_T, b + 2)
                    act.wait_ge(s_mm["v"], b)
                    act.activation(xt[1 - k][:], xp[:], ACT.Copy).then_inc(s_xt, 1)
                act.wait_ge(s_out[k], NOUT * i)
                for n in "qk":
                    act.wait_ge(s_full[n], b + 1)
                    act.activation(part[n][k][:, 0].rearrange("p c s -> p (c s)"), full[n][k][:], ACT.Copy).then_inc(s_hi[n], 1)
                act.wait_ge(s_full["v"], b + 1)
                for q in range(T):
                    last = act.activation(vcols(vpart[k], q, 0), vfull(full["v"][k], q), ACT.Copy)
                last.then_inc(s_hi["v"], 1)
                if not (isinstance(b, int) and b == 0):
                    middle(b - 1, 1 - k)
                if not more:
                    middle(b, k)

            act.wait_ge(s_T, 1)
            act.activation(xt[0][:], xp[:], ACT.Copy).then_inc(s_xt, 1)
            act.wait_ge(s_ones, 2)
            slots(act, body)

        @block.gpsimd
        def _(pool):
            rstd_from_stats(None, pool, K, None, (s_var, s_rstd, s_ch))
            for k in range(2):
                pool.memset(vpart[k][:], 1.0).then_inc(s_ones, 1)

            def body(i, k, more):
                b = 2 * i + k
                for n in "qk":
                    pool.wait_ge(s_hi[n], b + 1)
                    if not (isinstance(b, int) and b < 2):
                        pool.wait_ge(s_lo[n], b - 1)
                    pool.tensor_tensor(rest[n][k][:], full[n][k][:], part[n][k][:, 0].rearrange("p c s -> p (c s)"), ALU.subtract)\
                        .then_inc(s_rest[n], 1)
                pool.wait_ge(s_hi["v"], b + 1)
                if not (isinstance(b, int) and b < 2):
                    pool.wait_ge(s_lo["v"], b - 1)
                for q in range(T):
                    last = pool.tensor_tensor(vfull(rest["v"][k], q), vfull(full["v"][k], q), vcols(vpart[k], q, 0), ALU.subtract)
                last.then_inc(s_rest["v"], 1)

            slots(pool, body)

        @block.vector
        def _(dve):
            rstd_from_stats(dve, None, K, None, (s_var, s_rstd, s_ch))
            dve.wait_ge(s_rstd, 1)
            dve.wait_ge(s_w, 96)
            dve.tensor_scalar(bqs[:], bq_sb[:], SCALE, None, ALU.mult).then_inc(s_bq, 1)
            for k in range(2):
                apply_norm(dve, K, xn[k], k).then_inc(s_xn, 1)
            dve.wait_ge(s_bq, 1)

            def last_part(b, k):
                for n in "qk":
                    dve.wait_ge(s_mid[n], b + 1)
                    dve.tensor_tensor(part[n][k][:, 2].rearrange("p c s -> p (c s)"), rest[n][k][:],
                                      part[n][k][:, 1].rearrange("p c s -> p (c s)"), ALU.subtract).then_inc(s_lo[n], 1)
                dve.wait_ge(s_mid["v"], b + 1)
                for q in range(T):
                    last = dve.tensor_tensor(vcols(vpart[k], q, 2), vfull(rest["v"][k], q), vcols(vpart[k], q, 1), ALU.subtract)
                last.then_inc(s_lo["v"], 1)

            def body(i, k, more):
                b = 2 * i + k
                for n in "qk":
                    dve.wait_ge(s_mm[n], b + 1)
                    if not (isinstance(b, int) and b < 2):
                        dve.wait_ge(s_rest[n], b - 1)
                    for m in range(C):
                        cols = slice(m * S, (m + 1) * S)
                        if n == "q":
                            last = dve.tensor_scalar(full[n][k][:, cols], ps[n][:, cols], SCALE, bqs[:, m:m + 1], ALU.mult, ALU.add)
                        else:
                            last = dve.tensor_scalar(full[n][k][:, cols], ps[n][:, cols], bk_sb[:, m:m + 1], None, ALU.add)
                    last.then_inc(s_full[n], 1)
                dve.wait_ge(s_mm["v"], b + 1)
                if not (isinstance(b, int) and b < 2):
                    dve.wait_ge(s_rest["v"], b - 1)
                dve.tensor_tensor(full["v"][k][:].rearrange("p (q d) -> p q d", d=D), ps["v"][:].rearrange("p (q d) -> p q d", d=D),
                                  bv_sb[:].rearrange("p (a d) -> p a d", a=1).to_broadcast([P, T, D]), ALU.add)\
                   .then_inc(s_full["v"], 1)
                if more and not (isinstance(b, int) and b == B - 2):
                    apply_norm(dve, K, xn[k], b + 2).then_inc(s_xn, 1)
                if not (isinstance(b, int) and b == 0):
                    last_part(b - 1, 1 - k)
                if not more:
                    last_part(b, k)

            slots(dve, body)


def attention(nc, K, pos_bias, q_dram, k_dram, v_dram, heads_dram, experts_f32, experts_parts):
    BODY = 8
    PER_HP = B * 4 // BODY
    UNITS = PAIRS * B * 4
    WHOLE = (1, 3, 5, 7)
    SPLIT = BODY - len(WHOLE)
    EXP_LAG, T_LAG, HI_LAG, LO_LAG, PV_LAG, NORM_LAG = 1, 2, 2, 3, 4, 5
    with ExitStack() as ctx:
        ph = Phase(nc, ctx, "att")
        qs = [ph.sb(f"qs{k}", [STACK, 2, S], BF16) for k in range(2)]
        ks = [ph.sb(f"ks{k}", [STACK, 2, S], BF16) for k in range(2)]
        vs = [ph.sb(f"vs{k}", [P, T, 2 * VW], BF16) for k in range(2)]
        bias = [ph.sb(f"bias{k}", [P, 2, BIASW]) for k in range(2)]
        score = [ph.sb(f"score{k}", [P, 2, S]) for k in range(4)]
        top = [ph.sb(f"top{k}", [P, 2]) for k in range(4)]
        shift = [ph.sb(f"shift{k}", [P, 2]) for k in range(4)]
        prob = [ph.sb(f"prob{k}", [P, 2, S]) for k in range(2)]
        hi = [ph.sb(f"hi{k}", [P, 2, T, P], F16) for k in range(2)]
        lo = [ph.sb(f"lo{k}", [P, 2, T, P], F16) for k in range(2)]
        whole = ph.sb("whole", [P, 2, T, P])
        vsum = ph.sb("vsum", [P, T * 2, DH])
        vf = [ph.sb(f"vf{k}", [P, T, 2 * VW]) for k in range(2)]
        osum = [ph.sb(f"osum{k}", [P, 2, T, DH]) for k in range(2)]
        rec = [ph.sb(f"rec{k}", [P, 2, T]) for k in range(2)]
        heads = [ph.sb(f"heads{k}", [P, T, 2, DH]) for k in range(2)]
        ps_s = [ph.ps(f"s{j}", [P, S]) for j in range(2)]
        ps_t = [ph.ps(f"t{k}", [P, 2, T, P]) for k in range(2)]
        ps_o = [ph.ps(f"o{k}", [P, 512]) for k in range(2)]
        s_qk, s_top, s_shift, s_exp, s_turn, s_hi, s_lo, s_pv, s_norm, s_part = (
            ph.sem(n) for n in ("qk", "top", "shift", "exp", "turn", "hi", "lo", "pv", "norm", "part"))
        s_vone, s_vsum, s_vf = (ph.sem(n) for n in ("vone", "vsum", "vf"))
        slab = ph.sb("slab", [P, SLAB])
        slab_parts = ph.sb("slabparts", [P, 2, SLAB], F16)
        s_slab, s_slabhi, s_slablo, s_slabout = (ph.sem(n) for n in ("slab", "slabhi", "slablo", "slabout"))
        s_ldqk = [ph.sem(f"ldqk{k}") for k in range(2)]
        s_ldv = [ph.sem(f"ldv{k}") for k in range(2)]
        s_bias = [ph.sem(f"bias{k}") for k in range(2)]
        s_store = [ph.sem(f"store{k}") for k in range(2)]
        block = ctx.enter_context(nc.Block())

        def wait(eng, sem, value):
            if not (isinstance(value, int) and value <= 0):
                eng.wait_ge(sem, value)

        def flat(eng, steps):
            for j in range(BODY):
                steps(0, j)
            with eng.Fori(1, UNITS // BODY) as m:
                for j in range(BODY):
                    steps(m, j)
            for j in range(BODY):
                steps(UNITS // BODY, j)

        def wait_parts(eng, m, j):
            m, j = m + j // BODY, j % BODY
            if isinstance(m, int) and m < 0:
                return
            if j in WHOLE:
                eng.wait_ge(s_hi, m * BODY + j + 1)
            else:
                eng.wait_ge(s_lo, m * SPLIT + sum(n not in WHOLE for n in range(j + 1)))

        def live(m, j, lag):
            return not (isinstance(m, int) and not 0 <= m * BODY + j - lag < UNITS)

        @block.sync
        def _(sp):
            def load_bias(hp, k):
                src = bass.AP(pos_bias.tensor, pos_bias.offset + hp * (2 * (2 * MAXLEN - 1)),
                              [[1, P], [2 * MAXLEN - 1, 2], [1, BIASW]])
                sp.dma_start(bias[k][:], src).then_inc(s_bias[k], 16)

            def load_pair(hp, b, n, k):
                wait(sp, s_qk, 8 * (n - 1))
                for dst, dram in ((qs, q_dram), (ks, k_dram)):
                    for e in range(2):
                        sp.dma_start(dst[k][:, e, :], dram[bass.ds(b, 1), :, bass.ds(hp * 2 * DH + e * DH, DH), :]
                                     .rearrange("a c d s -> (a c) d s")).then_inc(s_ldqk[k], 16)
                wait(sp, s_pv, 4 * (n - 1))
                wait(sp, s_vf, n - 1)
                sp.dma_start(vs[k][:].rearrange("p q w -> p (q w)"),
                             v_dram[bass.ds(hp, 1), bass.ds(b, 1)].rearrange("h a p w -> (h a p) w"))\
                    .then_inc(s_ldv[k], 16)

            def rows(hp, first):
                for k in range(2):
                    load_pair(hp, k, hp * B + k, k)
                with sp.Fori(1, B // 2) as i:
                    for k in range(2):
                        load_pair(hp, 2 * i + k, hp * B + 2 * i + k, k)

            load_bias(0, 0)
            load_bias(1, 1)
            rows(0, True)
            rows(1, False)
            with sp.Fori(1, PAIRS // 2) as i:
                for k in range(2):
                    hp = 2 * i + k
                    sp.wait_ge(s_top, (hp - 1) * (2 * 4 * B))
                    load_bias(hp, k)
                    with sp.Fori(0, B // 2) as r:
                        for kk in range(2):
                            load_pair(hp, 2 * r + kk, hp * B + 2 * r + kk, kk)

        @block.gpsimd
        def _(pool):
            def store(n, k):
                pool.wait_ge(s_norm, n + 1)
                pool.dma_start(heads_dram[bass.ds(n, 1)].rearrange("a p w -> (a p) w"),
                               heads[k][:].rearrange("p q e d -> p (q e d)")).then_inc(s_store[k], 16)

            def whole_v(i, k):
                n = 2 * i + k
                pool.wait_ge(s_ldv[k], 16 * i + 16)
                wait(pool, s_pv, 4 * (n - 1))
                wait(pool, s_vf, n)
                v = vs[k][:].rearrange("p q (e w) -> p (q e) w", w=VW)
                pool.tensor_tensor(vsum[:], v[:, :, 0:DH], v[:, :, DH:2 * DH], ALU.add).then_inc(s_vsum, 1)
                pool.wait_ge(s_vsum, n + 1)
                pool.tensor_tensor(vf[k][:].rearrange("p q (e w) -> p (q e) w", w=VW)[:, :, 0:DH], vsum[:], v[:, :, 2 * DH:3 * DH],
                                   ALU.add).then_inc(s_vf, 1)

            for k in range(2):
                pool.memset(vf[k][:], 0.0).then_inc(s_vone, 1)
            pool.wait_ge(s_vone, 2)
            for k in range(2):
                pool.memset(vf[k][:].rearrange("p q (e w) -> p (q e) w", w=VW)[:, :, 3 * DH:VW], 1.0).then_inc(s_vone, 1)
            pool.wait_ge(s_vone, 4)
            for k in range(2):
                whole_v(0, k)
            def load_slab(s):
                pool.dma_start(slab[:], experts_f32[bass.ds(s, 1)].rearrange("a p w -> (a p) w")).then_inc(s_slab, 16)

            def split_slab(s, k, more):
                if k == 0:
                    pool.wait_ge(s_slab, 16 * s + 16)
                    if not (isinstance(s, int) and s == 0):
                        pool.wait_ge(s_slabout, 16 * s)
                    pool.nop(nofuse=True)
                    pool.tensor_copy(slab_parts[:, 0, :], slab[:]).then_inc(s_slabhi, 1)
                else:
                    pool.wait_ge(s_slabhi, s + 1)
                    pool.tensor_tensor(slab_parts[:, 1, :], slab[:], slab_parts[:, 0, :], ALU.subtract).then_inc(s_slablo, 1)
                    pool.wait_ge(s_slablo, s + 1)
                    pool.dma_start(experts_parts[bass.ds(s, 1)].rearrange("a p w -> (a p) w"),
                                   slab_parts[:].rearrange("p c w -> p (c w)")).then_inc(s_slabout, 16)
                    if more:
                        load_slab(s + 1)

            def pairs(i, s=None, more=True):
                for k in range(2):
                    store(2 * i + k - 2, k)
                    whole_v(i, k)
                    if s is not None:
                        split_slab(s, k, more)

            load_slab(0)
            pairs(1, 0)
            with pool.Fori(2, SLABS) as i:
                pairs(i, i - 1)
            pairs(SLABS, SLABS - 1, more=False)
            with pool.Fori(SLABS + 1, PAIRS * B // 2) as i:
                pairs(i)
            pool.wait_ge(s_slabout, 16 * SLABS)
            for k in range(2):
                store(PAIRS * B - 2 + k, k)
            for k in range(2):
                pool.wait_ge(s_store[k], 16 * (PAIRS * B // 2))

        @block.tensor
        def _(pe):
            def steps(m, j):
                if live(m, j, 0):
                    e, half, k = j // 2 % 2, j % 2, j // 4
                    if j % 4 == 0:
                        pe.wait_ge(s_ldqk[k], 64 * m + 64)
                    for t in range(2):
                        tile = 2 * (m * BODY + j) + t
                        wait(pe, s_top, tile - 1)
                        q = 2 * half + t
                        pe.matmul(ps_s[t][:], qs[k][:, e, q * P:(q + 1) * P], ks[k][:, e, :], start=True, stop=True)\
                            .then_inc(s_qk, 1)
                if live(m, j, PV_LAG):
                    jj = (j - PV_LAG) % BODY
                    u = m * BODY + j - PV_LAG
                    e, half, k, sl = jj // 2 % 2, jj % 2, jj // 4, jj % 2
                    if jj % 4 == 0:
                        n = 2 * m + (j - PV_LAG) // 4
                        pe.wait_ge(s_ldv[k], 16 * (m + (j - PV_LAG) // BODY) + 16)
                        pe.wait_ge(s_vf, n + 1)
                        wait(pe, s_norm, n - 1)
                    wait_parts(pe, m, j - PV_LAG)
                    factors = ((whole, vf),) if jj in WHOLE else ((hi[sl], vs), (lo[sl], vs))
                    for t in range(2):
                        o = (e * T + 2 * half + t) * VW
                        for kt in range(T):
                            for f, (part, v) in enumerate(factors):
                                last = pe.matmul(ps_o[k][:, o:o + VW], part[:, t, kt, :], v[k][:, kt, e * VW:(e + 1) * VW],
                                                 start=(kt == 0 and f == 0), stop=(kt == T - 1 and f == len(factors) - 1))
                    last.then_inc(s_pv, 1)
                if live(m, j, T_LAG):
                    u = m * BODY + j - T_LAG
                    sl = (j - T_LAG) % 2
                    pe.wait_ge(s_exp, u + 1)
                    wait_parts(pe, m, j - T_LAG - 2)
                    for t in range(2):
                        for kt in range(T):
                            last = pe.transpose(ps_t[sl][:, t, kt, :], prob[sl][:, t, kt * P:(kt + 1) * P], K.ident[:])
                    last.then_inc(s_turn, 1)

            flat(pe, steps)

        @block.scalar
        def _(act):
            def steps(m, j):
                if live(m, j, EXP_LAG):
                    u, jj = m * BODY + j - EXP_LAG, (j - EXP_LAG) % BODY
                    act.wait_ge(s_shift, u + 1)
                    wait(act, s_turn, u - 1)
                    for t in range(2):
                        last = act.activation(prob[jj % 2][:, t, :], score[jj % 4][:, t, :], ACT.Exp, bias=shift[jj % 4][:, t:t + 1])
                    last.then_inc(s_exp, 1)
                if live(m, j, HI_LAG):
                    u, jj = m * BODY + j - HI_LAG, (j - HI_LAG) % BODY
                    act.wait_ge(s_turn, u + 1)
                    wait(act, s_pv, u - 1)
                    act.activation(whole[:] if jj in WHOLE else hi[jj % 2][:], ps_t[jj % 2][:], ACT.Copy).then_inc(s_hi, 1)

            flat(act, steps)

        @block.vector
        def _(dve):
            def steps(m, j, bk):
                if live(m, j, 0):
                    e, half, r = j // 2 % 2, j % 2, j % 4
                    u = m * BODY + j
                    wait(dve, s_exp, u - 3)
                    for t in range(2):
                        dve.wait_ge(s_qk, 2 * u + t + 1)
                        dve.nop(nofuse=True)
                        off = (2 * half + t) * P
                        dve.tensor_tensor_reduce(score[r][:, t, :], ps_s[t][:], bias[bk][:, e, off:off + S][:, ::-1], 1.0, -3.0e38,
                                                 ALU.add, ALU.max, top[r][:, t:t + 1]).then_inc(s_top, 1)
                    dve.wait_ge(s_top, 2 * u + 2)
                    dve.tensor_scalar(shift[r][:], top[r][:], -1.0, LIFT, ALU.mult, ALU.add).then_inc(s_shift, 1)
                if live(m, j, LO_LAG) and (j - LO_LAG) % BODY not in WHOLE:
                    u, sl = m * BODY + j - LO_LAG, (j - LO_LAG) % 2
                    dve.wait_ge(s_hi, u + 1)
                    wait(dve, s_pv, u - 1)
                    dve.tensor_tensor(lo[sl][:], ps_t[sl][:], hi[sl][:], ALU.subtract).then_inc(s_lo, 1)
                if (j - NORM_LAG) % 4 == 3 and live(m, j, NORM_LAG):
                    k = (j - NORM_LAG) % BODY // 4
                    n = 2 * m + (j - NORM_LAG) // 4
                    dve.wait_ge(s_pv, m * BODY + j - NORM_LAG + 1)
                    wait(dve, s_store[k], 16 * (m + (j - NORM_LAG) // BODY))
                    o = ps_o[k][:, 0:2 * T * VW].rearrange("p (e w) -> p e w", w=VW)
                    dve.tensor_reduce(osum[k][:].rearrange("p e q d -> p (e q) d"),
                                      o[:, :, 0:3 * DH].rearrange("p e (c d) -> p e d c", d=DH), AX.X, ALU.add).then_inc(s_part, 1)
                    dve.reciprocal(rec[k][:].rearrange("p e q -> p (e q)"), o[:, :, 3 * DH]).then_inc(s_part, 1)
                    dve.wait_ge(s_part, 2 * n + 2)
                    dve.tensor_tensor(heads[k][:].rearrange("p q e d -> p e q d"), osum[k][:],
                                      rec[k][:].rearrange("p e (q a) -> p e q a", a=1).to_broadcast([P, 2, T, DH]), ALU.mult)\
                        .then_inc(s_norm, 1)

            def bodies(first, last, bk):
                with dve.Fori(first, last) as m:
                    for j in range(BODY):
                        steps(m, j, bk)

            dve.wait_ge(s_bias[0], 16)
            for j in range(BODY):
                steps(0, j, 0)
            bodies(1, PER_HP, 0)
            dve.wait_ge(s_bias[1], 16)
            bodies(PER_HP, 2 * PER_HP, 1)
            with dve.Fori(1, PAIRS // 2) as h:
                for bk in range(2):
                    dve.wait_ge(s_bias[bk], 16 * h + 16)
                    bodies(h * (2 * PER_HP) + bk * PER_HP, h * (2 * PER_HP) + (bk + 1) * PER_HP, bk)
            for j in range(BODY):
                steps(UNITS // BODY, j, 0)


def attention_output(nc, K, heads_dram, woT, bo):
    with ExitStack() as ctx:
        ph = Phase(nc, ctx, "wo")
        w = ph.sb("w", [P, C, D])
        bo_sb = ph.sb("bo", [P, D])
        heads = [ph.sb(f"heads{k}", [P, T, PAIRS, 2 * DH]) for k in range(2)]
        ht = [ph.sb(f"ht{k}", [P, C, S]) for k in range(2)]
        xp = ph.ps("xp", [P, C, S])
        po = [ph.ps(f"po{k}", [P, T, D]) for k in range(2)]
        s_w, s_T, s_ht, s_mm, s_add, s_bias, s_st, s_ch, s_var, s_rstd = (
            ph.sem(n) for n in ("w", "T", "ht", "mm", "add", "bias", "st", "ch", "var", "rstd"))
        s_in = [ph.sem(f"in{k}") for k in range(2)]
        block = ctx.enter_context(nc.Block())

        @block.sync
        def _(sp):
            sp.dma_start(w[:], woT.rearrange("(c p) n -> p c n", p=P)).then_inc(s_w, 16)
            sp.dma_start(bo_sb[:], row_to_all(bo)).then_inc(s_w, 16)

            def load(b, k):
                row = heads_dram.rearrange("(h b) p w -> b p h w", b=B)[bass.ds(b, 1)].rearrange("a p h w -> (a p) h w")
                for q in range(T):
                    sp.dma_start(heads[k][:, q], row[:, :, q * 2 * DH:(q + 1) * 2 * DH]).then_inc(s_in[k], 16)

            for k in range(2):
                load(k, k)
            with sp.Fori(1, B // 2) as i:
                for k in range(2):
                    sp.wait_ge(s_T, 2 * i + k - 1)
                    load(2 * i + k, k)

        @block.tensor
        def _(pe):
            def turn(i, b, k):
                pe.wait_ge(s_in[k], 16 * T * i + 16 * T)
                pe.wait_ge(s_ht, b)
                for q in range(T):
                    for c in range(C):
                        last = pe.transpose(xp[:, c, q * P:(q + 1) * P], heads[k][:, q, 4 * c:4 * c + 4, :].rearrange("p h d -> p (h d)"), K.ident[:])
                last.then_inc(s_T, 1)

            def body(i, k, more):
                b = 2 * i + k
                if more:
                    turn(i + k, b + 1, 1 - k)
                pe.wait_ge(s_ht, b + 1)
                pe.wait_ge(s_add, b)
                for q in range(T):
                    for c in range(C):
                        last = pe.matmul(po[k][:, q, :], ht[k][:, c, q * P:(q + 1) * P], w[:, c, :], start=(c == 0), stop=(c == C - 1))
                last.then_inc(s_mm, 1)

            turn(0, 0, 0)
            pe.wait_ge(s_w, 32)
            slots(pe, body)

        @block.scalar
        def _(act):
            def body(i, k, more):
                b = 2 * i + k
                act.wait_ge(s_T, b + 1)
                if not (isinstance(i, int) and i == 0):
                    act.wait_ge(s_mm, b)
                else:
                    act.wait_ge(s_mm, b)
                act.activation(ht[k][:], xp[:], ACT.Copy).then_inc(s_ht, 1)

            slots(act, body)

        @block.gpsimd
        def _(pool):
            rstd_from_stats(None, pool, K, None, (s_var, s_rstd, s_ch))

        @block.vector
        def _(dve):
            dve.wait_ge(s_w, 32)

            def body(i, k, more):
                b = 2 * i + k
                rows = K.H[:, bass.ds(b * T, T), :]
                dve.tensor_tensor(rows, rows, bo_sb[:].rearrange("p (a d) -> p a d", a=1).to_broadcast([P, T, D]), ALU.add)\
                   .then_inc(s_bias, 1)
                dve.wait_ge(s_bias, b + 1)
                dve.wait_ge(s_mm, b + 1)
                dve.tensor_tensor(rows, rows, po[k][:], ALU.add).then_inc(s_add, 1)
                dve.wait_ge(s_add, b + 1)
                stats_of_row(dve, K, b).then_inc(s_st, 1)

            slots(dve, body)
            dve.wait_ge(s_st, B)
            rstd_from_stats(dve, None, K, None, (s_var, s_rstd, s_ch))
            dve.wait_ge(s_rstd, 1)


def stats_of_row(dve, K, b):
    for q in range(T):
        last = dve.bn_stats(K.stats[:, bass.ds(b * T + q, 1), :].rearrange("p a d -> p (a d)"),
                            K.H[:, bass.ds(b * T + q, 1), :].rearrange("p a d -> p (a d)"))
    return last


def inner_ffn(nc, K, w_in, b_in, w1, b1, w2, b2, w_out, b_out, xs_dram):
    RING = 4
    SUMS = INNER + 1
    with ExitStack() as ctx:
        ph = Phase(nc, ctx, "ffn")
        win_sb = ph.sb("win", [P, C, M])
        bin_sb = ph.sb("bin", [P, 1])
        w1_sb, b1_sb, w2_sb = (ph.sb(n, [P, INNER]) for n in ("w1", "b1", "w2"))
        b2_sb = ph.sb("b2", [P, 1])
        wout_sb = ph.sb("wout", [P, D])
        bout_sb = ph.sb("bout", [P, D])
        xn = [ph.sb(f"xn{k}", [P, T, D]) for k in range(2)]
        xt = [ph.sb(f"xt{k}", [P, C, S]) for k in range(2)]
        sv = ph.sb("s", [P, S])
        unit = [ph.sb(f"unit{r}", [P, S]) for r in range(RING)]
        g, g_odd = ph.sb("g", [P, S]), ph.sb("godd", [P, S])
        xp = ph.ps("xp", [P, C, S])
        ps_s = ph.ps("sp", [P, S])
        po = [ph.ps(f"po{k}", [P, T, D]) for k in range(2)]
        s_w, s_xn, s_T, s_xt, s_s, s_sv, s_unit, s_g, s_mm, s_add, s_bias, s_st, s_ch, s_var, s_rstd = (
            ph.sem(n) for n in ("w", "xn", "T", "xt", "s", "sv", "unit", "g", "mm", "add", "bias", "st", "ch", "var", "rstd"))
        s_fill = ph.sem("fill")
        NLOAD = 16 * (2 + 2 * 6)
        block = ctx.enter_context(nc.Block())

        def pairs(eng, body):
            body(0)
            with eng.Fori(1, B // 2 - 1) as i:
                body(i)
            body(B // 2 - 1, more=False)

        @block.sync
        def _(sp):
            sp.dma_start(win_sb[:], w_in.rearrange("(c p) n -> p c n", p=P)).then_inc(s_w, 16)
            sp.dma_start(bout_sb[:], row_to_all(b_out)).then_inc(s_w, 16)
            for h in range(2):
                half = slice(M * h, M * h + M)
                sp.dma_start(bin_sb[half], b_in.rearrange("(m a) -> m a", a=1)).then_inc(s_w, 16)
                sp.dma_start(b2_sb[half], b2.rearrange("(m a) -> m a", a=1)).then_inc(s_w, 16)
                sp.dma_start(w1_sb[half], w1).then_inc(s_w, 16)
                sp.dma_start(b1_sb[half], b1).then_inc(s_w, 16)
                sp.dma_start(w2_sb[half], w2).then_inc(s_w, 16)
                sp.dma_start(wout_sb[half], w_out).then_inc(s_w, 16)
            sp.dma_start(xs_dram.rearrange("(t p) w -> p t w", p=P),
                         K.pad[:].rearrange("p (a w) -> p a w", a=1).to_broadcast([P, SLOTS + 1, XW])).then_inc(s_fill, 16)
            sp.wait_ge(s_fill, 16)

        @block.tensor
        def _(pe):
            pe.wait_ge(s_w, NLOAD)

            def prepare(i):
                for k in range(2):
                    b = 2 * i + k
                    pe.wait_ge(s_xn, b + 1)
                    pe.wait_ge(s_xt, b)
                    transpose_row(pe, K, xp, xn[k]).then_inc(s_T, 1)
                    pe.wait_ge(s_xt, b + 1)
                    pe.wait_ge(s_sv, i)
                    for c in range(C):
                        last = pe.matmul(ps_s[M * k:M * k + M, :], win_sb[:, c, :], xt[k][:, c, :], start=(c == 0), stop=(c == C - 1))
                    last.then_inc(s_s, 1)

            def body(i, more=True):
                if more:
                    prepare(i + 1)
                pe.wait_ge(s_g, SUMS * i + SUMS)
                pe.wait_ge(s_add, 2 * i)
                for k in range(2):
                    for q in range(T):
                        last = pe.matmul(po[k][:, q, :], g[M * k:M * k + M, q * P:(q + 1) * P], wout_sb[M * k:M * k + M, :],
                                         start=True, stop=True)
                    last.then_inc(s_mm, 1)

            prepare(0)
            pairs(pe, body)

        @block.scalar
        def _(act):
            def copy_x(b, k):
                act.wait_ge(s_T, b + 1)
                act.wait_ge(s_s, b)
                act.activation(xt[k][:], xp[:], ACT.Copy).then_inc(s_xt, 1)

            def body(i, more=True):
                act.wait_ge(s_s, 2 * i + 2)
                act.wait_ge(s_unit, INNER * i)
                act.activation(sv[:], ps_s[:], ACT.Identity, bias=bin_sb[:]).then_inc(s_sv, 1)
                act.wait_ge(s_sv, i + 1)
                for h in range(INNER):
                    if h >= RING:
                        act.wait_ge(s_g, SUMS * i + h - RING + 1)
                    else:
                        act.wait_ge(s_g, SUMS * i)
                    act.activation(unit[h % RING][:], sv[:], ACT.Relu, scale=w1_sb[:, h:h + 1], bias=b1_sb[:, h:h + 1])\
                        .then_inc(s_unit, 1)
                    if more and h in (5, 10):
                        copy_x(2 * i + 2 + h // 10, h // 10)

            act.wait_ge(s_w, NLOAD)
            for k in range(2):
                copy_x(k, k)
            pairs(act, body)

        @block.gpsimd
        def _(pool):
            pool.wait_ge(s_w, NLOAD)

            def add_bias(b):
                rows = K.H[:, bass.ds(b * T, T), :]
                pool.wait_ge(s_xn, b + 1)
                pool.nop(nofuse=True)
                pool.tensor_tensor(rows, rows, bout_sb[:].rearrange("p (a d) -> p a d", a=1).to_broadcast([P, T, D]), ALU.add)\
                    .then_inc(s_bias, 1)

            with pool.Fori(0, B) as b:
                add_bias(b)
            rstd_from_stats(None, pool, K, None, (s_var, s_rstd, s_ch))

        @block.vector
        def _(dve):
            def norm(b, k):
                dve.wait_ge(s_T, b)
                apply_norm(dve, K, xn[k], b).then_inc(s_xn, 1)

            def body(i, more=True):
                if more:
                    norm(2 * i + 2, 0)
                for h in range(INNER):
                    dve.wait_ge(s_unit, INNER * i + h + 1)
                    if h == 0:
                        last = dve.tensor_scalar(g[:], unit[0][:], w2_sb[:, 0:1], b2_sb[:], ALU.mult, ALU.add)
                    elif h == 1:
                        last = dve.tensor_scalar(g_odd[:], unit[1][:], w2_sb[:, 1:2], None, ALU.mult)
                    else:
                        total = (g, g_odd)[h % 2]
                        dve.wait_ge(s_g, SUMS * i + h - 1)
                        last = dve.scalar_tensor_tensor(total[:], unit[h % RING][:], w2_sb[:, h:h + 1], total[:], ALU.mult, ALU.add)
                    last.then_inc(s_g, 1)
                    if more and h == 7:
                        norm(2 * i + 3, 1)
                dve.wait_ge(s_g, SUMS * i + INNER)
                dve.tensor_tensor(g[:], g[:], g_odd[:], ALU.add).then_inc(s_g, 1)
                if not (isinstance(i, int) and i == 0):
                    stats(i - 1)
                for k in range(2):
                    b = 2 * i + k
                    rows = K.H[:, bass.ds(b * T, T), :]
                    dve.wait_ge(s_mm, b + 1)
                    dve.wait_ge(s_bias, b + 1)
                    dve.tensor_tensor(rows, rows, po[k][:], ALU.add).then_inc(s_add, 1)
                if not more:
                    stats(i)

            def stats(i):
                dve.wait_ge(s_add, 2 * i + 2)
                for k in range(2):
                    stats_of_row(dve, K, 2 * i + k).then_inc(s_st, 1)

            dve.wait_ge(s_w, NLOAD)
            for k in range(2):
                norm(k, k)
            pairs(dve, body)
            dve.wait_ge(s_st, B)
            rstd_from_stats(dve, None, K, None, (s_var, s_rstd, s_ch))
            dve.wait_ge(s_rstd, 1)


def recurrence(nc, K, a_param, ig_w, ig_b, ag_w, ag_b):
    FLOOR = 1e-7
    BLK = D // 8
    with ExitStack() as ctx:
        ph = Phase(nc, ctx, "rg")
        gate_in = ph.sb("gatein", [P, B, C, S])
        gate_a = ph.sb("gatea", [P, B, C, S])
        igw, agw = ph.sb("igw", [P, C, P]), ph.sb("agw", [P, C, P])
        igb, agb, ap = ph.sb("igb", [P, C]), ph.sb("agb", [P, C]), ph.sb("ap", [P, C])
        z, w, d, l, t1 = (ph.sb(n, [P, C]) for n in ("z", "w", "d", "l", "t1"))
        rate = {n: ph.sb(f"rate{n}", [P, C]) for n in (1, 2, -1)}
        s_w, s_z, s_ch, s_rate, s_act = (ph.sem(n) for n in ("w", "z", "ch", "rate", "act"))
        s_xn, s_T, s_xt, s_g, s_sig, s_xg = (ph.sem(n) for n in ("xn", "T", "xt", "g", "sig", "xg"))
        NLOAD = 16 * (3 + 16)
        with ExitStack() as c1:
            p1 = Phase(nc, c1, "rga")
            xn = [p1.sb(f"xn{k}", [P, T, D]) for k in range(2)]
            xt = [p1.sb(f"xt{k}", [P, C, S]) for k in range(2)]
            sig = [p1.sb(f"sig{k}", [P, C, S]) for k in range(2)]
            xp = p1.ps("xp", [P, C, S])
            ps_i = p1.ps("i", [P, C, S])
            ps_a = p1.ps("a", [P, C, S])
            block = c1.enter_context(nc.Block())

            @block.sync
            def _(sp):
                sp.dma_start(igb[:], columns(ig_b.rearrange("h w -> (h w)")), allow_slow_non_contiguous=True).then_inc(s_w, 16)
                sp.dma_start(agb[:], columns(ag_b.rearrange("h w -> (h w)")), allow_slow_non_contiguous=True).then_inc(s_w, 16)
                sp.dma_start(ap[:], columns(a_param), allow_slow_non_contiguous=True).then_inc(s_w, 16)
                sp.wait_ge(s_z, 2)
                for dst, src in ((igw, ig_w), (agw, ag_w)):
                    for blk in range(8):
                        at = blk % 4 * BLK
                        sp.dma_start(dst[at:at + BLK, blk // 4, at:at + BLK], src[blk]).then_inc(s_w, 16)

            @block.gpsimd
            def _(pool):
                pool.memset(igw[:], 0.0).then_inc(s_z, 1)
                pool.memset(agw[:], 0.0).then_inc(s_z, 1)

                def body(i, k, more):
                    b = 2 * i + k
                    pool.wait_ge(s_sig, 2 * b + 1)
                    pool.tensor_tensor(gate_in[:, bass.ds(b, 1)].rearrange("p a c s -> p (a c s)"),
                                       sig[k][:].rearrange("p c s -> p (c s)"), xt[k][:].rearrange("p c s -> p (c s)"), ALU.mult)\
                        .then_inc(s_xg, 1)

                slots(pool, body)

            @block.tensor
            def _(pe):
                def turn(b, k):
                    pe.wait_ge(s_xn, b + 1)
                    pe.wait_ge(s_xt, b)
                    transpose_row(pe, K, xp, xn[k]).then_inc(s_T, 1)

                def body(i, k, more):
                    b = 2 * i + k
                    if more:
                        turn(b + 1, 1 - k)
                    pe.wait_ge(s_xt, b + 1)
                    for n, (ps, gw) in enumerate(((ps_i, igw), (ps_a, agw))):
                        pe.wait_ge(s_sig, 2 * b - 1 + n if not isinstance(b, int) or b else 0)
                        for c in range(C):
                            last = pe.matmul(ps[:, c, :], gw[:, c, :], xt[k][:, c, :], start=True, stop=True)
                        last.then_inc(s_g, 1)

                turn(0, 0)
                pe.wait_ge(s_w, NLOAD)
                for k in range(2):
                    body(0, k, True)
                with pe.Fori(1, B // 2 - 1) as i:
                    for k in range(2):
                        body(i, k, True)
                body(B // 2 - 1, 0, True)
                body(B // 2 - 1, 1, False)

            @block.scalar
            def _(act):
                act.wait_ge(s_w, NLOAD)
                act.wait_ge(s_ch, 2)
                act.activation(z[:], t1[:], ACT.Exp).then_inc(s_act, 1)
                act.wait_ge(s_ch, 3)
                act.activation(l[:], w[:], ACT.Ln).then_inc(s_act, 1)

                def body(i, k, more):
                    b = 2 * i + k
                    if more:
                        act.wait_ge(s_T, b + 2)
                        act.wait_ge(s_xg, b)
                        act.activation(xt[1 - k][:], xp[:], ACT.Copy).then_inc(s_xt, 1)
                    act.wait_ge(s_g, 2 * b + 1)
                    act.wait_ge(s_xg, b)
                    for c in range(C):
                        last = act.activation(sig[k][:, c, :], ps_i[:, c, :], ACT.Sigmoid, bias=igb[:, c:c + 1])
                    last.then_inc(s_sig, 1)
                    act.wait_ge(s_g, 2 * b + 2)
                    act.nop(nofuse=True)
                    for c in range(C):
                        last = act.activation(gate_a[:, bass.ds(b, 1), c, :].rearrange("p a s -> p (a s)"), ps_a[:, c, :],
                                              ACT.Sigmoid, bias=agb[:, c:c + 1])
                    last.then_inc(s_sig, 1)

                act.wait_ge(s_T, 1)
                act.activation(xt[0][:], xp[:], ACT.Copy).then_inc(s_xt, 1)
                slots(act, body)

            @block.vector
            def _(dve):
                n = 0

                def step(ins):
                    nonlocal n
                    n += 1
                    ins.then_inc(s_ch, 1)
                    dve.wait_ge(s_ch, n)

                apply_norm(dve, K, xn[0], 0).then_inc(s_xn, 1)
                dve.wait_ge(s_w, NLOAD)
                step(dve.tensor_scalar(t1[:], ap[:], -1.0, None, ALU.mult))
                step(dve.tensor_tensor(t1[:], t1[:], ap[:], ALU.min))
                dve.wait_ge(s_act, 1)
                step(dve.tensor_scalar(w[:], z[:], 1.0, None, ALU.add))
                step(dve.tensor_scalar(d[:], w[:], -1.0, None, ALU.add))
                step(dve.tensor_scalar(t1[:], d[:], 0.0, None, ALU.is_equal))
                step(dve.tensor_tensor(d[:], d[:], t1[:], ALU.add))
                step(dve.reciprocal(d[:], d[:]))
                dve.wait_ge(s_act, 2)
                step(dve.tensor_tensor(l[:], l[:], d[:], ALU.mult))
                step(dve.tensor_tensor(l[:], l[:], t1[:], ALU.add))
                step(dve.tensor_tensor(l[:], l[:], z[:], ALU.mult))
                step(dve.tensor_scalar(ap[:], ap[:], 0.0, None, ALU.max))
                step(dve.tensor_tensor(l[:], l[:], ap[:], ALU.add))
                for m, r in rate.items():
                    dve.tensor_scalar(r[:], l[:], -8.0 * m, None, ALU.mult).then_inc(s_rate, 1)

                def body(i, k, more):
                    b = 2 * i + k
                    if more:
                        dve.wait_ge(s_T, b)
                        apply_norm(dve, K, xn[1 - k], b + 1).then_inc(s_xn, 1)

                slots(dve, body)
                dve.wait_ge(s_rate, 3)

        with ExitStack() as c2:
            p2 = Phase(nc, c2, "rgb")
            a = [p2.sb(f"a{k}", [P, C, S]) for k in range(2)]
            ai = [p2.sb(f"ai{k}", [P, C, S]) for k in range(2)]
            q = [p2.sb(f"q{k}", [P, C, S]) for k in range(2)]
            ratio = p2.sb("ratio", [P, B, C, S])
            h = [p2.sb(f"h{k}", [P, C, S]) for k in range(2)]
            cap = p2.sb("cap", [P, S])
            pt = [p2.ps(f"t{k}", [P, T, D]) for k in range(2)]
            s_a, s_ai, s_a2, s_q, s_r, s_om, s_root, s_x, s_h, s_turn, s_add, s_st, s_cap, s_c2, s_var, s_rstd = (
                p2.sem(n) for n in ("a", "ai", "a2", "q", "r", "om", "root", "x", "h", "turn", "add", "st", "cap", "c2", "var", "rstd"))
            block = c2.enter_context(nc.Block())

            def row(t, b):
                return t[:, bass.ds(b, 1)].rearrange("p a c s -> p (a c) s")

            @block.scalar
            def _(act):
                def body(i, k, more):
                    b = 2 * i + k
                    act.wait_ge(s_r, b)
                    act.nop(nofuse=True)
                    for c in range(C):
                        last = act.activation(a[k][:, c, :], row(gate_a, b)[:, c, :], ACT.Exp, scale=rate[1][:, c:c + 1])
                    last.then_inc(s_a, 1)
                    for c in range(C):
                        last = act.activation(ai[k][:, c, :], row(gate_a, b)[:, c, :], ACT.Exp, scale=rate[-1][:, c:c + 1])
                    last.then_inc(s_ai, 1)
                    act.wait_ge(s_ai, b + 1)
                    act.nop(nofuse=True)
                    for c in range(C):
                        last = act.activation(row(gate_a, b)[:, c, :], row(gate_a, b)[:, c, :], ACT.Exp, scale=rate[2][:, c:c + 1])
                    last.then_inc(s_a2, 1)

                slots(act, body)
                with act.Fori(0, B) as b:
                    act.wait_ge(s_om, b + 1)
                    act.nop(nofuse=True)
                    act.activation(row(gate_a, b), row(gate_a, b), ACT.Sqrt).then_inc(s_root, 1)

            @block.gpsimd
            def _(pool):
                with pool.Fori(0, B) as b:
                    pool.wait_ge(s_root, b + 1)
                    x = gate_in[:, bass.ds(b, 1)].rearrange("p a c s -> p (a c s)")
                    pool.tensor_tensor(x, x, gate_a[:, bass.ds(b, 1)].rearrange("p a c s -> p (a c s)"), ALU.mult).then_inc(s_x, 1)
                rstd_from_stats(None, pool, K, None, (s_var, s_rstd, s_c2))

            @block.tensor
            def _(pe):
                def body(i, k, more):
                    b = 2 * i + k
                    pe.wait_ge(s_h, b + 1)
                    pe.wait_ge(s_add, b)
                    for t in range(T):
                        for c in range(C):
                            last = pe.transpose(pt[k][:, t, c * P:(c + 1) * P], h[k][:, c, t * P:(t + 1) * P], K.ident[:])
                    last.then_inc(s_turn, 1)

                slots(pe, body)

            @block.vector
            def _(dve):
                dve.memset(cap[:], 1.0 / FLOOR).then_inc(s_cap, 1)
                for k in range(2):
                    dve.memset(q[k][:, :, 0:1], 1.0).then_inc(s_cap, 1)
                dve.memset(ratio[:, :, :, 0:1], 0.0).then_inc(s_cap, 1)
                dve.wait_ge(s_cap, 4)

                def body(i, k, more):
                    b = 2 * i + k
                    dve.wait_ge(s_ai, b + 1)
                    for c in range(C):
                        last = dve.tensor_tensor_scan(q[k][:, c, 1:S], ai[k][:, c, 0:S - 1], cap[:, 0:S - 1], 1.0, ALU.mult, ALU.min)
                    last.then_inc(s_q, 1)
                    dve.wait_ge(s_q, b + 1)
                    dve.wait_ge(s_a, b + 1)
                    dve.scalar_tensor_tensor(row(ratio, b)[:, :, 1:S], q[k][:, :, 0:S - 1], FLOOR, a[k][:, :, 0:S - 1], ALU.mult, ALU.max)\
                       .then_inc(s_r, 1)
                    dve.wait_ge(s_a2, b + 1)
                    dve.tensor_scalar(row(gate_a, b), row(gate_a, b), -1.0, 1.0, ALU.mult, ALU.add).then_inc(s_c2, 1)
                    dve.wait_ge(s_c2, b + 1)
                    dve.tensor_scalar(row(gate_a, b), row(gate_a, b), FLOOR, None, ALU.max).then_inc(s_om, 1)

                slots(dve, body)

                def scan(i, k, more):
                    b = 2 * i + k
                    dve.wait_ge(s_x, b + 1)
                    dve.wait_ge(s_turn, b)
                    for c in range(C):
                        last = dve.tensor_tensor_scan(h[k][:, c, :], row(ratio, b)[:, c, :], row(gate_in, b)[:, c, :], 0.0,
                                                      ALU.mult, ALU.add)
                    last.then_inc(s_h, 1)
                    dve.wait_ge(s_turn, b + 1)
                    rows = K.H[:, bass.ds(b * T, T), :]
                    dve.tensor_tensor(rows, rows, pt[k][:], ALU.add).then_inc(s_add, 1)
                    dve.wait_ge(s_add, b + 1)
                    stats_of_row(dve, K, b).then_inc(s_st, 1)

                slots(dve, scan)
                dve.wait_ge(s_st, B)
                rstd_from_stats(dve, None, K, None, (s_var, s_rstd, s_c2), B)
                dve.wait_ge(s_rstd, 1)


def route(nc, K, gate_w, gate_b, h_dram, xs_dram):
    E = EXPERTS
    with ExitStack() as ctx:
        ph = Phase(nc, ctx, "route")
        gw, gb = ph.sb("gw", [P, C, E]), ph.sb("gb", [P, E])
        xa = [ph.sb(f"xa{j}", [P, TILES, XW]) for j in range(2)]
        xt = [ph.sb(f"xt{k}", [P, C, S]) for k in range(2)]
        tok_i, tok = ph.sb("toki", [P, TILES], I32), ph.sb("tok", [P, TILES])
        rank_i, rank = ph.sb("ranki", [P, E], I32), ph.sb("rank", [P, E])
        start_i, start = ph.sb("starti", [1, SLOTS], I32), ph.sb("start", [1, SLOTS])
        before, ones = ph.sb("before", [P, P]), ph.sb("ones", [P, P])
        pr, eq, tot, inc, slot, hit = (ph.sb(n, [P, TILES, E]) for n in ("pr", "eq", "tot", "inc", "slot", "hit"))
        pick = [ph.sb(f"pick{j}", [P, TILES, E]) for j in range(2)]
        best = [ph.sb(f"best{j}", [P, TILES]) for j in range(2)]
        col, posf = ph.sb("col", [P, TILES]), ph.sb("posf", [P, TILES])
        size, end, base = ph.sb("size", [P, E]), ph.sb("end", [P, E]), ph.sb("base", [P, E])
        size_i = ph.sb("sizei", [P, E], I32)
        ge = ph.sb("ge", [1, SLOTS, E])
        owner = ph.sb("owner", [1, SLOTS])
        pos = [ph.sb(f"pos{j}", [P, TILES], U32) for j in range(2)]
        xp = ph.ps("xp", [P, C, S])
        ps_g = [ph.ps(f"g{k}", [P, T, E]) for k in range(2)]
        ps_b, ps_n = ph.ps("b", [P, TILES, E]), ph.ps("n", [P, TILES, E])
        s_w, s_const, s_made, s_xn, s_T, s_xt, s_g, s_lg, s_ch, s_sub, s_exp, s_pick, s_cnt, s_copy, s_pos, s_xs, s_h, s_half = (
            ph.sem(n) for n in ("w", "const", "made", "xn", "T", "xt", "g", "lg", "ch", "sub", "exp", "pick", "cnt", "copy",
                                "pos", "xs", "h", "half"))
        block = ctx.enter_context(nc.Block())

        @block.sync
        def _(sp):
            sp.dma_start(gw[:], gate_w.rearrange("(c p) n -> p c n", p=P)).then_inc(s_w, 16)
            sp.dma_start(gb[:], row_to_all(gate_b)).then_inc(s_w, 16)
            sp.dma_start(h_dram.rearrange("(t p) d -> p t d", p=P), K.H[:]).then_inc(s_h, 16)
            sp.wait_ge(s_h, 16)

        @block.gpsimd
        def _(pool):
            pool.iota(tok_i[:], [[P, TILES]], base=0, channel_multiplier=1).then_inc(s_const, 1)
            pool.iota(rank_i[:], [[-1, E]], base=E, channel_multiplier=0).then_inc(s_const, 1)
            pool.iota(start_i[:], [[P, SLOTS]], base=0, channel_multiplier=0).then_inc(s_const, 1)
            pool.memset(ones[:], 1.0).then_inc(s_const, 1)
            pool.wait_ge(s_const, 4)
            pool.affine_select(out=before[:], in_=ones[:], compare_op=ALU.is_gt, fill=0.0, base=0,
                               pattern=[[1, P]], channel_multiplier=-1).then_inc(s_const, 1)
            pool.wait_ge(s_copy, B)
            for j in range(2):
                pool.wait_ge(s_pos, j + 1)
                for t in range(TILES):
                    pool.indirect_dma_start(out=xs_dram[:], out_offset=bass.IndirectOffsetOnAxis(ap=pos[j][:, t:t + 1], axis=0),
                                            in_=xa[j][:, t, :], in_offset=None).then_inc(s_xs, 16)
            pool.wait_ge(s_xs, 16 * 2 * TILES)

        @block.tensor
        def _(pe):
            def turn(b):
                pe.wait_ge(s_xn, b + 1)
                pe.wait_ge(s_xt, b)
                for q in range(T):
                    for c in range(C):
                        last = pe.transpose(xp[:, c, q * P:(q + 1) * P], xa[0][:, b * T + q, c * P:(c + 1) * P], K.ident[:])
                last.then_inc(s_T, 1)

            turn(0)
            pe.wait_ge(s_w, 32)
            for b in range(B):
                if b + 1 < B:
                    turn(b + 1)
                pe.wait_ge(s_xt, b + 1)
                if b >= 2:
                    pe.wait_ge(s_lg, b - 1)
                for q in range(T):
                    for c in range(C):
                        last = pe.matmul(ps_g[b % 2][:, q, :], xt[b % 2][:, c, q * P:(q + 1) * P], gw[:, c, :],
                                         start=(c == 0), stop=(c == C - 1))
                last.then_inc(s_g, 1)
            pe.wait_ge(s_pick, 1)
            pe.wait_ge(s_const, 5)
            both = hit[:].rearrange("p t e -> p (t e)")
            pe.matmul(ps_b[:].rearrange("p t e -> p (t e)"), before[:], both, start=True, stop=True)
            pe.matmul(ps_n[:].rearrange("p t e -> p (t e)"), ones[:], both, start=True, stop=True).then_inc(s_cnt, 1)

        @block.scalar
        def _(act):
            for b in range(B):
                act.wait_ge(s_T, b + 1)
                if b >= 2:
                    act.wait_ge(s_g, b - 1)
                act.activation(xt[b % 2][:], xp[:], ACT.Copy).then_inc(s_xt, 1)
                act.activation(xa[1][:, b * T:b * T + T, 0:D], xa[0][:, b * T:b * T + T, 0:D], ACT.Copy).then_inc(s_copy, 1)
            act.wait_ge(s_sub, 1)
            act.activation(pr[:], pr[:], ACT.Exp).then_inc(s_exp, 1)

        @block.vector
        def _(dve):
            n = 0

            def step(ins):
                nonlocal n
                n += 1
                ins.then_inc(s_ch, 1)
                dve.wait_ge(s_ch, n)

            def wide(col):
                return col[:].rearrange("p (t a) -> p t a", a=1).to_broadcast([P, TILES, E])

            def by_expert(row, n=TILES, parts=P):
                return row[0:parts].rearrange("p (a e) -> p a e", a=1).to_broadcast([parts, n, E])

            for b in range(B):
                for q in range(T):
                    t = b * T + q
                    last = dve.tensor_scalar(xa[0][:, t, 0:D], K.H[:, t, :], K.mean[:, t:t + 1], K.rstd[:, t:t + 1],
                                             ALU.subtract, ALU.mult)
                last.then_inc(s_xn, 1)
            dve.wait_ge(s_const, 5)
            step(dve.tensor_copy(tok[:], tok_i[:]))
            step(dve.tensor_copy(rank[:], rank_i[:]))
            step(dve.tensor_copy(start[:], start_i[:]))
            step(dve.tensor_copy(xa[0][:, :, D:XW], tok[:].rearrange("p (t a) -> p t a", a=1)))
            step(dve.tensor_scalar(xa[1][:, :, D:XW], tok[:].rearrange("p (t a) -> p t a", a=1), float(TOKENS), None, ALU.add))
            dve.wait_ge(s_w, 32)
            for b in range(B):
                dve.wait_ge(s_g, b + 1)
                dve.tensor_tensor(pr[:, b * T:b * T + T, :], ps_g[b % 2][:], by_expert(gb, T), ALU.add).then_inc(s_lg, 1)
            dve.wait_ge(s_lg, B)
            step(dve.tensor_reduce(col[:], pr[:], AX.X, ALU.max))
            dve.tensor_tensor(pr[:], pr[:], wide(col), ALU.subtract).then_inc(s_sub, 1)
            dve.wait_ge(s_exp, 1)
            step(dve.tensor_reduce(col[:], pr[:], AX.X, ALU.add))
            step(dve.reciprocal(col[:], col[:]))
            step(dve.tensor_tensor(pr[:], pr[:], wide(col), ALU.mult))
            for j in range(2):
                step(dve.tensor_reduce(best[j][:], pr[:], AX.X, ALU.max))
                step(dve.tensor_tensor(eq[:], pr[:], wide(best[j]), ALU.is_equal))
                step(dve.tensor_tensor(eq[:], eq[:], by_expert(rank), ALU.mult))
                step(dve.tensor_reduce(col[:], eq[:], AX.X, ALU.max))
                step(dve.tensor_tensor(pick[j][:], eq[:], wide(col), ALU.is_equal))
                if j == 0:
                    step(dve.scalar_tensor_tensor(pr[:], pick[0][:], -2.0, pr[:], ALU.mult, ALU.add))
            dve.tensor_tensor(hit[:], pick[0][:], pick[1][:], ALU.add).then_inc(s_pick, 1)
            step(dve.tensor_tensor(col[:], best[0][:], best[1][:], ALU.add))
            step(dve.reciprocal(col[:], col[:]))
            for j in range(2):
                step(dve.tensor_tensor(K.share[j][:], best[j][:], col[:], ALU.mult))
            dve.wait_ge(s_cnt, 1)
            step(dve.tensor_copy(tot[:], ps_n[:]))
            step(dve.memset(eq[:], 1.0))
            for e in range(E):
                step(dve.tensor_tensor_scan(inc[:, :, e], eq[:, :, e], tot[:, :, e], 0.0, ALU.mult, ALU.add))
            step(dve.tensor_scalar(size[:], inc[:, TILES - 1, :], float(P - 1), None, ALU.add))
            step(dve.tensor_copy(size_i[:], size[:]))
            step(dve.tensor_single_scalar(size_i[:], size_i[:], 0x7FFFFFFF - (P - 1), ALU.bitwise_and))
            step(dve.tensor_copy(size[:], size_i[:]))
            step(dve.tensor_tensor_scan(end[:], eq[:, 0, :], size[:], 0.0, ALU.mult, ALU.add))
            step(dve.tensor_tensor(base[:], end[:], size[:], ALU.subtract))
            step(dve.tensor_tensor(slot[:], inc[:], tot[:], ALU.subtract))
            step(dve.tensor_tensor(slot[:], slot[:], ps_b[:], ALU.add))
            step(dve.tensor_tensor(slot[:], slot[:], by_expert(base), ALU.add))
            for j in range(2):
                step(dve.tensor_tensor(eq[:], pick[j][:], slot[:], ALU.mult))
                step(dve.tensor_reduce(posf[:], eq[:], AX.X, ALU.add))
                dve.tensor_copy(pos[j][:], posf[:]).then_inc(s_pos, 1)
                dve.wait_ge(s_pos, j + 1)
            step(dve.tensor_tensor(ge[:], start[:].rearrange("p (t a) -> p t a", a=1).to_broadcast([1, SLOTS, E]),
                                   by_expert(end, SLOTS, 1), ALU.is_ge))
            step(dve.tensor_reduce(owner[:], ge[:], AX.X, ALU.add))
            step(dve.tensor_scalar(owner[:], owner[:], float(E - 1), None, ALU.min))
            step(dve.tensor_copy(K.owner[:, 0:SLOTS], owner[:]))
            step(dve.tensor_scalar(size[0:1, 0:1], end[0:1, E - 1:E], float(-P), None, ALU.add))
            step(dve.tensor_copy(size_i[0:1, 0:1], size[0:1, 0:1]))
            step(dve.tensor_single_scalar(size_i[0:1, 0:1], size_i[0:1, 0:1], 0x7FFFFFFF - (2 * P - 1), ALU.bitwise_and))
            step(dve.tensor_copy(size[0:1, 0:1], size_i[0:1, 0:1]))
            step(dve.tensor_scalar(size[0:1, 0:1], size[0:1, 0:1], 1.0 / (2 * P), None, ALU.mult))
            step(dve.tensor_copy(K.owner[:, SLOTS:SLOTS + 1], size[0:1, 0:1]))


def experts(nc, K, parts_dram, xs_dram, y_dram):
    HALF = FFN // 2
    FC = FFN // P
    DOWN = 1.0 / 16
    PASSES = ((0, 0), (0, 1), (1, 0))
    with ExitStack() as ctx:
        ph = Phase(nc, ctx, "moe")
        weights = ph.sb("w", [P, EXPERTS, 3, 2, SLAB], F16)
        xin = [ph.sb(f"xin{k}", [P, D]) for k in range(2)]
        dest_all = ph.sb("destall", [P, SLOTS])
        xt = [ph.sb(f"xt{k}", [P, 2, C, P], F16) for k in range(2)]
        dest = [ph.sb(f"dest{k}", [P, 1], U32) for k in range(2)]
        h = ph.sb("h", [P, 2, HALF])
        ht = ph.sb("ht", [P, 2, 2, FC // 2, P], F16)
        y = ph.sb("y", [P, D])
        ps_a = [ph.ps(f"a{j}", [P, HALF]) for j in range(2)]
        ps_b = [ph.ps(f"b{j}", [P, HALF]) for j in range(2)]
        ps_h = [ph.ps(f"h{j}", [P, FC // 2, P]) for j in range(2)]
        ps_y = ph.ps("py", [P, 512])
        ps_x = ph.ps("x", [P, 4, P])
        s_w, s_turnx, s_xhi, s_xt, s_turnh, s_mmy, s_yc, s_dest = (ph.sem(n) for n in ("w", "turnx", "xhi", "xt", "turnh", "mmy", "yc", "dest"))
        s_x = [ph.sem(f"x{k}") for k in range(2)]
        s_out = ph.sem("out")
        s_a, s_b, s_silu, s_h, s_hhi, s_ht = ([ph.sem(f"{n}{j}") for j in range(2)] for n in ("a", "b", "silu", "h", "hhi", "ht"))
        block = ctx.enter_context(nc.Block())

        def last_pair(eng):
            return eng.value_load(K.owner[0:1, SLOTS:SLOTS + 1], min_val=TILES - 1, max_val=SLOTS // 2 - 1)

        def tiles(eng, body, m):
            body(0, 0, start=True)
            body(0, 1)
            with eng.Fori(1, m + 1) as i:
                for k in range(2):
                    body(i, k)

        @block.sync
        def _(sp):
            def load(t, k):
                sp.dma_start(xin[k][:], xs_dram[bass.ds(t * P, P), 0:D]).then_inc(s_x[k], 16)

            for k in range(2):
                load(k, k)
            sp.dma_start(dest_all[:], xs_dram[0:SLOTS * P, D:XW].rearrange("(t p) a -> p (t a)", p=P), allow_slow_non_contiguous=True)\
                .then_inc(s_dest, 16)
            m = last_pair(sp)
            with sp.Fori(1, m + 1) as i:
                for k in range(2):
                    sp.wait_ge(s_turnx, 2 * i + k - 1)
                    load(2 * i + k, k)
            sp.wait_ge(s_turnx, 2 * m + 1)
            load(2 * m + 2, 0)

        @block.gpsimd
        def _(pool):
            for e in range(EXPERTS):
                pool.dma_start(weights[:, e].rearrange("p m c w -> p m (c w)"),
                               parts_dram[3 * e:3 * e + 3].rearrange("m p w -> p m w")).then_inc(s_w, 16)
                pool.wait_ge(s_w, 16 * e + 16)

            def store(i, k):
                t = 2 * i + k
                pool.wait_ge(s_yc, t + 1)
                pool.wait_ge(s_out, 16 * t)
                pool.nop(nofuse=True)
                pool.indirect_dma_start(out=y_dram[:], out_offset=bass.IndirectOffsetOnAxis(ap=dest[k][:, 0:1], axis=0),
                                        in_=y[:], in_offset=None).then_inc(s_out, 16)

            m = last_pair(pool)
            with pool.Fori(0, m + 1) as i:
                for k in range(2):
                    store(i, k)
            pool.wait_ge(s_out, 32 * m + 32)

        @block.tensor
        def _(pe):
            def turn_x(i, t, k):
                pe.wait_ge(s_x[k], 16 * i + 16)
                pe.wait_ge(s_xt, t)
                for c in range(C):
                    last = pe.transpose(ps_x[:, c, :], xin[k][:, c * P:(c + 1) * P], K.ident[:])
                last.then_inc(s_turnx, 1)

            def weight(e, matrix, part, first, n):
                return weights[:, bass.ds(e, 1), matrix, part, first:first + n].rearrange("p a f -> p (a f)")

            def first(ps, matrix, half, k, e):
                for c in range(C):
                    for n, (px, pw) in enumerate(PASSES):
                        last = pe.matmul(ps[half][:], xt[k][:, px, c, :], weight(e, matrix, pw, c * FFN + half * HALF, HALF),
                                         start=(c == 0 and n == 0), stop=(c == C - 1 and n == len(PASSES) - 1))
                return last

            def turn_h(t):
                for j in range(2):
                    pe.wait_ge(s_h[j], t + 1)
                    if not (isinstance(t, int) and t < 1):
                        pe.wait_ge(s_ht[j], t)
                    for f in range(FC // 2):
                        last = pe.transpose(ps_h[j][:, f, :], h[:, j, f * P:(f + 1) * P], K.ident[:])
                last.then_inc(s_turnh, 1)

            def last_product(t, e):
                if not (isinstance(t, int) and t < 1):
                    pe.wait_ge(s_yc, t)
                for j in range(2):
                    pe.wait_ge(s_ht[j], t + 1)
                    for f in range(FC // 2):
                        g = j * (FC // 2) + f
                        for n, (px, pw) in enumerate(PASSES):
                            last = pe.matmul(ps_y[:, 0:D], ht[:, px, j, f, :], weight(e, 2, pw, g * D, D),
                                             start=(g == 0 and n == 0), stop=(g == FC - 1 and n == len(PASSES) - 1))
                last.then_inc(s_mmy, 1)

            def owner(t):
                return pe.value_load(K.owner[0:1, bass.ds(t, 1)], min_val=0, max_val=EXPERTS - 1)

            def body(i, k, start=False):
                t = 2 * i + k
                e = owner(t)
                pe.wait_ge(s_w, 16 * e + 16)
                pe.wait_ge(s_xt, t + 1)
                pe.wait_ge(s_silu[0], t)
                first(ps_a, 0, 0, k, e).then_inc(s_a[0], 1)
                if not start:
                    turn_h(t - 1)
                pe.wait_ge(s_h[0], t)
                first(ps_b, 1, 0, k, e).then_inc(s_b[0], 1)
                pe.wait_ge(s_silu[1], t)
                first(ps_a, 0, 1, k, e).then_inc(s_a[1], 1)
                if not start:
                    last_product(t - 1, owner(t - 1))
                turn_x(i + k, t + 1, 1 - k)
                pe.wait_ge(s_h[1], t)
                first(ps_b, 1, 1, k, e).then_inc(s_b[1], 1)

            turn_x(0, 0, 0)
            m = last_pair(pe)
            tiles(pe, body, m)
            turn_h(2 * m + 1)
            last_product(2 * m + 1, owner(2 * m + 1))

        @block.scalar
        def _(act):
            def copy_h(t):
                act.wait_ge(s_turnh, t + 1)
                if not (isinstance(t, int) and t < 1):
                    act.wait_ge(s_mmy, t)
                for j in range(2):
                    act.activation(ht[:, 0, j], ps_h[j][:], ACT.Copy, scale=DOWN).then_inc(s_hhi[j], 1)

            def copy_x(t, k):
                act.wait_ge(s_turnx, t + 1)
                if not (isinstance(t, int) and t < 2):
                    act.wait_ge(s_b[1], t - 1)
                act.activation(xt[k][:, 0], ps_x[:, 0:C, :], ACT.Copy).then_inc(s_xhi, 1)

            def copy_y(k, t):
                act.wait_ge(s_mmy, t + 1)
                if isinstance(t, int) and t < 1:
                    act.wait_ge(s_dest, 16)
                if not (isinstance(t, int) and t < 1):
                    act.wait_ge(s_out, 16 * t)
                act.nop(nofuse=True)
                act.activation(dest[k][:], dest_all[:, bass.ds(t, 1)], ACT.Copy)
                act.activation(y[:], ps_y[:, 0:D], ACT.Copy, scale=1.0 / DOWN).then_inc(s_yc, 1)

            def body(i, k, start=False):
                t = 2 * i + k
                if not start:
                    copy_h(t - 1)
                act.wait_ge(s_a[0], t + 1)
                act.wait_ge(s_turnh, t)
                act.activation(h[:, 0], ps_a[0][:], ACT.Silu).then_inc(s_silu[0], 1)
                act.wait_ge(s_a[1], t + 1)
                act.activation(h[:, 1], ps_a[1][:], ACT.Silu).then_inc(s_silu[1], 1)
                copy_x(t + 1, 1 - k)
                if not start:
                    copy_y(1 - k, t - 1)

            copy_x(0, 0)
            m = last_pair(act)
            tiles(act, body, m)
            copy_h(2 * m + 1)
            copy_y(1, 2 * m + 1)

        @block.vector
        def _(dve):
            def rest_x(t, k):
                dve.wait_ge(s_xhi, t + 1)
                if not (isinstance(t, int) and t < 2):
                    dve.wait_ge(s_b[1], t - 1)
                dve.tensor_tensor(xt[k][:, 1], ps_x[:, 0:C, :], xt[k][:, 0], ALU.subtract).then_inc(s_xt, 1)

            def rest_h(t):
                for j in range(2):
                    dve.wait_ge(s_hhi[j], t + 1)
                    if not (isinstance(t, int) and t < 1):
                        dve.wait_ge(s_mmy, t)
                    dve.scalar_tensor_tensor(ht[:, 1, j], ps_h[j][:], DOWN, ht[:, 0, j], ALU.mult, ALU.subtract).then_inc(s_ht[j], 1)

            def body(i, k, start=False):
                t = 2 * i + k
                if not start:
                    rest_h(t - 1)
                for j in range(2):
                    if j == 1:
                        rest_x(t + 1, 1 - k)
                    dve.wait_ge(s_silu[j], t + 1)
                    dve.wait_ge(s_b[j], t + 1)
                    dve.tensor_tensor(h[:, j], h[:, j], ps_b[j][:], ALU.mult).then_inc(s_h[j], 1)

            rest_x(0, 0)
            m = last_pair(dve)
            tiles(dve, body, m)
            rest_h(2 * m + 1)


def combine(nc, K, h_dram, y_dram, out):
    G = 4
    N = TILES // G
    with ExitStack() as ctx:
        ph = Phase(nc, ctx, "comb")
        hh = ph.sb("h", [P, TILES, D])
        yy = [ph.sb(f"y{j}", [P, TILES, D]) for j in range(2)]
        s_in, s_one, s_two, s_out = (ph.sem(n) for n in ("in", "one", "two", "out"))
        block = ctx.enter_context(nc.Block())
        s_step = [ph.sem(f"step{g}") for g in range(N)]

        def rows(dram, g, first=0):
            return dram[first + g * G * P:first + (g + 1) * G * P, :].rearrange("(t p) d -> p t d", p=P)

        @block.sync
        def _(sp):
            for g in range(N):
                cut = slice(g * G, (g + 1) * G)
                sp.dma_start(hh[:, cut, :], rows(h_dram, g)).then_inc(s_step[g], 16)
                for j in range(2):
                    sp.dma_start(yy[j][:, cut, :], rows(y_dram, g, j * TOKENS)).then_inc(s_step[g], 16)

        @block.scalar
        def _(act):
            flat = out.rearrange("b s d -> (b s) d")
            for g in range(N):
                act.wait_ge(s_two, g + 1)
                act.dma_start(rows(flat, g), hh[:, g * G:(g + 1) * G, :]).then_inc(s_out, 16)
            act.wait_ge(s_out, 16 * N)

        @block.vector
        def _(dve):
            for g in range(N):
                dve.wait_ge(s_step[g], 48)
                for j, s in ((0, s_one), (1, s_two)):
                    for t in range(g * G, (g + 1) * G):
                        last = dve.scalar_tensor_tensor(hh[:, t, :], yy[j][:, t, :], K.share[j][:, t:t + 1], hh[:, t, :],
                                                        ALU.mult, ALU.add)
                    last.then_inc(s, 1)
                    if j == 0:
                        dve.wait_ge(s_one, g + 1)


def program(nc, I, out):
    Phase.used = []
    with ExitStack() as ctx:
        class K:
            pass
        ph = Phase(nc, ctx, "k")
        K.ident = ph.sb("ident", [P, P])
        K.share = [ph.sb(f"share{j}", [P, TILES]) for j in range(2)]
        K.owner = ph.sb("owner", [1, SLOTS + 1], I32)

        def dram(name, shape, dt=F32):
            return nc.dram_tensor(name, shape, dt, kind="Internal")

        h_dram = dram("h", [TOKENS, D])
        xs_dram = dram("x_sorted", [(SLOTS + 1) * P, XW])
        experts_parts = dram("experts_parts", [SLABS, P, 2 * SLAB], F16)
        y_dram = dram("y", [2 * TOKENS + P, D])
        with ExitStack() as stream:
            ph = Phase(nc, stream, "k")
            K.H = ph.sb("H", [P, TILES, D])
            K.pad = ph.sb("pad", [P, XW])
            K.stats = ph.sb("stats", [P, TILES, 6])
            K.mean = ph.sb("mean", [P, TILES])
            K.var = ph.sb("var", [P, TILES])
            K.rstd = ph.sb("rstd", [P, TILES])
            K.minus_half = ph.sb("mhalf", [P, TILES])
            rlen = dram("rlen", [B, S])
            q_dram = dram("q_parts", [B, len(SPLITS), D, S], BF16)
            k_dram = dram("k_parts", [B, len(SPLITS), D, S], BF16)
            v_dram = dram("v_parts", [PAIRS, B, P, T * 2 * VW], BF16)
            heads_dram = dram("heads", [PAIRS * B, P, T * 2 * DH])
            constants(nc, K)
            embed(nc, K, I["x"], I["mask"], I["embT"], I["pcaT"], I["proj_w"], I["proj_b"], I["fus_w"], I["fus_b"],
                  I["ln_g"], I["ln_b"], rlen)
            project_qkv(nc, K, I["wqT"], I["bq"], I["wkT"], I["bk"], I["wvT"], I["bv"], q_dram, k_dram, v_dram)
            attention(nc, K, I["pos_bias"], q_dram, k_dram, v_dram, heads_dram, I["experts"], experts_parts)
            attention_output(nc, K, heads_dram, I["woT"], I["bo"])
            inner_ffn(nc, K, *(I[n] for n in ("f_win", "f_bin", "f_w1", "f_b1", "f_w2", "f_b2", "f_wout", "f_bout")), xs_dram)
            recurrence(nc, K, *(I[n] for n in ("a_param", "ig_w", "ig_b", "ag_w", "ag_b")))
            recycle(nc)
            route(nc, K, I["gate_w"], I["gate_b"], h_dram, xs_dram)
        experts(nc, K, experts_parts, xs_dram, y_dram)
        combine(nc, K, h_dram, y_dram, out)


def kernel(**inputs):
    import numpy as np
    import concourse.bacc as bacc
    from concourse.bass_utils import run_bass_kernel_spmd

    a = {k: np.asarray(v) for k, v in inputs.items()}
    slabs = np.stack([a[n].reshape(EXPERTS, -1, P, a[n].shape[2]).transpose(0, 2, 1, 3).reshape(EXPERTS, P, SLAB)
                      for n in ("L1_ffn_w1", "L1_ffn_w3", "L1_ffn_w2")], axis=1).reshape(SLABS, P, SLAB)
    arrays = {
        "x": a["x"], "mask": a["mask_BS_i1_0"],
        "embT": a["L0_tok_emb"].T, "pcaT": a["L0_tok_pca_lookup"].T,
        "wqT": a["L0_attn_Wq"].T, "bq": a["L0_attn_bq"], "wkT": a["L0_attn_Wk"].T, "bk": a["L0_attn_bk"],
        "wvT": a["L0_attn_Wv"].T, "bv": a["L0_attn_bv"],
        "pos_bias": a["L0_attn_pos_bias"],
        "woT": a["L0_attn_Wo"].T, "bo": a["L0_attn_bo"],
        "f_win": a["L0_ffn_Win"], "f_bin": a["L0_ffn_bin_"], "f_w1": a["L0_ffn_W1"], "f_b1": a["L0_ffn_b1"],
        "f_w2": a["L0_ffn_W2"], "f_b2": a["L0_ffn_b2"], "f_wout": a["L0_ffn_Wout"], "f_bout": a["L0_ffn_bout"],
        "a_param": a["L1_attn_a_param"], "ig_w": a["L1_attn_ig_w"], "ig_b": a["L1_attn_ig_b"],
        "ag_w": a["L1_attn_ag_w"], "ag_b": a["L1_attn_ag_b"],
        "gate_w": a["L1_ffn_gate_w"], "gate_b": a["L1_ffn_gate_b"], "experts": slabs,
        "proj_w": a["L0_tok_proj_w"], "proj_b": a["L0_tok_proj_b"],
        "fus_w": a["L0_tok_fus_w"], "fus_b": a["L0_tok_fus_b"], "ln_g": a["L0_tok_ln_g"], "ln_b": a["L0_tok_ln_b"],
    }
    arrays = {k: np.ascontiguousarray(v) for k, v in arrays.items()}
    nc = bacc.Bacc("TRN2", target_bir_lowering=False, num_devices=1)
    args = {k: nc.dram_tensor(f"in_{k}", v.shape, mybir.dt.from_np(v.dtype), kind="ExternalInput").ap() for k, v in arrays.items()}
    out = nc.dram_tensor("out", (B, S, D), F32, kind="ExternalOutput").ap()
    program(nc, args, out)
    r = run_bass_kernel_spmd(nc, [{f"in_{k}": v for k, v in arrays.items()}], core_ids=[0])
    return r.results[0]["out"]
```

```python
from contextlib import ExitStack

import concourse.bass as bass
from concourse import mybir

F32 = mybir.dt.float32
BF16 = mybir.dt.bfloat16
F16 = mybir.dt.float16
I32 = mybir.dt.int32
U32 = mybir.dt.uint32
ALU = mybir.AluOpType
ACT = mybir.ActivationFunctionType
AX = mybir.AxisListType

P = 128
B, S, D = 8, 512, 256
C = D // P
T = S // P
TILES = B * T
V = 28
HEADS, DH = 16, 16
PAIRS = HEADS // 2
MAXLEN = 512
SCALE = float(DH) ** -0.5
BIASW = S + MAXLEN - P
SPLITS = ((0, 0), (1, 0), (2, 0), (0, 1), (1, 1), (0, 2))
RUNS = ((0, 3), (3, 5), (5, 6))
STACK = DH * len(SPLITS)
VW = 3 * DH + 1
LIFT = 10.0
M, INNER = 64, 16
FFN, EXPERTS = 1024, 8
SLOTS = 2 * TILES + EXPERTS
EPS = 1e-5
TOKENS = B * S
GROUP = 2 * T
SLABS, SLAB = 3 * EXPERTS, C * FFN


class Phase:

    used = []

    def __init__(self, nc, ctx, name):
        self.nc, self.ctx, self.name = nc, ctx, name

    def sb(self, name, shape, dt=F32):
        return self.ctx.enter_context(self.nc.sbuf_tensor(f"{self.name}_{name}", shape, dt))

    def ps(self, name, shape, dt=F32):
        return self.ctx.enter_context(self.nc.psum_tensor(f"{self.name}_{name}", shape, dt))

    def sem(self, name):
        Phase.used.append(self.nc.alloc_semaphore(f"{self.name}_{name}"))
        return Phase.used[-1]


def recycle(nc):
    nc.clear_and_free_semaphores(Phase.used)
    Phase.used = []
    with nc.Block() as block:
        @block.gpsimd
        def _(pool):
            pool.nop(nofuse=True)


def row_to_all(dram_row, n=P):
    return dram_row.rearrange("(a w) -> a w", a=1).partition_broadcast(n)


def columns(dram_vec):
    return dram_vec.rearrange("(c p) -> p c", p=P)


def constants(nc, K):
    with ExitStack() as ctx:
        ph = Phase(nc, ctx, "const")
        s_id = ph.sem("id")
        block = ctx.enter_context(nc.Block())

        @block.gpsimd
        def _(pool):
            pool.memset(K.ident[:], 1.0).then_inc(s_id, 1)
            pool.wait_ge(s_id, 1)
            pool.affine_select(out=K.ident[:], in_=K.ident[:], compare_op=ALU.is_equal, fill=0.0, base=0,
                               pattern=[[-1, P]], channel_multiplier=1).then_inc(s_id, 1)
            pool.memset(K.minus_half[:], -0.5).then_inc(s_id, 1)
            pool.memset(K.igw[:], 0.0).then_inc(s_id, 1)
            pool.memset(K.agw[:], 0.0).then_inc(s_id, 1)
            pool.wait_ge(s_id, 5)


def bias_rows(pos_bias, hp):
    return bass.AP(pos_bias.tensor, pos_bias.offset + hp * (2 * (2 * MAXLEN - 1)), [[1, P], [2 * MAXLEN - 1, 2], [1, BIASW]])


def allocate_parameters(nc, ctx, K):
    ph = Phase(nc, ctx, "par")
    K.bias = [ph.sb(f"bias{k}", [P, 2, BIASW]) for k in range(2)]
    K.s_bias = [ph.sem(f"bias{k}") for k in range(2)]
    K.wqkv = {n: ph.sb(f"w{n}", [P, C, D]) for n in "qkv"}
    K.bq, K.bk, K.bv = ph.sb("bq", [P, C]), ph.sb("bk", [P, C]), ph.sb("bv", [P, D])
    K.wo, K.bo = ph.sb("wo", [P, C, D]), ph.sb("bo", [P, D])
    K.win, K.bin = ph.sb("win", [P, C, M]), ph.sb("bin", [P, 1])
    K.w1, K.b1, K.w2 = (ph.sb(n, [P, INNER]) for n in ("w1", "b1", "w2"))
    K.b2, K.wout, K.bout = ph.sb("b2", [P, 1]), ph.sb("wout", [P, D]), ph.sb("bout", [P, D])
    K.igw, K.agw = ph.sb("igw", [P, C, P]), ph.sb("agw", [P, C, P])
    K.igb, K.agb, K.ap = ph.sb("igb", [P, C]), ph.sb("agb", [P, C]), ph.sb("ap", [P, C])
    K.gw, K.gb = ph.sb("gw", [P, C, EXPERTS]), ph.sb("gb", [EXPERTS, 1])
    K.s_par = ph.sem("par")
    K.parameters = 16 * (6 + 2 + 2 + 2 * 6 + 3 + 2 * 8 + 2)


def load_parameters(sp, K, I):
    for dst, name in ((K.wqkv["q"], "wqT"), (K.wqkv["k"], "wkT"), (K.wqkv["v"], "wvT"), (K.wo, "woT"), (K.win, "f_win"),
                      (K.gw, "gate_w")):
        sp.dma_start(dst[:], I[name].rearrange("(c p) n -> p c n", p=P)).then_inc(K.s_par, 16)
    for dst, name in ((K.bq, "bq"), (K.bk, "bk"), (K.ap, "a_param")):
        sp.dma_start(dst[:], columns(I[name]), allow_slow_non_contiguous=True).then_inc(K.s_par, 16)
    for dst, name in ((K.igb, "ig_b"), (K.agb, "ag_b")):
        sp.dma_start(dst[:], columns(I[name].rearrange("h w -> (h w)")), allow_slow_non_contiguous=True).then_inc(K.s_par, 16)
    for dst, name in ((K.bv, "bv"), (K.bo, "bo"), (K.bout, "f_bout")):
        sp.dma_start(dst[:], row_to_all(I[name])).then_inc(K.s_par, 16)
    sp.dma_start(K.gb[:], I["gate_b"].rearrange("(e a) -> e a", a=1)).then_inc(K.s_par, 16)
    for h in range(2):
        half = slice(M * h, M * h + M)
        for dst, name in ((K.bin, "f_bin"), (K.b2, "f_b2")):
            sp.dma_start(dst[half], I[name].rearrange("(m a) -> m a", a=1)).then_inc(K.s_par, 16)
        for dst, name in ((K.w1, "f_w1"), (K.b1, "f_b1"), (K.w2, "f_w2"), (K.wout, "f_wout")):
            sp.dma_start(dst[half], I[name]).then_inc(K.s_par, 16)
    width = D // 8
    for dst, name in ((K.igw, "ig_w"), (K.agw, "ag_w")):
        for blk in range(8):
            at = blk % 4 * width
            sp.dma_start(dst[at:at + width, blk // 4, at:at + width], I[name][blk]).then_inc(K.s_par, 16)
    for k in range(2):
        sp.dma_start(K.bias[k][:], bias_rows(I["pos_bias"], k)).then_inc(K.s_bias[k], 16)


def rstd_from_stats(dve, pool, K, sems, done=0, group=None):
    s_var, s_rstd, s_chain = sems
    g, tiles = (0, slice(0, TILES)) if group is None else (group, slice(group * GROUP, (group + 1) * GROUP))
    ev, od = K.stats[:, tiles, 0:3], K.stats[:, tiles, 3:6]
    mean, var = K.mean[:, tiles], K.var[:, tiles]
    if dve is not None:
        n = done

        def step(ins):
            nonlocal n
            n += 1
            ins.then_inc(s_chain, 1)
            dve.wait_ge(s_chain, n)

        step(dve.tensor_tensor(mean, ev[:, :, 1], od[:, :, 1], ALU.add))
        step(dve.tensor_scalar(mean, mean, 0.5, None, ALU.mult))
        step(dve.tensor_tensor(var, ev[:, :, 1], od[:, :, 1], ALU.subtract))
        step(dve.scalar_tensor_tensor(var, var, 0.25, var, ALU.mult, ALU.mult))
        step(dve.scalar_tensor_tensor(var, ev[:, :, 2], 1.0 / D, var, ALU.mult, ALU.add))
        step(dve.scalar_tensor_tensor(var, od[:, :, 2], 1.0 / D, var, ALU.mult, ALU.add))
        dve.tensor_scalar(var, var, EPS, None, ALU.add).then_inc(s_var, 1)
    if pool is not None:
        pool.wait_ge(s_var, g + 1)
        pool.tensor_tensor(K.rstd[:, tiles], var, K.minus_half[:, tiles], ALU.pow).then_inc(s_rstd, 1)


def rstd_groups(pool, K, s_rstd):
    for g in range(TILES // GROUP):
        tiles = slice(g * GROUP, (g + 1) * GROUP)
        pool.tensor_tensor(K.rstd[:, tiles], K.var[:, tiles], K.minus_half[:, tiles], ALU.pow).then_inc(s_rstd, 1)


def embed(nc, K, x, mask, embT, pcaT, proj_w, proj_b, fus_w, fus_b, ln_g, ln_b, rlen_dram, I):
    HB = B // 2
    with ExitStack() as ctx:
        ph = Phase(nc, ctx, "emb")
        ids = ph.sb("ids", [P, HB, S], I32)
        mk = ph.sb("mk", [P, HB, S], I32)
        m8 = ph.sb("m8", [B, S], I32)
        mf = ph.sb("mf", [B, S + 2])
        rl8 = ph.sb("rl8", [B, S])
        rl = ph.sb("rl", [P, HB, S])
        vocab = ph.sb("vocab", [P, 1], I32)
        vocabf = ph.sb("vocabf", [P, 1])
        onerow = ph.sb("onerow", [P, 1])
        hot = ph.sb("hot", [P, HB, S])
        win = ph.sb("win", [P, HB, S + 2])
        embT_sb = ph.sb("embT", [P, C, V])
        pcaT_sb = ph.sb("pcaT", [20, V])
        proj_sb = ph.sb("proj", [20, D])
        projb_sb = ph.sb("projb", [P, C])
        fus_sb = ph.sb("fus", [P, 2 * C, D])
        fusb_sb = ph.sb("fusb", [1, D])
        fold = ph.sb("fold", [P, 2 * C, P])
        foldb = ph.sb("foldb", [1, P])
        table = ph.sb("table", [P, D])
        negm = ph.sb("negm", [P, TILES])
        g_sb = ph.sb("g", [P, D])
        b_sb = ph.sb("b", [P, D])
        ps_c = ph.ps("c", [P, C, V])
        ps_t = ph.ps("t", [P, D])
        ps_f = [ph.ps(f"f{i}", [P, 2, D]) for i in range(4)]
        s_io, s_w, s_m8, s_voc, s_rl, s_rlb = (ph.sem(n) for n in ("io", "w", "m8", "voc", "rl", "rlb"))
        s_zero, s_fold, s_c, s_tab, s_tabsb, s_cols = (ph.sem(n) for n in ("zero", "fold", "c", "tab", "tabsb", "cols"))
        s_mm, s_keep, s_st, s_ch, s_var, s_rstd, s_ln = (ph.sem(n) for n in ("mm", "keep", "st", "ch", "var", "rstd", "ln"))
        s_chain, s_negm, s_scaled, s_shifted = (ph.sem(n) for n in ("chain", "negm", "scaled", "shifted"))
        block = ctx.enter_context(nc.Block())

        @block.sync
        def _(sp):
            sp.dma_start(m8[:], mask).then_inc(s_m8, 16)
            for h in range(2):
                sp.dma_start(ids[64 * h:64 * h + 64].rearrange("p b s -> p (b s)"),
                             row_to_all(x[HB * h:HB * h + HB].rearrange("b s -> (b s)"), 64)).then_inc(s_io, 16)
                sp.dma_start(mk[64 * h:64 * h + 64].rearrange("p b s -> p (b s)"),
                             row_to_all(mask[HB * h:HB * h + HB].rearrange("b s -> (b s)"), 64)).then_inc(s_io, 16)
            sp.wait_ge(s_rl, 1)
            sp.dma_start(rlen_dram[:], rl8[:]).then_inc(s_rlb, 16)
            sp.wait_ge(s_rlb, 16)
            for h in range(2):
                sp.dma_start(rl[64 * h:64 * h + 64].rearrange("p b s -> p (b s)"),
                             row_to_all(rlen_dram[HB * h:HB * h + HB].rearrange("b s -> (b s)"), 64)).then_inc(s_rlb, 16)
            load_parameters(sp, K, I)

        @block.scalar
        def _(act):
            act.dma_start(fus_sb[:], fus_w.rearrange("(c p) n -> p c n", p=P)).then_inc(s_w, 16)
            act.dma_start(embT_sb[:], embT.rearrange("(c p) v -> p c v", p=P)).then_inc(s_w, 16)
            act.dma_start(pcaT_sb[:], pcaT).then_inc(s_w, 16)
            act.dma_start(proj_sb[:], proj_w).then_inc(s_w, 16)
            act.dma_start(projb_sb[:], columns(proj_b), allow_slow_non_contiguous=True).then_inc(s_w, 16)
            act.dma_start(fusb_sb[:], fus_b.rearrange("(a n) -> a n", a=1)).then_inc(s_w, 16)
            act.dma_start(g_sb[:], row_to_all(ln_g)).then_inc(s_w, 16)
            act.dma_start(b_sb[:], row_to_all(ln_b)).then_inc(s_w, 16)
            def normalise(g):
                act.wait_ge(s_negm, g + 1)
                for t in range(g * GROUP, (g + 1) * GROUP):
                    last = act.activation(K.H[:, t, :], K.H[:, t, :], ACT.Identity, scale=K.rstd[:, t:t + 1], bias=negm[:, t:t + 1])
                last.then_inc(s_ln, 1)

            for i in range(TILES // 2):
                act.wait_ge(s_mm, i + 1)
                act.activation(K.H[:, 2 * i:2 * i + 2, :], ps_f[i % 4][:], ACT.Copy).then_inc(s_keep, 1)
                if (i - 3) % (GROUP // 2) == 0 and i > 3:
                    normalise((i - 3) // (GROUP // 2) - 1)
            normalise(TILES // GROUP - 1)

        @block.gpsimd
        def _(pool):
            pool.iota(vocab[:], [[0, 1]], base=0, channel_multiplier=1).then_inc(s_voc, 1)
            pool.memset(fold[:], 0.0).then_inc(s_zero, 1)
            pool.memset(foldb[:], 0.0).then_inc(s_zero, 1)
            pool.memset(win[:], 0.0).then_inc(s_zero, 1)

            def shift(g):
                pool.wait_ge(s_scaled, g + 1)
                rows = K.H[:, g * GROUP:(g + 1) * GROUP, :]
                pool.tensor_tensor(rows, rows, b_sb[:].rearrange("p (a d) -> p a d", a=1).to_broadcast([P, GROUP, D]), ALU.add)\
                    .then_inc(s_shifted, 1)

            for g in range(TILES // GROUP):
                rstd_from_stats(None, pool, K, (s_var, s_rstd, s_ch), group=g)
                if g > 0:
                    shift(g - 1)
            shift(TILES // GROUP - 1)

        @block.tensor
        def _(pe):
            pe.wait_ge(s_w, 128)
            for c in range(C):
                pe.matmul(ps_c[:, c, :], proj_sb[:, c * P:(c + 1) * P], pcaT_sb[:], start=True, stop=True).then_inc(s_c, 1)
            pe.wait_ge(s_fold, 1)
            for c in range(2 * C):
                pe.matmul(ps_t[:], fold[:, c, :], fus_sb[:, c, :], start=(c == 0), stop=False)
            pe.matmul(ps_t[:], foldb[:], fusb_sb[:], start=False, stop=True).then_inc(s_tab, 1)
            pe.wait_ge(s_tabsb, 1)
            pe.wait_ge(s_cols, 1)
            for i in range(TILES // 2):
                if i >= 4:
                    pe.wait_ge(s_keep, i - 3)
                for j in range(2):
                    t = 2 * i + j
                    h, b, q = t // (TILES // 2), t // T % HB, t % T
                    last = pe.matmul(ps_f[i % 4][:, j, :], hot[64 * h:64 * h + 64, b, q * P:(q + 1) * P],
                                     table[64 * h:64 * h + 64, :], start=True, stop=True)
                last.then_inc(s_mm, 1)

        @block.vector
        def _(dve):
            n = 0

            def step(ins):
                nonlocal n
                n += 1
                ins.then_inc(s_ch, 1)
                dve.wait_ge(s_ch, n)

            step(dve.memset(mf[:], 0.0))
            dve.wait_ge(s_m8, 16)
            step(dve.tensor_copy(mf[:, 1:S + 1], m8[:]))
            step(dve.tensor_tensor(rl8[:], mf[:, 0:S], mf[:, 1:S + 1], ALU.add))
            step(dve.tensor_tensor(rl8[:], rl8[:], mf[:, 2:S + 2], ALU.add))
            step(dve.tensor_scalar(rl8[:], rl8[:], 1.0, None, ALU.max))
            n += 1
            dve.reciprocal(rl8[:], rl8[:]).then_inc(s_ch, 1)
            dve.wait_ge(s_ch, n)
            dve.sem_inc(s_rl, 1)
            dve.wait_ge(s_voc, 1)
            step(dve.tensor_single_scalar(vocab[:], vocab[:], 31, ALU.bitwise_and))
            step(dve.tensor_copy(vocabf[:], vocab[:]))
            step(dve.tensor_scalar(onerow[:], vocabf[:], float(V), None, ALU.is_equal))
            dve.wait_ge(s_io, 64)
            dve.wait_ge(s_zero, 3)
            step(dve.scalar_tensor_tensor(win[:, :, 1:S + 1], ids[:], vocabf[:], mk[:], ALU.is_equal, ALU.mult))
            dve.wait_ge(s_w, 128)
            dve.wait_ge(s_c, C)
            for h in range(2):
                step(dve.tensor_copy(fold[:, 0:C, 64 * h:64 * h + V], embT_sb[:]))
                step(dve.tensor_copy(fold[:, C:2 * C, 64 * h + 32:64 * h + 32 + V], ps_c[:]))
                step(dve.tensor_copy(fold[:, C:2 * C, 64 * h + V:64 * h + V + 1], projb_sb[:].rearrange("p (c a) -> p c a", a=1)))
                step(dve.memset(foldb[:, 64 * h + V:64 * h + V + 1], 1.0))
            dve.sem_inc(s_fold, 1)
            step(dve.tensor_tensor(hot[:], win[:, :, 0:S], win[:, :, 1:S + 1], ALU.add))
            step(dve.tensor_tensor(hot[:], hot[:], win[:, :, 2:S + 2], ALU.add))
            dve.wait_ge(s_rlb, 48)
            step(dve.tensor_tensor(hot[:], hot[:], rl[:], ALU.mult))
            for h in range(2):
                p = slice(64 * h, 64 * h + 32)
                step(dve.tensor_scalar(hot[p], ids[p], vocabf[p], onerow[p], ALU.is_equal, ALU.max))
            dve.sem_inc(s_cols, 1)
            dve.wait_ge(s_tab, 1)
            dve.tensor_copy(table[:], ps_t[:]).then_inc(s_tabsb, 1)
            groups = TILES // GROUP

            def scale(g):
                dve.wait_ge(s_ln, g + 1)
                rows = K.H[:, g * GROUP:(g + 1) * GROUP, :]
                dve.tensor_tensor(rows, rows, g_sb[:].rearrange("p (a d) -> p a d", a=1).to_broadcast([P, GROUP, D]), ALU.mult)\
                   .then_inc(s_scaled, 1)

            def next_stats(g):
                dve.wait_ge(s_shifted, g + 1)
                for t in range(g * GROUP, (g + 1) * GROUP):
                    last = dve.bn_stats(K.stats[:, t, :], K.H[:, t, :])
                last.then_inc(s_st, 1)

            for g in range(groups):
                for i in range(g * GROUP // 2, (g + 1) * GROUP // 2):
                    dve.wait_ge(s_keep, i + 1)
                    for j in range(2):
                        last = dve.bn_stats(K.stats[:, 2 * i + j, :], K.H[:, 2 * i + j, :])
                    last.then_inc(s_st, 1)
                dve.wait_ge(s_st, (g + 1) * GROUP // 2 + max(g - 2, 0))
                rstd_from_stats(dve, None, K, (s_var, s_rstd, s_chain), 6 * g, g)
                if g > 0:
                    scale(g - 1)
                dve.wait_ge(s_rstd, g + 1)
                tiles = slice(g * GROUP, (g + 1) * GROUP)
                dve.scalar_tensor_tensor(negm[:, tiles], K.mean[:, tiles], -1.0, K.rstd[:, tiles], ALU.mult, ALU.mult).then_inc(s_negm, 1)
                if g > 1:
                    next_stats(g - 2)
            scale(groups - 1)
            for g in range(groups - 2, groups):
                next_stats(g)
            dve.wait_ge(s_st, TILES // 2 + groups)


def slots(eng, body):
    for k in range(2):
        body(0, k, True)
    with eng.Fori(1, B // 2 - 1) as i:
        for k in range(2):
            body(i, k, True)
    body(B // 2 - 1, 0, True)
    body(B // 2 - 1, 1, False)


def apply_norm(dve, K, xn, b):
    for q in range(T):
        t = b * T + q
        last = dve.tensor_scalar(xn[:, q, :], K.H[:, bass.ds(t, 1), :].rearrange("p a d -> p (a d)"),
                                 K.mean[:, bass.ds(t, 1)], K.rstd[:, bass.ds(t, 1)], ALU.subtract, ALU.mult)
    return last


def transpose_row(pe, K, xp, xn):
    for q in range(T):
        for c in range(C):
            last = pe.transpose(xp[:, c, q * P:(q + 1) * P], xn[:, q, c * P:(c + 1) * P], K.ident[:])
    return last


def project_qkv(nc, K, q_dram, k_dram, v_dram):
    with ExitStack() as ctx:
        ph = Phase(nc, ctx, "qkv")
        w_sb, bq_sb, bk_sb, bv_sb = K.wqkv, K.bq, K.bk, K.bv
        bqs = ph.sb("bqs", [P, C])
        xn = [ph.sb(f"xn{k}", [P, T, D]) for k in range(2)]
        xt = [ph.sb(f"xt{k}", [P, C, S]) for k in range(2)]
        full = {n: [ph.sb(f"full{n}{k}", [P, C * S]) for k in range(2)] for n in "qkv"}
        rest = {n: [ph.sb(f"rest{n}{k}", [P, C * S]) for k in range(2)] for n in "qkv"}
        part = {n: [ph.sb(f"part{n}{k}", [P, 3, C, S], BF16) for k in range(2)] for n in "qk"}
        vpart = [ph.sb(f"partv{k}", [P, PAIRS, T, 2 * VW], BF16) for k in range(2)]
        xp = ph.ps("xp", [P, C, S])
        ps = {n: ph.ps(f"ps{n}", [P, C * S]) for n in "qkv"}
        s_ones, s_bq, s_xn, s_T, s_xt = (ph.sem(n) for n in ("ones", "bq", "xn", "T", "xt"))
        s_ch, s_var, s_rstd = (ph.sem(n) for n in ("ch", "var", "rstd"))
        s_mm, s_full, s_hi, s_rest, s_mid, s_lo = ({n: ph.sem(f"{m}{n}") for n in "qkv"}
                                                  for m in ("mm", "full", "hi", "rest", "mid", "lo"))
        s_out = [ph.sem(f"out{k}") for k in range(2)]
        NOUT = 16 * (2 * 3 + 1)
        block = ctx.enter_context(nc.Block())

        def vcols(tile, q, part):
            return tile[:, :, q, :].rearrange("p h (e w) -> p h e w", e=2)[:, :, :, part * DH:(part + 1) * DH]

        def vfull(tile, q):
            return tile[:, q * D:(q + 1) * D].rearrange("p (h e d) -> p h e d", e=2, d=DH)

        @block.sync
        def _(sp):
            def body(i, k, more):
                b = 2 * i + k
                for n, dram in (("q", q_dram), ("k", k_dram)):
                    sp.wait_ge(s_lo[n], b + 1)
                    for j in range(3):
                        sp.dma_start(dram[bass.ds(b, 1), j].rearrange("a (c p) s -> p (a c) s", p=P),
                                     part[n][k][:, j, :, :]).then_inc(s_out[k], 16)
                sp.wait_ge(s_lo["v"], b + 1)
                sp.dma_start(v_dram[:, bass.ds(b, 1)].rearrange("h a p w -> p (a h) w"),
                             vpart[k][:].rearrange("p h q w -> p h (q w)")).then_inc(s_out[k], 16)

            slots(sp, body)
            for k in range(2):
                sp.wait_ge(s_out[k], NOUT * (B // 2))

        @block.tensor
        def _(pe):
            def turn(b, k):
                pe.wait_ge(s_xn, b + 1)
                pe.wait_ge(s_xt, b)
                transpose_row(pe, K, xp, xn[k]).then_inc(s_T, 1)

            def body(i, k, more):
                b = 2 * i + k
                if more:
                    turn(b + 1, 1 - k)
                pe.wait_ge(s_xt, b + 1)
                for n in "qk":
                    pe.wait_ge(s_full[n], b)
                    for m in range(C):
                        for c in range(C):
                            last = pe.matmul(ps[n][:, m * S:(m + 1) * S], w_sb[n][:, c, m * P:(m + 1) * P], xt[k][:, c, :],
                                             start=(c == 0), stop=(c == C - 1))
                    last.then_inc(s_mm[n], 1)
                pe.wait_ge(s_full["v"], b)
                for q in range(T):
                    for c in range(C):
                        last = pe.matmul(ps["v"][:, q * D:(q + 1) * D], xt[k][:, c, q * P:(q + 1) * P], w_sb["v"][:, c, :],
                                         start=(c == 0), stop=(c == C - 1))
                last.then_inc(s_mm["v"], 1)

            turn(0, 0)
            pe.wait_ge(K.s_par, K.parameters)
            slots(pe, body)

        @block.scalar
        def _(act):
            def middle(b, k):
                for n in "qk":
                    act.wait_ge(s_rest[n], b + 1)
                    act.activation(part[n][k][:, 1].rearrange("p c s -> p (c s)"), rest[n][k][:], ACT.Copy).then_inc(s_mid[n], 1)
                act.wait_ge(s_rest["v"], b + 1)
                for q in range(T):
                    last = act.activation(vcols(vpart[k], q, 1), vfull(rest["v"][k], q), ACT.Copy)
                last.then_inc(s_mid["v"], 1)

            def body(i, k, more):
                b = 2 * i + k
                if more:
                    act.wait_ge(s_T, b + 2)
                    act.wait_ge(s_mm["v"], b)
                    act.activation(xt[1 - k][:], xp[:], ACT.Copy).then_inc(s_xt, 1)
                act.wait_ge(s_out[k], NOUT * i)
                for n in "qk":
                    act.wait_ge(s_full[n], b + 1)
                    act.activation(part[n][k][:, 0].rearrange("p c s -> p (c s)"), full[n][k][:], ACT.Copy).then_inc(s_hi[n], 1)
                act.wait_ge(s_full["v"], b + 1)
                for q in range(T):
                    last = act.activation(vcols(vpart[k], q, 0), vfull(full["v"][k], q), ACT.Copy)
                last.then_inc(s_hi["v"], 1)
                if not (isinstance(b, int) and b == 0):
                    middle(b - 1, 1 - k)
                if not more:
                    middle(b, k)

            act.wait_ge(s_T, 1)
            act.activation(xt[0][:], xp[:], ACT.Copy).then_inc(s_xt, 1)
            act.wait_ge(s_ones, 2)
            slots(act, body)

        @block.gpsimd
        def _(pool):
            pool.wait_ge(s_var, 1)
            rstd_groups(pool, K, s_rstd)
            for k in range(2):
                pool.memset(vpart[k][:], 1.0).then_inc(s_ones, 1)

            def body(i, k, more):
                b = 2 * i + k
                for n in "qk":
                    pool.wait_ge(s_hi[n], b + 1)
                    if not (isinstance(b, int) and b < 2):
                        pool.wait_ge(s_lo[n], b - 1)
                    pool.tensor_tensor(rest[n][k][:], full[n][k][:], part[n][k][:, 0].rearrange("p c s -> p (c s)"), ALU.subtract)\
                        .then_inc(s_rest[n], 1)
                pool.wait_ge(s_hi["v"], b + 1)
                if not (isinstance(b, int) and b < 2):
                    pool.wait_ge(s_lo["v"], b - 1)
                for q in range(T):
                    last = pool.tensor_tensor(vfull(rest["v"][k], q), vfull(full["v"][k], q), vcols(vpart[k], q, 0), ALU.subtract)
                last.then_inc(s_rest["v"], 1)

            slots(pool, body)

        @block.vector
        def _(dve):
            rstd_from_stats(dve, None, K, (s_var, s_rstd, s_ch))
            dve.wait_ge(s_rstd, 1)
            dve.wait_ge(K.s_par, K.parameters)
            dve.tensor_scalar(bqs[:], bq_sb[:], SCALE, None, ALU.mult).then_inc(s_bq, 1)
            for k in range(2):
                apply_norm(dve, K, xn[k], k).then_inc(s_xn, 1)
            dve.wait_ge(s_bq, 1)

            def last_part(b, k):
                for n in "qk":
                    dve.wait_ge(s_mid[n], b + 1)
                    dve.tensor_tensor(part[n][k][:, 2].rearrange("p c s -> p (c s)"), rest[n][k][:],
                                      part[n][k][:, 1].rearrange("p c s -> p (c s)"), ALU.subtract).then_inc(s_lo[n], 1)
                dve.wait_ge(s_mid["v"], b + 1)
                for q in range(T):
                    last = dve.tensor_tensor(vcols(vpart[k], q, 2), vfull(rest["v"][k], q), vcols(vpart[k], q, 1), ALU.subtract)
                last.then_inc(s_lo["v"], 1)

            def body(i, k, more):
                b = 2 * i + k
                if more and not (isinstance(b, int) and b == B - 2):
                    dve.wait_ge(s_T, b + 1)
                    dve.wait_ge(s_rstd, i + 2)
                    apply_norm(dve, K, xn[k], b + 2).then_inc(s_xn, 1)
                for n in "qk":
                    dve.wait_ge(s_mm[n], b + 1)
                    if not (isinstance(b, int) and b < 2):
                        dve.wait_ge(s_rest[n], b - 1)
                    for m in range(C):
                        cols = slice(m * S, (m + 1) * S)
                        if n == "q":
                            last = dve.tensor_scalar(full[n][k][:, cols], ps[n][:, cols], SCALE, bqs[:, m:m + 1], ALU.mult, ALU.add)
                        else:
                            last = dve.tensor_scalar(full[n][k][:, cols], ps[n][:, cols], bk_sb[:, m:m + 1], None, ALU.add)
                    last.then_inc(s_full[n], 1)
                dve.wait_ge(s_mm["v"], b + 1)
                if not (isinstance(b, int) and b < 2):
                    dve.wait_ge(s_rest["v"], b - 1)
                dve.tensor_tensor(full["v"][k][:].rearrange("p (q d) -> p q d", d=D), ps["v"][:].rearrange("p (q d) -> p q d", d=D),
                                  bv_sb[:].rearrange("p (a d) -> p a d", a=1).to_broadcast([P, T, D]), ALU.add)\
                   .then_inc(s_full["v"], 1)
                if not (isinstance(b, int) and b == 0):
                    last_part(b - 1, 1 - k)
                if not more:
                    last_part(b, k)

            slots(dve, body)


def attention(nc, K, pos_bias, q_dram, k_dram, v_dram, heads_dram, experts_f32, experts_parts):
    BODY = 8
    PER_HP = B * 4 // BODY
    UNITS = PAIRS * B * 4
    WHOLE = (1, 3, 5, 7)
    SPLIT = BODY - len(WHOLE)
    NQK = 16 * 4 * len(RUNS)
    EXP_LAG, T_LAG, HI_LAG, LO_LAG, PV_LAG, NORM_LAG = 1, 2, 2, 3, 4, 5
    with ExitStack() as ctx:
        ph = Phase(nc, ctx, "att")
        qs = [ph.sb(f"qs{k}", [STACK, 2, S], BF16) for k in range(2)]
        ks = [ph.sb(f"ks{k}", [STACK, 2, S], BF16) for k in range(2)]
        vs = [ph.sb(f"vs{k}", [P, T, 2 * VW], BF16) for k in range(2)]
        bias, s_bias = K.bias, K.s_bias
        score = [ph.sb(f"score{k}", [P, 2, S]) for k in range(4)]
        top = [ph.sb(f"top{k}", [P, 2]) for k in range(4)]
        shift = [ph.sb(f"shift{k}", [P, 2]) for k in range(4)]
        prob = [ph.sb(f"prob{k}", [P, 2, S]) for k in range(2)]
        hi = [ph.sb(f"hi{k}", [P, 2, T, P], F16) for k in range(2)]
        lo = [ph.sb(f"lo{k}", [P, 2, T, P], F16) for k in range(2)]
        whole = ph.sb("whole", [P, 2, T, P])
        vsum = ph.sb("vsum", [P, T * 2, DH])
        vf = [ph.sb(f"vf{k}", [P, T, 2 * VW]) for k in range(2)]
        osum = [ph.sb(f"osum{k}", [P, 2, T, DH]) for k in range(2)]
        rec = [ph.sb(f"rec{k}", [P, 2, T]) for k in range(2)]
        heads = [ph.sb(f"heads{k}", [P, T, 2, DH]) for k in range(2)]
        ps_s = [ph.ps(f"s{j}", [P, S]) for j in range(2)]
        ps_t = [ph.ps(f"t{k}", [P, 2, T, P]) for k in range(2)]
        ps_o = [ph.ps(f"o{k}", [P, 512]) for k in range(2)]
        s_qk, s_top, s_shift, s_exp, s_turn, s_hi, s_lo, s_pv, s_norm, s_part = (
            ph.sem(n) for n in ("qk", "top", "shift", "exp", "turn", "hi", "lo", "pv", "norm", "part"))
        s_vone, s_vsum, s_vf = (ph.sem(n) for n in ("vone", "vsum", "vf"))
        slab = ph.sb("slab", [P, SLAB])
        slab_parts = ph.sb("slabparts", [P, 2, SLAB], F16)
        s_slab, s_slabhi, s_slablo, s_slabout = (ph.sem(n) for n in ("slab", "slabhi", "slablo", "slabout"))
        s_ldqk = [ph.sem(f"ldqk{k}") for k in range(2)]
        s_ldv = [ph.sem(f"ldv{k}") for k in range(2)]
        s_store = [ph.sem(f"store{k}") for k in range(2)]
        block = ctx.enter_context(nc.Block())

        def wait(eng, sem, value):
            if not (isinstance(value, int) and value <= 0):
                eng.wait_ge(sem, value)

        def flat(eng, steps):
            for j in range(BODY):
                steps(0, j)
            with eng.Fori(1, UNITS // BODY) as m:
                for j in range(BODY):
                    steps(m, j)
            for j in range(BODY):
                steps(UNITS // BODY, j)

        def wait_parts(eng, m, j):
            m, j = m + j // BODY, j % BODY
            if isinstance(m, int) and m < 0:
                return
            if j in WHOLE:
                eng.wait_ge(s_hi, m * BODY + j + 1)
            else:
                eng.wait_ge(s_lo, m * SPLIT + sum(n not in WHOLE for n in range(j + 1)))

        def live(m, j, lag):
            return not (isinstance(m, int) and not 0 <= m * BODY + j - lag < UNITS)

        @block.sync
        def _(sp):
            def load_bias(hp, k):
                sp.dma_start(bias[k][:], bias_rows(pos_bias, hp)).then_inc(s_bias[k], 16)

            def load_pair(hp, b, n, k):
                wait(sp, s_qk, 8 * (n - 1))
                for part, (first, last) in enumerate(RUNS):
                    n_blk, to = last - first, slice(first * DH, last * DH)
                    for e in range(2):
                        head = bass.ds(hp * 2 * DH + e * DH, DH)
                        sp.dma_start(qs[k][to, e, :], q_dram[bass.ds(b, 1), 0:n_blk, head, :].rearrange("a c d s -> (a c) d s"))\
                            .then_inc(s_ldqk[k], 16)
                        sp.dma_start(ks[k][to, e, :], k_dram[bass.ds(b, 1), part:part + 1, head, :]
                                     .rearrange("a c d s -> (a c) d s").to_broadcast([n_blk, DH, S])).then_inc(s_ldqk[k], 16)
                wait(sp, s_pv, 4 * (n - 1))
                wait(sp, s_vf, n - 1)
                sp.dma_start(vs[k][:].rearrange("p q w -> p (q w)"),
                             v_dram[bass.ds(hp, 1), bass.ds(b, 1)].rearrange("h a p w -> (h a p) w"))\
                    .then_inc(s_ldv[k], 16)

            def rows(hp, next_bias=None):
                for k in range(2):
                    load_pair(hp, k, hp * B + k, k)
                if next_bias is not None:
                    sp.wait_ge(s_top, hp * (2 * 4 * B))
                    load_bias(hp + 1, next_bias)
                with sp.Fori(1, B // 2) as i:
                    for k in range(2):
                        load_pair(hp, 2 * i + k, hp * B + 2 * i + k, k)

            rows(0)
            rows(1, 0)
            with sp.Fori(1, PAIRS // 2 - 1) as i:
                for k in range(2):
                    rows(2 * i + k, 1 - k)
            rows(PAIRS - 2, 1)
            rows(PAIRS - 1)

        @block.gpsimd
        def _(pool):
            def store(hp, b, n, k):
                pool.wait_ge(s_norm, n + 1)
                pool.dma_start(heads_dram[bass.ds(b, 1), :, :, bass.ds(hp * 2 * DH, 2 * DH)].rearrange("a q p w -> p (a q) w"),
                               heads[k][:].rearrange("p q e d -> p q (e d)")).then_inc(s_store[k], 16)

            def whole_v(i, k):
                n = 2 * i + k
                pool.wait_ge(s_ldv[k], 16 * i + 16)
                wait(pool, s_pv, 4 * (n - 1))
                wait(pool, s_vf, n)
                v = vs[k][:].rearrange("p q (e w) -> p (q e) w", w=VW)
                pool.tensor_tensor(vsum[:], v[:, :, 0:DH], v[:, :, DH:2 * DH], ALU.add).then_inc(s_vsum, 1)
                pool.wait_ge(s_vsum, n + 1)
                pool.tensor_tensor(vf[k][:].rearrange("p q (e w) -> p (q e) w", w=VW)[:, :, 0:DH], vsum[:], v[:, :, 2 * DH:3 * DH],
                                   ALU.add).then_inc(s_vf, 1)

            for k in range(2):
                pool.memset(vf[k][:], 0.0).then_inc(s_vone, 1)
            pool.wait_ge(s_vone, 2)
            for k in range(2):
                pool.memset(vf[k][:].rearrange("p q (e w) -> p (q e) w", w=VW)[:, :, 3 * DH:VW], 1.0).then_inc(s_vone, 1)
            pool.wait_ge(s_vone, 4)
            for k in range(2):
                whole_v(0, k)
            def load_slab(s):
                pool.dma_start(slab[:], experts_f32[bass.ds(s, 1)].rearrange("a p w -> (a p) w")).then_inc(s_slab, 16)

            def split_slab(s, k, more):
                if k == 0:
                    pool.wait_ge(s_slab, 16 * s + 16)
                    if not (isinstance(s, int) and s == 0):
                        pool.wait_ge(s_slabout, 16 * s)
                    pool.nop(nofuse=True)
                    pool.dma_start(slab_parts[:, 0, :], slab[:]).then_inc(s_slabhi, 16)
                else:
                    pool.wait_ge(s_slabhi, 16 * s + 16)
                    pool.tensor_tensor(slab_parts[:, 1, :], slab[:], slab_parts[:, 0, :], ALU.subtract).then_inc(s_slablo, 1)
                    pool.wait_ge(s_slablo, s + 1)
                    pool.dma_start(experts_parts[bass.ds(s, 1)].rearrange("a p w -> (a p) w"),
                                   slab_parts[:].rearrange("p c w -> p (c w)")).then_inc(s_slabout, 16)
                    if more:
                        load_slab(s + 1)

            PER = B // 2

            def pairs(hp, i, split=True, more=True, end=False):
                for k in range(2):
                    store(hp, 2 * i + k, hp * B + 2 * i + k, k)
                    if not end:
                        whole_v(hp * PER + i + 1, k)
                    if split:
                        split_slab(hp * PER + i, k, more)

            load_slab(0)
            pairs(0, 0)
            with pool.Fori(1, PER) as i:
                pairs(0, i)
            with pool.Fori(1, SLABS // PER - 1) as hp:
                with pool.Fori(0, PER) as i:
                    pairs(hp, i)
            last = SLABS // PER - 1
            with pool.Fori(0, PER - 1) as i:
                pairs(last, i)
            pairs(last, PER - 1, more=False)
            with pool.Fori(last + 1, PAIRS - 1) as hp:
                with pool.Fori(0, PER) as i:
                    pairs(hp, i, split=False)
            with pool.Fori(0, PER - 1) as i:
                pairs(PAIRS - 1, i, split=False)
            pairs(PAIRS - 1, PER - 1, split=False, end=True)
            pool.wait_ge(s_slabout, 16 * SLABS)
            for k in range(2):
                pool.wait_ge(s_store[k], 16 * (PAIRS * B // 2))

        @block.tensor
        def _(pe):
            def steps(m, j):
                if live(m, j, 0):
                    e, half, k = j // 2 % 2, j % 2, j // 4
                    if j % 4 == 0:
                        pe.wait_ge(s_ldqk[k], NQK * m + NQK)
                    for t in range(2):
                        tile = 2 * (m * BODY + j) + t
                        wait(pe, s_top, tile - 1)
                        q = 2 * half + t
                        pe.matmul(ps_s[t][:], qs[k][:, e, q * P:(q + 1) * P], ks[k][:, e, :], start=True, stop=True)\
                            .then_inc(s_qk, 1)
                if live(m, j, PV_LAG):
                    jj = (j - PV_LAG) % BODY
                    u = m * BODY + j - PV_LAG
                    e, half, k, sl = jj // 2 % 2, jj % 2, jj // 4, jj % 2
                    if jj % 4 == 0:
                        n = 2 * m + (j - PV_LAG) // 4
                        pe.wait_ge(s_ldv[k], 16 * (m + (j - PV_LAG) // BODY) + 16)
                        pe.wait_ge(s_vf, n + 1)
                        wait(pe, s_norm, n - 1)
                    wait_parts(pe, m, j - PV_LAG)
                    factors = ((whole, vf),) if jj in WHOLE else ((hi[sl], vs), (lo[sl], vs))
                    for t in range(2):
                        o = (e * T + 2 * half + t) * VW
                        for kt in range(T):
                            for f, (part, v) in enumerate(factors):
                                last = pe.matmul(ps_o[k][:, o:o + VW], part[:, t, kt, :], v[k][:, kt, e * VW:(e + 1) * VW],
                                                 start=(kt == 0 and f == 0), stop=(kt == T - 1 and f == len(factors) - 1))
                    last.then_inc(s_pv, 1)
                if live(m, j, T_LAG):
                    u = m * BODY + j - T_LAG
                    sl = (j - T_LAG) % 2
                    pe.wait_ge(s_exp, u + 1)
                    wait_parts(pe, m, j - T_LAG - 2)
                    for t in range(2):
                        for kt in range(T):
                            last = pe.transpose(ps_t[sl][:, t, kt, :], prob[sl][:, t, kt * P:(kt + 1) * P], K.ident[:])
                    last.then_inc(s_turn, 1)

            flat(pe, steps)

        @block.scalar
        def _(act):
            def steps(m, j):
                if live(m, j, EXP_LAG):
                    u, jj = m * BODY + j - EXP_LAG, (j - EXP_LAG) % BODY
                    act.wait_ge(s_shift, u + 1)
                    wait(act, s_turn, u - 1)
                    for t in range(2):
                        last = act.activation(prob[jj % 2][:, t, :], score[jj % 4][:, t, :], ACT.Exp, bias=shift[jj % 4][:, t:t + 1])
                    last.then_inc(s_exp, 1)
                if live(m, j, HI_LAG):
                    u, jj = m * BODY + j - HI_LAG, (j - HI_LAG) % BODY
                    act.wait_ge(s_turn, u + 1)
                    wait(act, s_pv, u - 1)
                    act.activation(whole[:] if jj in WHOLE else hi[jj % 2][:], ps_t[jj % 2][:], ACT.Copy).then_inc(s_hi, 1)

            flat(act, steps)

        @block.vector
        def _(dve):
            def steps(m, j, bk):
                if live(m, j, 0):
                    e, half, r = j // 2 % 2, j % 2, j % 4
                    u = m * BODY + j
                    wait(dve, s_exp, u - 3)
                    for t in range(2):
                        dve.wait_ge(s_qk, 2 * u + t + 1)
                        dve.nop(nofuse=True)
                        off = (2 * half + t) * P
                        dve.tensor_tensor_reduce(score[r][:, t, :], ps_s[t][:], bias[bk][:, e, off:off + S][:, ::-1], 1.0, -3.0e38,
                                                 ALU.add, ALU.max, top[r][:, t:t + 1]).then_inc(s_top, 1)
                    dve.wait_ge(s_top, 2 * u + 2)
                    dve.tensor_scalar(shift[r][:], top[r][:], -1.0, LIFT, ALU.mult, ALU.add).then_inc(s_shift, 1)
                if live(m, j, LO_LAG) and (j - LO_LAG) % BODY not in WHOLE:
                    u, sl = m * BODY + j - LO_LAG, (j - LO_LAG) % 2
                    dve.wait_ge(s_hi, u + 1)
                    wait(dve, s_pv, u - 1)
                    dve.tensor_tensor(lo[sl][:], ps_t[sl][:], hi[sl][:], ALU.subtract).then_inc(s_lo, 1)
                if (j - NORM_LAG) % 4 == 3 and live(m, j, NORM_LAG):
                    k = (j - NORM_LAG) % BODY // 4
                    n = 2 * m + (j - NORM_LAG) // 4
                    dve.wait_ge(s_pv, m * BODY + j - NORM_LAG + 1)
                    wait(dve, s_store[k], 16 * (m + (j - NORM_LAG) // BODY))
                    o = ps_o[k][:, 0:2 * T * VW].rearrange("p (e w) -> p e w", w=VW)
                    dve.tensor_reduce(osum[k][:].rearrange("p e q d -> p (e q) d"),
                                      o[:, :, 0:3 * DH].rearrange("p e (c d) -> p e d c", d=DH), AX.X, ALU.add).then_inc(s_part, 1)
                    dve.reciprocal(rec[k][:].rearrange("p e q -> p (e q)"), o[:, :, 3 * DH]).then_inc(s_part, 1)
                    dve.wait_ge(s_part, 2 * n + 2)
                    dve.tensor_tensor(heads[k][:].rearrange("p q e d -> p e q d"), osum[k][:],
                                      rec[k][:].rearrange("p e (q a) -> p e q a", a=1).to_broadcast([P, 2, T, DH]), ALU.mult)\
                        .then_inc(s_norm, 1)

            def bodies(first, last, bk):
                with dve.Fori(first, last) as m:
                    for j in range(BODY):
                        steps(m, j, bk)

            dve.wait_ge(s_bias[0], 16)
            for j in range(BODY):
                steps(0, j, 0)
            bodies(1, PER_HP, 0)
            dve.wait_ge(s_bias[1], 16)
            bodies(PER_HP, 2 * PER_HP, 1)
            with dve.Fori(1, PAIRS // 2) as h:
                for bk in range(2):
                    dve.wait_ge(s_bias[bk], 16 * h + 16)
                    bodies(h * (2 * PER_HP) + bk * PER_HP, h * (2 * PER_HP) + (bk + 1) * PER_HP, bk)
            for j in range(BODY):
                steps(UNITS // BODY, j, 0)


def attention_output(nc, K, heads_dram):
    with ExitStack() as ctx:
        ph = Phase(nc, ctx, "wo")
        w, bo_sb = K.wo, K.bo
        heads = [ph.sb(f"heads{k}", [P, T, D]) for k in range(2)]
        ht = [ph.sb(f"ht{k}", [P, C, S]) for k in range(2)]
        xp = ph.ps("xp", [P, C, S])
        po = [ph.ps(f"po{k}", [P, T, D]) for k in range(2)]
        s_T, s_ht, s_mm, s_add, s_bias, s_st, s_ch, s_var = (
            ph.sem(n) for n in ("T", "ht", "mm", "add", "bias", "st", "ch", "var"))
        s_in = [ph.sem(f"in{k}") for k in range(2)]
        block = ctx.enter_context(nc.Block())

        @block.sync
        def _(sp):
            def load(b, k):
                sp.dma_start(heads[k][:], heads_dram[bass.ds(b, 1)].rearrange("a q p w -> p (a q) w")).then_inc(s_in[k], 16)

            for k in range(2):
                load(k, k)
            with sp.Fori(1, B // 2) as i:
                for k in range(2):
                    sp.wait_ge(s_T, 2 * i + k - 1)
                    load(2 * i + k, k)

        @block.tensor
        def _(pe):
            def turn(i, b, k):
                pe.wait_ge(s_in[k], 16 * i + 16)
                pe.wait_ge(s_ht, b)
                for q in range(T):
                    for c in range(C):
                        last = pe.transpose(xp[:, c, q * P:(q + 1) * P], heads[k][:, q, c * P:(c + 1) * P], K.ident[:])
                last.then_inc(s_T, 1)

            def body(i, k, more):
                b = 2 * i + k
                if more:
                    turn(i + k, b + 1, 1 - k)
                pe.wait_ge(s_ht, b + 1)
                pe.wait_ge(s_add, b)
                for q in range(T):
                    for c in range(C):
                        last = pe.matmul(po[k][:, q, :], ht[k][:, c, q * P:(q + 1) * P], w[:, c, :], start=(c == 0), stop=(c == C - 1))
                last.then_inc(s_mm, 1)

            turn(0, 0, 0)
            pe.wait_ge(K.s_par, K.parameters)
            slots(pe, body)

        @block.scalar
        def _(act):
            def body(i, k, more):
                b = 2 * i + k
                act.wait_ge(s_T, b + 1)
                if not (isinstance(b, int) and b < 2):
                    act.wait_ge(s_mm, b - 1)
                act.activation(ht[k][:], xp[:], ACT.Copy).then_inc(s_ht, 1)

            slots(act, body)

        @block.vector
        def _(dve):
            dve.wait_ge(K.s_par, K.parameters)

            def body(i, k, more):
                b = 2 * i + k
                rows = K.H[:, bass.ds(b * T, T), :]
                dve.tensor_tensor(rows, rows, bo_sb[:].rearrange("p (a d) -> p a d", a=1).to_broadcast([P, T, D]), ALU.add)\
                   .then_inc(s_bias, 1)
                dve.wait_ge(s_bias, b + 1)
                dve.wait_ge(s_mm, b + 1)
                dve.tensor_tensor(rows, rows, po[k][:], ALU.add).then_inc(s_add, 1)
                dve.wait_ge(s_add, b + 1)
                stats_of_row(dve, K, b).then_inc(s_st, 1)

            slots(dve, body)
            dve.wait_ge(s_st, B)
            rstd_from_stats(dve, None, K, (s_var, None, s_ch))
            dve.wait_ge(s_var, 1)


def stats_of_row(dve, K, b):
    for q in range(T):
        last = dve.bn_stats(K.stats[:, bass.ds(b * T + q, 1), :].rearrange("p a d -> p (a d)"),
                            K.H[:, bass.ds(b * T + q, 1), :].rearrange("p a d -> p (a d)"))
    return last


def inner_ffn(nc, K):
    RING = 4
    SUMS = INNER + 1
    with ExitStack() as ctx:
        ph = Phase(nc, ctx, "ffn")
        win_sb, bin_sb, w1_sb, b1_sb, w2_sb, b2_sb, wout_sb, bout_sb = K.win, K.bin, K.w1, K.b1, K.w2, K.b2, K.wout, K.bout
        xn = [ph.sb(f"xn{k}", [P, T, D]) for k in range(2)]
        xt = [ph.sb(f"xt{k}", [P, C, S]) for k in range(2)]
        sv = ph.sb("s", [P, S])
        unit = [ph.sb(f"unit{r}", [P, S]) for r in range(RING)]
        g, g_odd = ph.sb("g", [P, S]), ph.sb("godd", [P, S])
        xp = ph.ps("xp", [P, C, S])
        ps_s = ph.ps("sp", [P, S])
        po = [ph.ps(f"po{k}", [P, T, D]) for k in range(2)]
        s_xn, s_T, s_xt, s_s, s_sv, s_unit, s_g, s_mm, s_add, s_bias, s_st, s_ch, s_var, s_rstd = (
            ph.sem(n) for n in ("xn", "T", "xt", "s", "sv", "unit", "g", "mm", "add", "bias", "st", "ch", "var", "rstd"))
        block = ctx.enter_context(nc.Block())

        def pairs(eng, body):
            body(0)
            with eng.Fori(1, B // 2 - 2) as i:
                body(i)
            body(B // 2 - 2, ahead=False)
            body(B // 2 - 1, more=False, ahead=False)

        @block.tensor
        def _(pe):
            pe.wait_ge(K.s_par, K.parameters)

            def prepare(i):
                for k in range(2):
                    b = 2 * i + k
                    pe.wait_ge(s_xn, b + 1)
                    pe.wait_ge(s_xt, b)
                    transpose_row(pe, K, xp, xn[k]).then_inc(s_T, 1)
                    pe.wait_ge(s_xt, b + 1)
                    pe.wait_ge(s_sv, i)
                    for c in range(C):
                        last = pe.matmul(ps_s[M * k:M * k + M, :], win_sb[:, c, :], xt[k][:, c, :], start=(c == 0), stop=(c == C - 1))
                    last.then_inc(s_s, 1)

            def body(i, more=True, ahead=True):
                if more:
                    prepare(i + 1)
                pe.wait_ge(s_g, SUMS * i + SUMS)
                pe.wait_ge(s_add, 2 * i)
                for k in range(2):
                    for q in range(T):
                        last = pe.matmul(po[k][:, q, :], g[M * k:M * k + M, q * P:(q + 1) * P], wout_sb[M * k:M * k + M, :],
                                         start=True, stop=True)
                    last.then_inc(s_mm, 1)

            prepare(0)
            pairs(pe, body)

        @block.scalar
        def _(act):
            def copy_x(b, k):
                act.wait_ge(s_T, b + 1)
                act.wait_ge(s_s, b)
                act.activation(xt[k][:], xp[:], ACT.Copy).then_inc(s_xt, 1)

            def body(i, more=True, ahead=True):
                act.wait_ge(s_s, 2 * i + 2)
                act.wait_ge(s_unit, INNER * i)
                act.activation(sv[:], ps_s[:], ACT.Identity, bias=bin_sb[:]).then_inc(s_sv, 1)
                act.wait_ge(s_sv, i + 1)
                for h in range(INNER):
                    if h >= RING:
                        act.wait_ge(s_g, SUMS * i + h - RING + 1)
                    else:
                        act.wait_ge(s_g, SUMS * i)
                    act.activation(unit[h % RING][:], sv[:], ACT.Relu, scale=w1_sb[:, h:h + 1], bias=b1_sb[:, h:h + 1])\
                        .then_inc(s_unit, 1)
                    if more and h in (5, 10):
                        copy_x(2 * i + 2 + h // 10, h // 10)

            act.wait_ge(K.s_par, K.parameters)
            for k in range(2):
                copy_x(k, k)
            pairs(act, body)

        @block.gpsimd
        def _(pool):
            rstd_groups(pool, K, s_rstd)
            pool.wait_ge(K.s_par, K.parameters)

            def add_bias(b):
                rows = K.H[:, bass.ds(b * T, T), :]
                pool.wait_ge(s_xn, b + 1)
                pool.nop(nofuse=True)
                pool.tensor_tensor(rows, rows, bout_sb[:].rearrange("p (a d) -> p a d", a=1).to_broadcast([P, T, D]), ALU.add)\
                    .then_inc(s_bias, 1)

            with pool.Fori(0, B) as b:
                add_bias(b)

        @block.vector
        def _(dve):
            def norm(i, k):
                b = 2 * i + k
                dve.wait_ge(s_rstd, i + 1)
                if not (isinstance(b, int) and b < 2):
                    dve.wait_ge(s_T, b - 1)
                apply_norm(dve, K, xn[k], b).then_inc(s_xn, 1)

            def body(i, more=True, ahead=True):
                for h in range(INNER):
                    dve.wait_ge(s_unit, INNER * i + h + 1)
                    if h == 0:
                        last = dve.tensor_scalar(g[:], unit[0][:], w2_sb[:, 0:1], b2_sb[:], ALU.mult, ALU.add)
                    elif h == 1:
                        last = dve.tensor_scalar(g_odd[:], unit[1][:], w2_sb[:, 1:2], None, ALU.mult)
                    else:
                        total = (g, g_odd)[h % 2]
                        dve.wait_ge(s_g, SUMS * i + h - 1)
                        last = dve.scalar_tensor_tensor(total[:], unit[h % RING][:], w2_sb[:, h:h + 1], total[:], ALU.mult, ALU.add)
                    last.then_inc(s_g, 1)
                    if more and h == 7:
                        norm(i + 1, 1)
                dve.wait_ge(s_g, SUMS * i + INNER)
                dve.tensor_tensor(g[:], g[:], g_odd[:], ALU.add).then_inc(s_g, 1)
                if ahead:
                    norm(i + 2, 0)
                for k in range(2):
                    b = 2 * i + k
                    if not (isinstance(i, int) and i == 0):
                        stats(b - 2)
                    rows = K.H[:, bass.ds(b * T, T), :]
                    dve.wait_ge(s_mm, b + 1)
                    dve.wait_ge(s_bias, b + 1)
                    dve.tensor_tensor(rows, rows, po[k][:], ALU.add).then_inc(s_add, 1)
                if not more:
                    for k in range(2):
                        stats(2 * i + k)

            def stats(b):
                dve.wait_ge(s_add, b + 1)
                stats_of_row(dve, K, b).then_inc(s_st, 1)

            dve.wait_ge(K.s_par, K.parameters)
            for b in range(3):
                norm(b // 2, b % 2)
            pairs(dve, body)
            dve.wait_ge(s_st, B)
            rstd_from_stats(dve, None, K, (s_var, None, s_ch))
            dve.wait_ge(s_var, 1)


def recurrence(nc, K):
    FLOOR = 1e-7
    with ExitStack() as ctx:
        ph = Phase(nc, ctx, "rg")
        gate_in = ph.sb("gatein", [P, B, C, S])
        gate_a = ph.sb("gatea", [P, B, C, S])
        igw, agw, igb, agb, ap = K.igw, K.agw, K.igb, K.agb, K.ap
        z, w, d, l, t1 = (ph.sb(n, [P, C]) for n in ("z", "w", "d", "l", "t1"))
        rate = {n: ph.sb(f"rate{n}", [P, C]) for n in (1, 2, -1)}
        s_ch, s_rate, s_act, s_rstd = (ph.sem(n) for n in ("ch", "rate", "act", "rstd"))
        s_xn, s_T, s_xt, s_g, s_sig, s_xg = (ph.sem(n) for n in ("xn", "T", "xt", "g", "sig", "xg"))
        with ExitStack() as c1:
            p1 = Phase(nc, c1, "rga")
            xn = [p1.sb(f"xn{k}", [P, T, D]) for k in range(2)]
            xt = [p1.sb(f"xt{k}", [P, C, S]) for k in range(2)]
            sig = [p1.sb(f"sig{k}", [P, C, S]) for k in range(2)]
            xp = p1.ps("xp", [P, C, S])
            ps_i = p1.ps("i", [P, C, S])
            ps_a = p1.ps("a", [P, C, S])
            block = c1.enter_context(nc.Block())

            @block.gpsimd
            def _(pool):
                rstd_groups(pool, K, s_rstd)

                def body(i, k, more):
                    b = 2 * i + k
                    pool.wait_ge(s_sig, 2 * b + 1)
                    pool.tensor_tensor(gate_in[:, bass.ds(b, 1)].rearrange("p a c s -> p (a c s)"),
                                       sig[k][:].rearrange("p c s -> p (c s)"), xt[k][:].rearrange("p c s -> p (c s)"), ALU.mult)\
                        .then_inc(s_xg, 1)

                slots(pool, body)

            @block.tensor
            def _(pe):
                def turn(b, k):
                    pe.wait_ge(s_xn, b + 1)
                    pe.wait_ge(s_xt, b)
                    transpose_row(pe, K, xp, xn[k]).then_inc(s_T, 1)

                def body(i, k, more):
                    b = 2 * i + k
                    if more:
                        turn(b + 1, 1 - k)
                    pe.wait_ge(s_xt, b + 1)
                    for n, (ps, gw) in enumerate(((ps_i, igw), (ps_a, agw))):
                        pe.wait_ge(s_sig, 2 * b - 1 + n if not isinstance(b, int) or b else 0)
                        for c in range(C):
                            last = pe.matmul(ps[:, c, :], gw[:, c, :], xt[k][:, c, :], start=True, stop=True)
                        last.then_inc(s_g, 1)

                turn(0, 0)
                pe.wait_ge(K.s_par, K.parameters)
                for k in range(2):
                    body(0, k, True)
                with pe.Fori(1, B // 2 - 1) as i:
                    for k in range(2):
                        body(i, k, True)
                body(B // 2 - 1, 0, True)
                body(B // 2 - 1, 1, False)

            @block.scalar
            def _(act):
                act.wait_ge(K.s_par, K.parameters)
                act.wait_ge(s_ch, 2)
                act.activation(z[:], t1[:], ACT.Exp).then_inc(s_act, 1)
                act.wait_ge(s_ch, 3)
                act.activation(l[:], w[:], ACT.Ln).then_inc(s_act, 1)

                def body(i, k, more):
                    b = 2 * i + k
                    if more:
                        act.wait_ge(s_T, b + 2)
                        act.wait_ge(s_xg, b)
                        act.activation(xt[1 - k][:], xp[:], ACT.Copy).then_inc(s_xt, 1)
                    act.wait_ge(s_g, 2 * b + 1)
                    act.wait_ge(s_xg, b)
                    for c in range(C):
                        last = act.activation(sig[k][:, c, :], ps_i[:, c, :], ACT.Sigmoid, bias=igb[:, c:c + 1])
                    last.then_inc(s_sig, 1)
                    act.wait_ge(s_g, 2 * b + 2)
                    act.nop(nofuse=True)
                    for c in range(C):
                        last = act.activation(gate_a[:, bass.ds(b, 1), c, :].rearrange("p a s -> p (a s)"), ps_a[:, c, :],
                                              ACT.Sigmoid, bias=agb[:, c:c + 1])
                    last.then_inc(s_sig, 1)

                act.wait_ge(s_T, 1)
                act.activation(xt[0][:], xp[:], ACT.Copy).then_inc(s_xt, 1)
                slots(act, body)

            @block.vector
            def _(dve):
                n = 0

                def step(ins):
                    nonlocal n
                    n += 1
                    ins.then_inc(s_ch, 1)
                    dve.wait_ge(s_ch, n)

                dve.wait_ge(s_rstd, 1)
                apply_norm(dve, K, xn[0], 0).then_inc(s_xn, 1)
                dve.wait_ge(K.s_par, K.parameters)
                step(dve.tensor_scalar(t1[:], ap[:], -1.0, None, ALU.mult))
                step(dve.tensor_tensor(t1[:], t1[:], ap[:], ALU.min))
                dve.wait_ge(s_act, 1)
                step(dve.tensor_scalar(w[:], z[:], 1.0, None, ALU.add))
                step(dve.tensor_scalar(d[:], w[:], -1.0, None, ALU.add))
                step(dve.tensor_scalar(t1[:], d[:], 0.0, None, ALU.is_equal))
                step(dve.tensor_tensor(d[:], d[:], t1[:], ALU.add))
                step(dve.reciprocal(d[:], d[:]))
                dve.wait_ge(s_act, 2)
                step(dve.tensor_tensor(l[:], l[:], d[:], ALU.mult))
                step(dve.tensor_tensor(l[:], l[:], t1[:], ALU.add))
                step(dve.tensor_tensor(l[:], l[:], z[:], ALU.mult))
                step(dve.tensor_scalar(ap[:], ap[:], 0.0, None, ALU.max))
                step(dve.tensor_tensor(l[:], l[:], ap[:], ALU.add))
                for m, r in rate.items():
                    dve.tensor_scalar(r[:], l[:], -8.0 * m, None, ALU.mult).then_inc(s_rate, 1)

                def body(i, k, more):
                    b = 2 * i + k
                    if more:
                        dve.wait_ge(s_T, b)
                        dve.wait_ge(s_rstd, i + k + 1)
                        apply_norm(dve, K, xn[1 - k], b + 1).then_inc(s_xn, 1)

                slots(dve, body)
                dve.wait_ge(s_rate, 3)

        with ExitStack() as c2:
            p2 = Phase(nc, c2, "rgb")
            a = [p2.sb(f"a{k}", [P, C, S]) for k in range(2)]
            ai = [p2.sb(f"ai{k}", [P, C, S]) for k in range(2)]
            q = [p2.sb(f"q{k}", [P, C, S]) for k in range(2)]
            ratio = p2.sb("ratio", [P, B, C, S])
            h = [p2.sb(f"h{k}", [P, C, S]) for k in range(2)]
            cap = p2.sb("cap", [P, S])
            pt = [p2.ps(f"t{k}", [P, T, D]) for k in range(2)]
            s_a, s_ai, s_a2, s_q, s_r, s_om, s_root, s_x, s_h, s_turn, s_add, s_st, s_cap, s_c2, s_var = (
                p2.sem(n) for n in ("a", "ai", "a2", "q", "r", "om", "root", "x", "h", "turn", "add", "st", "cap", "c2", "var"))
            block = c2.enter_context(nc.Block())

            def row(t, b):
                return t[:, bass.ds(b, 1)].rearrange("p a c s -> p (a c) s")

            @block.scalar
            def _(act):
                def body(i, k, more):
                    b = 2 * i + k
                    if not (isinstance(b, int) and b < 2):
                        act.wait_ge(s_r, b - 1)
                        act.nop(nofuse=True)
                    for c in range(C):
                        last = act.activation(a[k][:, c, :], row(gate_a, b)[:, c, :], ACT.Exp, scale=rate[1][:, c:c + 1])
                    last.then_inc(s_a, 1)
                    for c in range(C):
                        last = act.activation(ai[k][:, c, :], row(gate_a, b)[:, c, :], ACT.Exp, scale=rate[-1][:, c:c + 1])
                    last.then_inc(s_ai, 1)
                    act.wait_ge(s_ai, b + 1)
                    act.nop(nofuse=True)
                    for c in range(C):
                        last = act.activation(row(gate_a, b)[:, c, :], row(gate_a, b)[:, c, :], ACT.Exp, scale=rate[2][:, c:c + 1])
                    last.then_inc(s_a2, 1)

                slots(act, body)
                for b in range(B):
                    act.wait_ge(s_om, b + 1)
                    act.activation(gate_a[:, b], gate_a[:, b], ACT.Sqrt).then_inc(s_root, 1)

            @block.gpsimd
            def _(pool):
                with pool.Fori(0, B) as b:
                    pool.wait_ge(s_root, b + 1)
                    x = gate_in[:, bass.ds(b, 1)].rearrange("p a c s -> p (a c s)")
                    pool.tensor_tensor(x, x, gate_a[:, bass.ds(b, 1)].rearrange("p a c s -> p (a c s)"), ALU.mult).then_inc(s_x, 1)

            @block.tensor
            def _(pe):
                def body(i, k, more):
                    b = 2 * i + k
                    pe.wait_ge(s_h, b + 1)
                    if not (isinstance(b, int) and b < 2):
                        pe.wait_ge(s_add, b - 1)
                    for t in range(T):
                        for c in range(C):
                            last = pe.transpose(pt[k][:, t, c * P:(c + 1) * P], h[k][:, c, t * P:(t + 1) * P], K.ident[:])
                    last.then_inc(s_turn, 1)

                slots(pe, body)

            @block.vector
            def _(dve):
                dve.memset(cap[:], 1.0 / FLOOR).then_inc(s_cap, 1)
                for k in range(2):
                    dve.memset(q[k][:, :, 0:1], 1.0).then_inc(s_cap, 1)
                dve.memset(ratio[:, :, :, 0:1], 0.0).then_inc(s_cap, 1)
                dve.wait_ge(s_cap, 4)

                def body(i, k, more):
                    b = 2 * i + k
                    dve.wait_ge(s_ai, b + 1)
                    for c in range(C):
                        last = dve.tensor_tensor_scan(q[k][:, c, 1:S], ai[k][:, c, 0:S - 1], cap[:, 0:S - 1], 1.0, ALU.mult, ALU.min)
                    last.then_inc(s_q, 1)
                    dve.wait_ge(s_q, b + 1)
                    dve.wait_ge(s_a, b + 1)
                    dve.scalar_tensor_tensor(row(ratio, b)[:, :, 1:S], q[k][:, :, 0:S - 1], FLOOR, a[k][:, :, 0:S - 1], ALU.mult, ALU.max)\
                       .then_inc(s_r, 1)
                    dve.wait_ge(s_a2, b + 1)
                    dve.tensor_scalar(row(gate_a, b), row(gate_a, b), -1.0, 1.0, ALU.mult, ALU.add).then_inc(s_c2, 1)
                    dve.wait_ge(s_c2, b + 1)
                    dve.tensor_scalar(row(gate_a, b), row(gate_a, b), FLOOR, None, ALU.max).then_inc(s_om, 1)

                slots(dve, body)

                def scan(b, k):
                    dve.wait_ge(s_x, b + 1)
                    if not (isinstance(b, int) and b < 2):
                        dve.wait_ge(s_turn, b - 1)
                    for c in range(C):
                        last = dve.tensor_tensor_scan(h[k][:, c, :], row(ratio, b)[:, c, :], row(gate_in, b)[:, c, :], 0.0,
                                                      ALU.mult, ALU.add)
                    last.then_inc(s_h, 1)

                def add(i, k, more):
                    b = 2 * i + k
                    if more:
                        scan(b + 1, 1 - k)
                    dve.wait_ge(s_turn, b + 1)
                    rows = K.H[:, bass.ds(b * T, T), :]
                    dve.tensor_tensor(rows, rows, pt[k][:], ALU.add).then_inc(s_add, 1)
                    dve.wait_ge(s_add, b + 1)
                    stats_of_row(dve, K, b).then_inc(s_st, 1)

                scan(0, 0)
                slots(dve, add)
                dve.wait_ge(s_st, B)
                rstd_from_stats(dve, None, K, (s_var, None, s_c2), B)
                dve.wait_ge(s_var, 1)


def route(nc, K, h_dram, xn_dram):
    BATCH = 16
    E = EXPERTS
    with ExitStack() as ctx:
        ph = Phase(nc, ctx, "route")
        gw, gb = K.gw, K.gb
        xa = ph.sb("xa", [P, TILES, D])
        xt = [ph.sb(f"xt{k}", [P, C, S]) for k in range(2)]
        name_i, name = ph.sb("namei", [P, 2 * TILES], I32), ph.sb("name", [P, 2 * TILES])
        lane_i, lane = ph.sb("lanei", [P, P], I32), ph.sb("lane", [P, P])
        row_i, row = ph.sb("rowi", [P, 1], I32), ph.sb("row", [P, 1])
        rank_i, rank = ph.sb("ranki", [P, E], I32), ph.sb("rank", [P, E])
        start_i, start = ph.sb("starti", [P, SLOTS], I32), ph.sb("start", [P, SLOTS])
        before, ones = ph.sb("before", [P, P]), ph.sb("ones", [P, P])
        pr, eq, tot, inc, slot, hit = (ph.sb(n, [P, TILES, E]) for n in ("pr", "eq", "tot", "inc", "slot", "hit"))
        pick = [ph.sb(f"pick{j}", [P, TILES, E]) for j in range(2)]
        best = [ph.sb(f"best{j}", [P, TILES]) for j in range(2)]
        col = ph.sb("col", [P, TILES])
        pos, low, high = (ph.sb(n, [P, 2 * TILES]) for n in ("pos", "low", "high"))
        pos_i = ph.sb("posi", [P, 2 * TILES], I32)
        in_lane = [ph.sb(f"inlane{j}", [P, BATCH, P]) for j in range(2)]
        in_tile = [ph.sb(f"intile{j}", [P, BATCH, SLOTS]) for j in range(2)]
        named, unused = ph.sb("named", [P, SLOTS]), ph.sb("unused", [P, SLOTS])
        token_i = ph.sb("tokeni", [P, SLOTS], I32)
        size, end, base = ph.sb("size", [P, E]), ph.sb("end", [P, E]), ph.sb("base", [P, E])
        size_i = ph.sb("sizei", [P, E], I32)
        ge = ph.sb("ge", [1, SLOTS, E])
        owner = ph.sb("owner", [1, SLOTS])
        xp = ph.ps("xp", [P, C, S])
        lt = [ph.sb(f"lt{k}", [E, S]) for k in range(2)]
        ps_l = [ph.ps(f"l{k}", [E, S]) for k in range(2)]
        ps_g = [ph.ps(f"g{k}", [P, 4 * T, E]) for k in range(2)]
        ps_b, ps_n = ph.ps("b", [P, TILES, E]), ph.ps("n", [P, TILES, E])
        ps_v = ps_g[0][:].rearrange("p t e -> p (t e)")[:, 0:SLOTS]
        s_const, s_made, s_xn, s_T, s_xt, s_g, s_lg, s_ch, s_sub, s_exp, s_pick, s_cnt, s_l, s_lt, s_factor, s_used, s_h, s_rstd = (
            ph.sem(n) for n in ("const", "made", "xn", "T", "xt", "g", "lg", "ch", "sub", "exp", "pick", "cnt", "l", "lt",
                                "factor", "used", "h", "rstd"))
        block = ctx.enter_context(nc.Block())

        @block.sync
        def _(sp):
            sp.dma_start(h_dram.rearrange("(t p) d -> p t d", p=P), K.H[:]).then_inc(s_h, 16)
            sp.wait_ge(s_xn, B)
            sp.dma_start(xn_dram.rearrange("(t p) d -> p t d", p=P), xa[:]).then_inc(s_h, 16)
            sp.wait_ge(s_h, 32)

        @block.gpsimd
        def _(pool):
            rstd_groups(pool, K, s_rstd)
            pool.iota(name_i[:], [[TOKENS, 2], [P, TILES]], base=1, channel_multiplier=1).then_inc(s_const, 1)
            pool.iota(lane_i[:], [[1, P]], base=0, channel_multiplier=0).then_inc(s_const, 1)
            pool.iota(row_i[:], [[0, 1]], base=2 * TOKENS + 1, channel_multiplier=1).then_inc(s_const, 1)
            pool.memset(K.source[:], 0).then_inc(s_const, 1)
            pool.iota(rank_i[:], [[-1, E]], base=E, channel_multiplier=0).then_inc(s_const, 1)
            pool.iota(start_i[:], [[P, SLOTS]], base=0, channel_multiplier=0).then_inc(s_const, 1)
            pool.memset(ones[:], 1.0).then_inc(s_const, 1)
            pool.wait_ge(s_const, 7)
            pool.affine_select(out=before[:], in_=ones[:], compare_op=ALU.is_gt, fill=0.0, base=0,
                               pattern=[[1, P]], channel_multiplier=-1).then_inc(s_const, 1)

        @block.tensor
        def _(pe):
            def turn(b):
                pe.wait_ge(s_xn, b + 1)
                pe.wait_ge(s_xt, b)
                for q in range(T):
                    for c in range(C):
                        last = pe.transpose(xp[:, c, q * P:(q + 1) * P], xa[:, b * T + q, c * P:(c + 1) * P], K.ident[:])
                last.then_inc(s_T, 1)

            def turn_logits(b):
                pe.wait_ge(s_lt, b + 1)
                if b >= 2:
                    pe.wait_ge(s_lg, b - 1)
                for q in range(T):
                    last = pe.transpose(ps_g[b % 2][:, q, :], lt[b % 2][:, q * P:(q + 1) * P], K.ident[0:E, 0:E])
                last.then_inc(s_g, 1)

            turn(0)
            for b in range(B):
                if b + 1 < B:
                    turn(b + 1)
                pe.wait_ge(s_xt, b + 1)
                if b >= 2:
                    pe.wait_ge(s_lt, b - 1)
                for c in range(C):
                    last = pe.matmul(ps_l[b % 2][:], gw[:, c, :], xt[b % 2][:, c, :], start=(c == 0), stop=(c == C - 1))
                last.then_inc(s_l, 1)
                if b >= 1:
                    turn_logits(b - 1)
            turn_logits(B - 1)
            pe.wait_ge(s_pick, 1)
            pe.wait_ge(s_const, 8)
            both = hit[:].rearrange("p t e -> p (t e)")
            pe.matmul(ps_b[:].rearrange("p t e -> p (t e)"), before[:], both, start=True, stop=True)
            pe.matmul(ps_n[:].rearrange("p t e -> p (t e)"), ones[:], both, start=True, stop=True).then_inc(s_cnt, 1)
            batches = 2 * TILES // BATCH
            for g in range(batches):
                pe.wait_ge(s_factor, g + 1)
                for n in range(BATCH):
                    last = pe.matmul(ps_v, in_lane[g % 2][:, n, :], in_tile[g % 2][:, n, :], start=(g == 0 and n == 0),
                                     stop=(g == batches - 1 and n == BATCH - 1))
                last.then_inc(s_used, 1)

        @block.scalar
        def _(act):
            def logits(b):
                act.wait_ge(s_l, b + 1)
                if b >= 2:
                    act.wait_ge(s_g, b - 1)
                act.activation(lt[b % 2][:], ps_l[b % 2][:], ACT.Identity, bias=gb[:]).then_inc(s_lt, 1)

            for b in range(B):
                act.wait_ge(s_T, b + 1)
                if b >= 2:
                    act.wait_ge(s_l, b - 1)
                act.activation(xt[b % 2][:], xp[:], ACT.Copy).then_inc(s_xt, 1)
                if b >= 1:
                    logits(b - 1)
            logits(B - 1)
            act.wait_ge(s_sub, 1)
            act.activation(pr[:], pr[:], ACT.Exp).then_inc(s_exp, 1)

        @block.vector
        def _(dve):
            n = 0

            def step(ins):
                nonlocal n
                n += 1
                ins.then_inc(s_ch, 1)
                dve.wait_ge(s_ch, n)

            def wide(col):
                return col[:].rearrange("p (t a) -> p t a", a=1).to_broadcast([P, TILES, E])

            def by_expert(row, n=TILES, parts=P):
                return row[0:parts].rearrange("p (a e) -> p a e", a=1).to_broadcast([parts, n, E])

            for b in range(B):
                dve.wait_ge(s_rstd, b // 2 + 1)
                for q in range(T):
                    t = b * T + q
                    last = dve.tensor_scalar(xa[:, t, :], K.H[:, t, :], K.mean[:, t:t + 1], K.rstd[:, t:t + 1],
                                             ALU.subtract, ALU.mult)
                last.then_inc(s_xn, 1)
            dve.wait_ge(s_const, 8)
            step(dve.tensor_copy(name[:], name_i[:]))
            step(dve.tensor_copy(lane[:], lane_i[:]))
            step(dve.tensor_copy(row[:], row_i[:]))
            step(dve.tensor_copy(rank[:], rank_i[:]))
            step(dve.tensor_copy(start[:], start_i[:]))
            for b in range(B):
                dve.wait_ge(s_g, b + 1)
                dve.tensor_copy(pr[:, b * T:b * T + T, :], ps_g[b % 2][:, 0:T, :]).then_inc(s_lg, 1)
            dve.wait_ge(s_lg, B)
            step(dve.tensor_reduce(col[:], pr[:], AX.X, ALU.max))
            dve.tensor_tensor(pr[:], pr[:], wide(col), ALU.subtract).then_inc(s_sub, 1)
            dve.wait_ge(s_exp, 1)
            step(dve.tensor_reduce(col[:], pr[:], AX.X, ALU.add))
            step(dve.reciprocal(col[:], col[:]))
            step(dve.tensor_tensor(pr[:], pr[:], wide(col), ALU.mult))
            for j in range(2):
                step(dve.tensor_reduce(best[j][:], pr[:], AX.X, ALU.max))
                step(dve.tensor_tensor(eq[:], pr[:], wide(best[j]), ALU.is_equal))
                step(dve.tensor_tensor(eq[:], eq[:], by_expert(rank), ALU.mult))
                step(dve.tensor_reduce(col[:], eq[:], AX.X, ALU.max))
                step(dve.tensor_tensor(pick[j][:], eq[:], wide(col), ALU.is_equal))
                if j == 0:
                    step(dve.scalar_tensor_tensor(pr[:], pick[0][:], -2.0, pr[:], ALU.mult, ALU.add))
            dve.tensor_tensor(hit[:], pick[0][:], pick[1][:], ALU.add).then_inc(s_pick, 1)
            step(dve.tensor_tensor(col[:], best[0][:], best[1][:], ALU.add))
            step(dve.reciprocal(col[:], col[:]))
            for j in range(2):
                step(dve.tensor_tensor(K.share[j][:], best[j][:], col[:], ALU.mult))
            dve.wait_ge(s_cnt, 1)
            step(dve.tensor_copy(tot[:], ps_n[:]))
            step(dve.memset(eq[:], 1.0))
            for e in range(E):
                step(dve.tensor_tensor_scan(inc[:, :, e], eq[:, :, e], tot[:, :, e], 0.0, ALU.mult, ALU.add))
            step(dve.tensor_scalar(size[:], inc[:, TILES - 1, :], float(P - 1), None, ALU.add))
            step(dve.tensor_copy(size_i[:], size[:]))
            step(dve.tensor_single_scalar(size_i[:], size_i[:], 0x7FFFFFFF - (P - 1), ALU.bitwise_and))
            step(dve.tensor_copy(size[:], size_i[:]))
            step(dve.tensor_tensor_scan(end[:], eq[:, 0, :], size[:], 0.0, ALU.mult, ALU.add))
            step(dve.tensor_tensor(base[:], end[:], size[:], ALU.subtract))
            step(dve.tensor_tensor(slot[:], inc[:], tot[:], ALU.subtract))
            step(dve.tensor_tensor(slot[:], slot[:], ps_b[:], ALU.add))
            step(dve.tensor_tensor(slot[:], slot[:], by_expert(base), ALU.add))
            for j in range(2):
                step(dve.tensor_tensor(eq[:], pick[j][:], slot[:], ALU.mult))
                step(dve.tensor_reduce(pos[:, j * TILES:(j + 1) * TILES], eq[:], AX.X, ALU.add))
            step(dve.tensor_copy(pos_i[:], pos[:]))
            step(dve.tensor_single_scalar(pos_i[:], pos_i[:], P - 1, ALU.bitwise_and))
            step(dve.tensor_copy(low[:], pos_i[:]))
            step(dve.tensor_tensor(high[:], pos[:], low[:], ALU.subtract))
            for g in range(2 * TILES // BATCH):
                if g >= 2:
                    dve.wait_ge(s_used, g - 1)
                batch = slice(g * BATCH, (g + 1) * BATCH)

                def spread(cols, n):
                    return cols[:, batch].rearrange("p (t a) -> p t a", a=1).to_broadcast([P, BATCH, n])

                step(dve.tensor_tensor(in_tile[g % 2][:], start[:].rearrange("p (a s) -> p a s", a=1).to_broadcast([P, BATCH, SLOTS]),
                                       spread(high, SLOTS), ALU.is_equal))
                dve.tensor_tensor(in_lane[g % 2][:], lane[:].rearrange("p (a s) -> p a s", a=1).to_broadcast([P, BATCH, P]),
                                  spread(low, P), ALU.is_equal)
                dve.tensor_tensor(in_tile[g % 2][:], in_tile[g % 2][:], spread(name, SLOTS), ALU.mult).then_inc(s_factor, 1)
            step(dve.tensor_tensor(ge[:], start[0:1].rearrange("p (t a) -> p t a", a=1).to_broadcast([1, SLOTS, E]),
                                   by_expert(end, SLOTS, 1), ALU.is_ge))
            step(dve.tensor_reduce(owner[:], ge[:], AX.X, ALU.add))
            step(dve.tensor_scalar(owner[:], owner[:], float(E - 1), None, ALU.min))
            step(dve.tensor_copy(K.owner[:, 0:SLOTS], owner[:]))
            step(dve.tensor_scalar(size[0:1, 0:1], end[0:1, E - 1:E], float(-P), None, ALU.add))
            step(dve.tensor_copy(size_i[0:1, 0:1], size[0:1, 0:1]))
            step(dve.tensor_single_scalar(size_i[0:1, 0:1], size_i[0:1, 0:1], 0x7FFFFFFF - (2 * P - 1), ALU.bitwise_and))
            step(dve.tensor_copy(size[0:1, 0:1], size_i[0:1, 0:1]))
            step(dve.tensor_scalar(size[0:1, 0:1], size[0:1, 0:1], 1.0 / (2 * P), None, ALU.mult))
            step(dve.tensor_copy(K.owner[:, SLOTS:SLOTS + 1], size[0:1, 0:1]))
            dve.wait_ge(s_used, 2 * TILES // BATCH)
            step(dve.tensor_copy(named[:], ps_v))
            step(dve.tensor_scalar(unused[:], named[:], 0.0, None, ALU.is_equal))
            step(dve.scalar_tensor_tensor(K.dest[:], unused[:], row[:], named[:], ALU.mult, ALU.add))
            step(dve.tensor_scalar(K.dest[:], K.dest[:], -1.0, None, ALU.add))
            step(dve.tensor_scalar(named[:], named[:], -1.0, 0.0, ALU.add, ALU.max))
            step(dve.tensor_copy(token_i[:], named[:]))
            step(dve.tensor_single_scalar(token_i[:], token_i[:], TOKENS - 1, ALU.bitwise_and))
            step(dve.tensor_copy(named[:], token_i[:]))
            step(dve.tensor_copy(K.source[:, 0:SLOTS], named[:]))


def experts(nc, K, parts_dram, xn_dram, y_dram):
    HALF = FFN // 2
    FC = FFN // P
    DOWN = 1.0 / 16
    PASSES = ((0, 0), (0, 1), (1, 0))
    with ExitStack() as ctx:
        ph = Phase(nc, ctx, "moe")
        weights = ph.sb("w", [P, EXPERTS, 3, 2, SLAB], F16)
        xin = [ph.sb(f"xin{k}", [P, D]) for k in range(2)]
        source = [ph.sb(f"source{k}", [P, 1], U32) for k in range(2)]
        xt = [ph.sb(f"xt{k}", [P, 2, C, P], F16) for k in range(2)]
        dest = ph.sb("dest", [P, 1], U32)
        h = ph.sb("h", [P, 2, HALF])
        ht = ph.sb("ht", [P, 2, 2, FC // 2, P], F16)
        y = ph.sb("y", [P, D])
        ps_a = [ph.ps(f"a{j}", [P, HALF]) for j in range(2)]
        ps_b = [ph.ps(f"b{j}", [P, HALF]) for j in range(2)]
        ps_h = [ph.ps(f"h{j}", [P, FC // 2, P]) for j in range(2)]
        ps_y = ph.ps("py", [P, 512])
        ps_x = ph.ps("x", [P, 4, P])
        s_w, s_turnx, s_xhi, s_xt, s_turnh, s_mmy, s_yc, s_source = (ph.sem(n) for n in ("w", "turnx", "xhi", "xt", "turnh", "mmy", "yc", "source"))
        s_x = [ph.sem(f"x{k}") for k in range(2)]
        s_out = ph.sem("out")
        s_a, s_b, s_silu, s_h, s_hhi, s_ht = ([ph.sem(f"{n}{j}") for j in range(2)] for n in ("a", "b", "silu", "h", "hhi", "ht"))
        block = ctx.enter_context(nc.Block())

        def last_pair(eng):
            return eng.value_load(K.owner[0:1, SLOTS:SLOTS + 1], min_val=TILES - 1, max_val=SLOTS // 2 - 1)

        def tiles(eng, body, m):
            body(0, 0, start=True)
            body(0, 1)
            with eng.Fori(1, m + 1) as i:
                for k in range(2):
                    body(i, k)

        @block.sync
        def _(sp):
            for e in range(EXPERTS):
                sp.dma_start(weights[:, e].rearrange("p m c w -> p m (c w)"),
                             parts_dram[3 * e:3 * e + 3].rearrange("m p w -> p m w")).then_inc(s_w, 16)
                sp.wait_ge(s_w, 16 * e + 16)

        @block.gpsimd
        def _(pool):
            def load(i, k):
                t = 2 * i + k
                if not (isinstance(t, int) and t < 2):
                    pool.wait_ge(s_x[k], 16 * i)
                    pool.nop(nofuse=True)
                pool.tensor_copy(source[k][:], K.source[:, bass.ds(t, 1)]).then_inc(s_source, 1)
                pool.wait_ge(s_source, t + 1)
                if not (isinstance(t, int) and t < 2):
                    pool.wait_ge(s_turnx, t - 1)
                pool.nop(nofuse=True)
                pool.indirect_dma_start(out=xin[k][:], out_offset=None, in_=xn_dram[:],
                                        in_offset=bass.IndirectOffsetOnAxis(ap=source[k][:, 0:1], axis=0)).then_inc(s_x[k], 16)

            def store(t):
                pool.wait_ge(s_yc, t + 1)
                pool.wait_ge(s_out, 16 * t)
                pool.nop(nofuse=True)
                pool.indirect_dma_start(out=y_dram[:], out_offset=bass.IndirectOffsetOnAxis(ap=dest[:, 0:1], axis=0),
                                        in_=y[:], in_offset=None).then_inc(s_out, 16)

            for t in range(4):
                load(t // 2, t % 2)
            store(0)
            m = last_pair(pool)
            with pool.Fori(1, m + 1) as i:
                for k in range(2):
                    load(i + 1, k)
                    store(2 * i + k - 1)
            store(2 * m + 1)
            pool.wait_ge(s_out, 32 * m + 32)
            for k in range(2):
                pool.wait_ge(s_x[k], 16 * m + 32)

        @block.tensor
        def _(pe):
            def turn_x(i, t, k):
                pe.wait_ge(s_x[k], 16 * i + 16)
                pe.wait_ge(s_xt, t)
                for c in range(C):
                    last = pe.transpose(ps_x[:, c, :], xin[k][:, c * P:(c + 1) * P], K.ident[:])
                last.then_inc(s_turnx, 1)

            def weight(e, matrix, part, first, n):
                return weights[:, bass.ds(e, 1), matrix, part, first:first + n].rearrange("p a f -> p (a f)")

            def first(ps, matrix, half, k, e):
                for c in range(C):
                    for n, (px, pw) in enumerate(PASSES):
                        last = pe.matmul(ps[half][:], xt[k][:, px, c, :], weight(e, matrix, pw, c * FFN + half * HALF, HALF),
                                         start=(c == 0 and n == 0), stop=(c == C - 1 and n == len(PASSES) - 1))
                return last

            def turn_h(t):
                for j in range(2):
                    pe.wait_ge(s_h[j], t + 1)
                    if not (isinstance(t, int) and t < 1):
                        pe.wait_ge(s_ht[j], t)
                    for f in range(FC // 2):
                        last = pe.transpose(ps_h[j][:, f, :], h[:, j, f * P:(f + 1) * P], K.ident[:])
                last.then_inc(s_turnh, 1)

            def last_product(t, e):
                if not (isinstance(t, int) and t < 1):
                    pe.wait_ge(s_yc, t)
                for j in range(2):
                    pe.wait_ge(s_ht[j], t + 1)
                    for f in range(FC // 2):
                        g = j * (FC // 2) + f
                        for n, (px, pw) in enumerate(PASSES):
                            last = pe.matmul(ps_y[:, 0:D], ht[:, px, j, f, :], weight(e, 2, pw, g * D, D),
                                             start=(g == 0 and n == 0), stop=(g == FC - 1 and n == len(PASSES) - 1))
                last.then_inc(s_mmy, 1)

            def owner(t):
                return pe.value_load(K.owner[0:1, bass.ds(t, 1)], min_val=0, max_val=EXPERTS - 1)

            def body(i, k, start=False, before=None):
                t = 2 * i + k
                e = owner(t)
                pe.wait_ge(s_w, 16 * e + 16)
                pe.wait_ge(s_xt, t + 1)
                pe.wait_ge(s_silu[0], t)
                first(ps_a, 0, 0, k, e).then_inc(s_a[0], 1)
                if not start:
                    turn_h(t - 1)
                pe.wait_ge(s_h[0], t)
                first(ps_b, 1, 0, k, e).then_inc(s_b[0], 1)
                pe.wait_ge(s_silu[1], t)
                first(ps_a, 0, 1, k, e).then_inc(s_a[1], 1)
                if not start:
                    last_product(t - 1, owner(t - 1) if before is None else before)
                turn_x(i + k, t + 1, 1 - k)
                pe.wait_ge(s_h[1], t)
                first(ps_b, 1, 1, k, e).then_inc(s_b[1], 1)
                return e

            turn_x(0, 0, 0)
            m = last_pair(pe)
            body(0, 1, before=body(0, 0, start=True))
            with pe.Fori(1, m + 1) as i:
                body(i, 1, before=body(i, 0))
            turn_h(2 * m + 1)
            last_product(2 * m + 1, owner(2 * m + 1))

        @block.scalar
        def _(act):
            def copy_h(t):
                act.wait_ge(s_turnh, t + 1)
                if not (isinstance(t, int) and t < 1):
                    act.wait_ge(s_mmy, t)
                for j in range(2):
                    act.activation(ht[:, 0, j], ps_h[j][:], ACT.Copy, scale=DOWN).then_inc(s_hhi[j], 1)

            def copy_x(t, k):
                act.wait_ge(s_turnx, t + 1)
                if not (isinstance(t, int) and t < 2):
                    act.wait_ge(s_b[1], t - 1)
                act.activation(xt[k][:, 0], ps_x[:, 0:C, :], ACT.Copy).then_inc(s_xhi, 1)

            def copy_y(k, t):
                act.wait_ge(s_mmy, t + 1)
                if not (isinstance(t, int) and t < 1):
                    act.wait_ge(s_out, 16 * t)
                act.nop(nofuse=True)
                act.activation(dest[:], K.dest[:, bass.ds(t, 1)], ACT.Copy)
                act.activation(y[:], ps_y[:, 0:D], ACT.Copy, scale=1.0 / DOWN).then_inc(s_yc, 1)

            def body(i, k, start=False):
                t = 2 * i + k
                if not start:
                    copy_h(t - 1)
                act.wait_ge(s_a[0], t + 1)
                act.wait_ge(s_turnh, t)
                act.activation(h[:, 0], ps_a[0][:], ACT.Silu).then_inc(s_silu[0], 1)
                act.wait_ge(s_a[1], t + 1)
                act.activation(h[:, 1], ps_a[1][:], ACT.Silu).then_inc(s_silu[1], 1)
                copy_x(t + 1, 1 - k)
                if not start:
                    copy_y(1 - k, t - 1)

            copy_x(0, 0)
            m = last_pair(act)
            tiles(act, body, m)
            copy_h(2 * m + 1)
            copy_y(1, 2 * m + 1)

        @block.vector
        def _(dve):
            def rest_x(t, k):
                dve.wait_ge(s_xhi, t + 1)
                if not (isinstance(t, int) and t < 2):
                    dve.wait_ge(s_b[1], t - 1)
                dve.tensor_tensor(xt[k][:, 1], ps_x[:, 0:C, :], xt[k][:, 0], ALU.subtract).then_inc(s_xt, 1)

            def rest_h(t):
                for j in range(2):
                    dve.wait_ge(s_hhi[j], t + 1)
                    if not (isinstance(t, int) and t < 1):
                        dve.wait_ge(s_mmy, t)
                    dve.scalar_tensor_tensor(ht[:, 1, j], ps_h[j][:], DOWN, ht[:, 0, j], ALU.mult, ALU.subtract).then_inc(s_ht[j], 1)

            def body(i, k, start=False):
                t = 2 * i + k
                if not start:
                    rest_h(t - 1)
                for j in range(2):
                    if j == 1:
                        rest_x(t + 1, 1 - k)
                    dve.wait_ge(s_silu[j], t + 1)
                    dve.wait_ge(s_b[j], t + 1)
                    dve.tensor_tensor(h[:, j], h[:, j], ps_b[j][:], ALU.mult).then_inc(s_h[j], 1)

            rest_x(0, 0)
            m = last_pair(dve)
            tiles(dve, body, m)
            rest_h(2 * m + 1)


def combine(nc, K, h_dram, y_dram, out):
    G = 4
    N = TILES // G
    with ExitStack() as ctx:
        ph = Phase(nc, ctx, "comb")
        hh = ph.sb("h", [P, TILES, D])
        yy = [ph.sb(f"y{j}", [P, TILES, D]) for j in range(2)]
        s_in, s_one, s_two, s_out = (ph.sem(n) for n in ("in", "one", "two", "out"))
        block = ctx.enter_context(nc.Block())
        s_step = [ph.sem(f"step{g}") for g in range(N)]

        def rows(dram, g, first=0):
            return dram[first + g * G * P:first + (g + 1) * G * P, :].rearrange("(t p) d -> p t d", p=P)

        @block.sync
        def _(sp):
            for g in range(N):
                cut = slice(g * G, (g + 1) * G)
                sp.dma_start(hh[:, cut, :], rows(h_dram, g)).then_inc(s_step[g], 16)
                for j in range(2):
                    sp.dma_start(yy[j][:, cut, :], rows(y_dram, g, j * TOKENS)).then_inc(s_step[g], 16)

        @block.scalar
        def _(act):
            flat = out.rearrange("b s d -> (b s) d")
            for g in range(N):
                act.wait_ge(s_two, g + 1)
                act.dma_start(rows(flat, g), hh[:, g * G:(g + 1) * G, :]).then_inc(s_out, 16)
            act.wait_ge(s_out, 16 * N)

        @block.vector
        def _(dve):
            for g in range(N):
                dve.wait_ge(s_step[g], 48)
                for j, s in ((0, s_one), (1, s_two)):
                    for t in range(g * G, (g + 1) * G):
                        last = dve.scalar_tensor_tensor(hh[:, t, :], yy[j][:, t, :], K.share[j][:, t:t + 1], hh[:, t, :],
                                                        ALU.mult, ALU.add)
                    last.then_inc(s, 1)
                    if j == 0:
                        dve.wait_ge(s_one, g + 1)


def program(nc, I, out):
    Phase.used = []
    with ExitStack() as ctx:
        class K:
            pass
        ph = Phase(nc, ctx, "k")
        K.ident = ph.sb("ident", [P, P])
        K.share = [ph.sb(f"share{j}", [P, TILES]) for j in range(2)]
        K.source = ph.sb("source", [P, SLOTS + 2], U32)
        K.dest = ph.sb("dest", [P, SLOTS])
        K.owner = ph.sb("owner", [1, SLOTS + 1], I32)

        def dram(name, shape, dt=F32):
            return nc.dram_tensor(name, shape, dt, kind="Internal")

        h_dram = dram("h", [TOKENS, D])
        xn_dram = dram("x_norm", [TOKENS, D])
        experts_parts = dram("experts_parts", [SLABS, P, 2 * SLAB], F16)
        y_dram = dram("y", [2 * TOKENS + P, D])
        with ExitStack() as stream:
            ph = Phase(nc, stream, "k")
            K.H = ph.sb("H", [P, TILES, D])
            K.stats = ph.sb("stats", [P, TILES, 6])
            K.mean = ph.sb("mean", [P, TILES])
            K.var = ph.sb("var", [P, TILES])
            K.rstd = ph.sb("rstd", [P, TILES])
            K.minus_half = ph.sb("mhalf", [P, TILES])
            rlen = dram("rlen", [B, S])
            q_dram = dram("q_parts", [B, 3, D, S], BF16)
            k_dram = dram("k_parts", [B, 3, D, S], BF16)
            v_dram = dram("v_parts", [PAIRS, B, P, T * 2 * VW], BF16)
            heads_dram = dram("heads", [B, T, P, D])
            allocate_parameters(nc, stream, K)
            constants(nc, K)
            embed(nc, K, I["x"], I["mask"], I["embT"], I["pcaT"], I["proj_w"], I["proj_b"], I["fus_w"], I["fus_b"],
                  I["ln_g"], I["ln_b"], rlen, I)
            project_qkv(nc, K, q_dram, k_dram, v_dram)
            attention(nc, K, I["pos_bias"], q_dram, k_dram, v_dram, heads_dram, I["experts"], experts_parts)
            attention_output(nc, K, heads_dram)
            inner_ffn(nc, K)
            recurrence(nc, K)
            recycle(nc)
            route(nc, K, h_dram, xn_dram)
        experts(nc, K, experts_parts, xn_dram, y_dram)
        combine(nc, K, h_dram, y_dram, out)


def kernel(**inputs):
    import numpy as np
    import concourse.bacc as bacc
    from concourse.bass_utils import run_bass_kernel_spmd

    a = {k: np.asarray(v) for k, v in inputs.items()}
    slabs = np.stack([a[n].reshape(EXPERTS, -1, P, a[n].shape[2]).transpose(0, 2, 1, 3).reshape(EXPERTS, P, SLAB)
                      for n in ("L1_ffn_w1", "L1_ffn_w3", "L1_ffn_w2")], axis=1).reshape(SLABS, P, SLAB)
    arrays = {
        "x": a["x"], "mask": a["mask_BS_i1_0"],
        "embT": a["L0_tok_emb"].T, "pcaT": a["L0_tok_pca_lookup"].T,
        "wqT": a["L0_attn_Wq"].T, "bq": a["L0_attn_bq"], "wkT": a["L0_attn_Wk"].T, "bk": a["L0_attn_bk"],
        "wvT": a["L0_attn_Wv"].T, "bv": a["L0_attn_bv"],
        "pos_bias": a["L0_attn_pos_bias"],
        "woT": a["L0_attn_Wo"].T, "bo": a["L0_attn_bo"],
        "f_win": a["L0_ffn_Win"], "f_bin": a["L0_ffn_bin_"], "f_w1": a["L0_ffn_W1"], "f_b1": a["L0_ffn_b1"],
        "f_w2": a["L0_ffn_W2"], "f_b2": a["L0_ffn_b2"], "f_wout": a["L0_ffn_Wout"], "f_bout": a["L0_ffn_bout"],
        "a_param": a["L1_attn_a_param"], "ig_w": a["L1_attn_ig_w"], "ig_b": a["L1_attn_ig_b"],
        "ag_w": a["L1_attn_ag_w"], "ag_b": a["L1_attn_ag_b"],
        "gate_w": a["L1_ffn_gate_w"], "gate_b": a["L1_ffn_gate_b"], "experts": slabs,
        "proj_w": a["L0_tok_proj_w"], "proj_b": a["L0_tok_proj_b"],
        "fus_w": a["L0_tok_fus_w"], "fus_b": a["L0_tok_fus_b"], "ln_g": a["L0_tok_ln_g"], "ln_b": a["L0_tok_ln_b"],
    }
    arrays = {k: np.ascontiguousarray(v) for k, v in arrays.items()}
    nc = bacc.Bacc("TRN2", target_bir_lowering=False, num_devices=1)
    args = {k: nc.dram_tensor(f"in_{k}", v.shape, mybir.dt.from_np(v.dtype), kind="ExternalInput").ap() for k, v in arrays.items()}
    out = nc.dram_tensor("out", (B, S, D), F32, kind="ExternalOutput").ap()
    program(nc, args, out)
    r = run_bass_kernel_spmd(nc, [{f"in_{k}": v for k, v in arrays.items()}], core_ids=[0])
    return r.results[0]["out"]
```
